# Optimizing a Trainium2 kernel written in Bass

```python
import numpy as np
import jax
import jax.numpy as jnp

def _softmax(x, axis=-1):
    return jax.nn.softmax(x, axis=axis)

def _gelu(x):
    return jax.nn.gelu(x, approximate=True)

def _silu(x):
    return jax.nn.silu(x)

def _sigmoid(x):
    return jax.nn.sigmoid(x)

def _layernorm(x, axis=-1, eps=1e-05):
    m = jnp.mean(x, axis=axis, keepdims=True)
    v = jnp.var(x, axis=axis, keepdims=True)
    return (x - m) / jnp.sqrt(v + eps)

def _scatter_add(tgt, idx, src, axis=0):
    return tgt.at[idx].add(src)

def _segment_sum(src, seg, n):
    return jax.ops.segment_sum(src, seg, n)
kernel_name = 'mk_gnn_preln_d4_gnn_r8_ff2d4a'

def setup_inputs(seed: int=0):
    np.random.seed(seed)
    _w = jnp.asarray

    def _rec_inputs():
        import jax
        import jax.numpy as jnp
        _gk = jax.random.key(seed)
        x = -0.000202 + 1 * jax.random.normal(jax.random.fold_in(_gk, 1), (6250, 128), jnp.float32)
        src = jax.random.randint(jax.random.fold_in(_gk, 2), (100000,), 0, 6250, jnp.int32)
        dst = jax.random.randint(jax.random.fold_in(_gk, 3), (100000,), 0, 6250, jnp.int32)
        _o = jnp.argsort(dst, stable=True)
        src = src[_o]
        dst = dst[_o]
        edge_attr_32 = jax.random.uniform(jax.random.fold_in(_gk, 12), (100000, 32), jnp.float32, 0.0, 1)
        edge_attr_4 = jax.random.uniform(jax.random.fold_in(_gk, 13), (100000, 4), jnp.float32, 0.0, 1)
        edge_weight = jax.random.uniform(jax.random.fold_in(_gk, 15), (100000,), jnp.float32, 0.0, 1)
        edge_weight_n2 = jax.random.uniform(jax.random.fold_in(_gk, 16), (100000,), jnp.float32, 0.0, 1)
        return (x, src, dst, edge_attr_32, edge_attr_4, edge_weight, edge_weight_n2)
    x, src, dst, edge_attr_32, edge_attr_4, edge_weight, edge_weight_n2 = _rec_inputs()

    def _L0_gnn_setup():
        import jax, jax.numpy as jnp
        import numpy as np
        N_NODES = 6250
        N_EDGES = 100000
        DIM = 128
        N_HEADS = 8
        HEAD_DIM = DIM // N_HEADS
        LN_EPS = 1e-05
        NEG_SLOPE = 0.2

        def _gat_forward(x, src, dst, ln_gamma, ln_beta, W_in, b_in, W_u, b_u, W_v, W_ff, b_ff):
            mu = jnp.mean(x, axis=-1, keepdims=True)
            var = jnp.mean(jnp.square(x - mu), axis=-1, keepdims=True)
            x = (x - mu) * jax.lax.rsqrt(var + LN_EPS) * ln_gamma + ln_beta
            x = x @ W_in + b_in
            scores_u = x @ W_u + b_u
            scores_v = x @ W_v
            e = scores_u[src] + scores_v[dst]
            e = jnp.where(e >= 0, e, NEG_SLOPE * e)
            m = jax.ops.segment_max(e, dst, num_segments=N_NODES)
            ex = jnp.exp(e - m[dst])
            s = jax.ops.segment_sum(ex, dst, num_segments=N_NODES)
            probs = ex / s[dst]
            xh = x.reshape(N_NODES, HEAD_DIM, N_HEADS)
            msg = xh[src] * probs[:, None, :]
            agg = jax.ops.segment_sum(msg, dst, num_segments=N_NODES)
            out = agg.reshape(N_NODES, DIM)
            return out @ W_ff + b_ff
        key = jax.random.key(seed)
        ks = jax.random.split(key, 10)
        inp = {'x': jax.random.normal(ks[0], (N_NODES, DIM), dtype=jnp.float32), 'src': jax.random.randint(ks[1], (N_EDGES,), 0, N_NODES, dtype=jnp.int32), 'dst': jax.random.randint(ks[2], (N_EDGES,), 0, N_NODES, dtype=jnp.int32), 'ln_gamma': jnp.ones((DIM,), dtype=jnp.float32), 'ln_beta': jnp.zeros((DIM,), dtype=jnp.float32), 'W_in': jax.random.normal(ks[3], (DIM, DIM), dtype=jnp.float32) * DIM ** (-0.5), 'b_in': jax.random.normal(ks[4], (DIM,), dtype=jnp.float32) * 0.02, 'W_u': jax.random.normal(ks[5], (DIM, N_HEADS), dtype=jnp.float32) * DIM ** (-0.5), 'b_u': jax.random.normal(ks[6], (N_HEADS,), dtype=jnp.float32) * 0.02, 'W_v': jax.random.normal(ks[7], (DIM, N_HEADS), dtype=jnp.float32) * DIM ** (-0.5), 'W_ff': jax.random.normal(ks[8], (DIM, DIM), dtype=jnp.float32) * DIM ** (-0.5), 'b_ff': jax.random.normal(ks[9], (DIM,), dtype=jnp.float32) * 0.02}
        return inp
    _L0_gnn_all = _L0_gnn_setup()
    _L0_gnn_in = {k: v for k, v in _L0_gnn_all.items() if k in ('ln_gamma', 'ln_beta', 'W_in', 'b_in', 'W_u', 'b_u', 'W_v', 'W_ff', 'b_ff')}
    del _L0_gnn_all

    def _L1_gnn_setup():
        import jax, jax.numpy as jnp
        import numpy as np
        N_NODES = 12500
        N_EDGES = 400000
        D_IN = 128
        D_OUT = 128
        BN_EPS = 1e-05
        key = jax.random.key(seed)
        k1, k2, k3, k4 = jax.random.split(key, 4)
        x = jax.random.normal(k1, (N_NODES, D_IN), dtype=jnp.float32)
        edge_index = jax.random.randint(k2, (2, N_EDGES), 0, N_NODES, dtype=jnp.int64)
        W = jax.random.normal(k3, (D_IN, D_OUT), dtype=jnp.float32) / np.sqrt(D_IN)
        b = jnp.zeros((D_OUT,), dtype=jnp.float32)
        gamma = jnp.ones((D_OUT,), dtype=jnp.float32)
        beta = jnp.zeros((D_OUT,), dtype=jnp.float32)
        return {'x': x, 'edge_index': edge_index, 'W': W, 'b': b, 'gamma': gamma, 'beta': beta}
    _L1_gnn_all = _L1_gnn_setup()
    _L1_gnn_in = {k: v for k, v in _L1_gnn_all.items() if k in ('W', 'b', 'gamma', 'beta')}
    del _L1_gnn_all

    def _L2_gnn_setup():
        import jax, jax.numpy as jnp
        import numpy as np
        N = 6250
        E = 75000
        C = 128
        NEG_SLOPE = 0.2

        def _gat_layer(x, src, dst, W, a_src, a_dst, bias):
            h = x @ W
            alpha_s = h @ a_src
            alpha_d = h @ a_dst
            e = jax.nn.leaky_relu(alpha_s[src] + alpha_d[dst], NEG_SLOPE)
            m = jax.ops.segment_max(e, dst, num_segments=N)
            ex = jnp.exp(e - m[dst])
            denom = jax.ops.segment_sum(ex, dst, num_segments=N)
            coef = ex / denom[dst]
            out = jax.ops.segment_sum(h[src] * coef[:, None], dst, num_segments=N)
            return out + bias
        key = jax.random.key(seed)
        ks = jax.random.split(key, 12)
        s = 1.0 / np.sqrt(C)
        x = jax.random.normal(ks[0], (N, C), jnp.float32)
        src = jax.random.randint(ks[1], (E,), 0, N, jnp.int32)
        dst = jax.random.randint(ks[2], (E,), 0, N, jnp.int32)
        W1 = jax.random.normal(ks[3], (C, C), jnp.float32) * s
        as1 = jax.random.normal(ks[4], (C,), jnp.float32) * s
        ad1 = jax.random.normal(ks[5], (C,), jnp.float32) * s
        b1 = jnp.zeros((C,), jnp.float32)
        W2 = jax.random.normal(ks[6], (C, C), jnp.float32) * s
        as2 = jax.random.normal(ks[7], (C,), jnp.float32) * s
        ad2 = jax.random.normal(ks[8], (C,), jnp.float32) * s
        b2 = jnp.zeros((C,), jnp.float32)
        return {'x': x, 'src': src, 'dst': dst, 'W1': W1, 'as1': as1, 'ad1': ad1, 'b1': b1, 'W2': W2, 'as2': as2, 'ad2': ad2, 'b2': b2}
    _L2_gnn_all = _L2_gnn_setup()
    _L2_gnn_in = {k: v for k, v in _L2_gnn_all.items() if k in ('W1', 'as1', 'ad1', 'b1', 'W2', 'as2', 'ad2', 'b2')}
    del _L2_gnn_all

    def _L3_gnn_setup():
        import jax, jax.numpy as jnp
        import numpy as np
        N_ATOMS = 6250
        N_PAIRS = 100000
        F = 128
        K = 32
        N_L = 4
        H = 4
        DH = F // H
        key = jax.random.key(seed)
        ks = jax.random.split(key, 16)
        inp = {'x': jax.random.normal(ks[0], (N_ATOMS, F), dtype=jnp.float32), 'rbf_ij': jax.random.uniform(ks[1], (N_PAIRS, K), dtype=jnp.float32), 'd_gamma': jax.random.uniform(ks[2], (N_PAIRS, N_L), dtype=jnp.float32), 'phi_r_cut': jax.random.uniform(ks[3], (N_PAIRS,), dtype=jnp.float32), 'pair_mask': jnp.ones((N_PAIRS,), dtype=jnp.float32), 'idx_i': jnp.sort(jax.random.randint(ks[4], (N_PAIRS,), 0, N_ATOMS)), 'idx_j': jax.random.randint(ks[5], (N_PAIRS,), 0, N_ATOMS), 'rad_W1': jax.random.normal(ks[6], (K, F), dtype=jnp.float32) / np.sqrt(K), 'rad_b1': jnp.zeros((F,), dtype=jnp.float32), 'rad_W2': jax.random.normal(ks[7], (F, F), dtype=jnp.float32) / np.sqrt(F), 'rad_b2': jnp.zeros((F,), dtype=jnp.float32), 'sph_W1': jax.random.normal(ks[8], (N_L, F), dtype=jnp.float32) / np.sqrt(N_L), 'sph_b1': jnp.zeros((F,), dtype=jnp.float32), 'sph_W2': jax.random.normal(ks[9], (F, F), dtype=jnp.float32) / np.sqrt(F), 'sph_b2': jnp.zeros((F,), dtype=jnp.float32), 'Wq': jax.random.normal(ks[10], (H, DH, DH), dtype=jnp.float32) / np.sqrt(DH), 'Wk': jax.random.normal(ks[11], (H, DH, DH), dtype=jnp.float32) / np.sqrt(DH), 'Wv': jax.random.normal(ks[12], (H, DH, DH), dtype=jnp.float32) / np.sqrt(DH)}
        return inp
    _L3_gnn_all = _L3_gnn_setup()
    _L3_gnn_in = {k: v for k, v in _L3_gnn_all.items() if k in ('rad_W1', 'rad_b1', 'rad_W2', 'rad_b2', 'sph_W1', 'sph_b1', 'sph_W2', 'sph_b2', 'Wq', 'Wk', 'Wv')}
    del _L3_gnn_all
    return {'x': x, 'src': src, 'dst': dst, 'edge_attr_32': edge_attr_32, 'edge_attr_4': edge_attr_4, 'edge_weight': edge_weight, 'edge_weight_n2': edge_weight_n2, 'L0_gnn_ln_gamma': _L0_gnn_in['ln_gamma'], 'L0_gnn_ln_beta': _L0_gnn_in['ln_beta'], 'L0_gnn_W_in': _L0_gnn_in['W_in'], 'L0_gnn_b_in': _L0_gnn_in['b_in'], 'L0_gnn_W_u': _L0_gnn_in['W_u'], 'L0_gnn_b_u': _L0_gnn_in['b_u'], 'L0_gnn_W_v': _L0_gnn_in['W_v'], 'L0_gnn_W_ff': _L0_gnn_in['W_ff'], 'L0_gnn_b_ff': _L0_gnn_in['b_ff'], 'L1_gnn_W': _L1_gnn_in['W'], 'L1_gnn_b': _L1_gnn_in['b'], 'L1_gnn_gamma': _L1_gnn_in['gamma'], 'L1_gnn_beta': _L1_gnn_in['beta'], 'L2_gnn_W1': _L2_gnn_in['W1'], 'L2_gnn_as1': _L2_gnn_in['as1'], 'L2_gnn_ad1': _L2_gnn_in['ad1'], 'L2_gnn_b1': _L2_gnn_in['b1'], 'L2_gnn_W2': _L2_gnn_in['W2'], 'L2_gnn_as2': _L2_gnn_in['as2'], 'L2_gnn_ad2': _L2_gnn_in['ad2'], 'L2_gnn_b2': _L2_gnn_in['b2'], 'L3_gnn_rad_W1': _L3_gnn_in['rad_W1'], 'L3_gnn_rad_b1': _L3_gnn_in['rad_b1'], 'L3_gnn_rad_W2': _L3_gnn_in['rad_W2'], 'L3_gnn_rad_b2': _L3_gnn_in['rad_b2'], 'L3_gnn_sph_W1': _L3_gnn_in['sph_W1'], 'L3_gnn_sph_b1': _L3_gnn_in['sph_b1'], 'L3_gnn_sph_W2': _L3_gnn_in['sph_W2'], 'L3_gnn_sph_b2': _L3_gnn_in['sph_b2'], 'L3_gnn_Wq': _L3_gnn_in['Wq'], 'L3_gnn_Wk': _L3_gnn_in['Wk'], 'L3_gnn_Wv': _L3_gnn_in['Wv']}

def reference(x, src, dst, edge_attr_32, edge_attr_4, edge_weight, edge_weight_n2, L0_gnn_ln_gamma, L0_gnn_ln_beta, L0_gnn_W_in, L0_gnn_b_in, L0_gnn_W_u, L0_gnn_b_u, L0_gnn_W_v, L0_gnn_W_ff, L0_gnn_b_ff, L1_gnn_W, L1_gnn_b, L1_gnn_gamma, L1_gnn_beta, L2_gnn_W1, L2_gnn_as1, L2_gnn_ad1, L2_gnn_b1, L2_gnn_W2, L2_gnn_as2, L2_gnn_ad2, L2_gnn_b2, L3_gnn_rad_W1, L3_gnn_rad_b1, L3_gnn_rad_W2, L3_gnn_rad_b2, L3_gnn_sph_W1, L3_gnn_sph_b1, L3_gnn_sph_W2, L3_gnn_sph_b2, L3_gnn_Wq, L3_gnn_Wk, L3_gnn_Wv):
    import jax
    import jax.numpy as jnp

    def _L0_gnn_ref(x, src, dst, ln_gamma, ln_beta, W_in, b_in, W_u, b_u, W_v, W_ff, b_ff):
        import jax, jax.numpy as jnp
        import numpy as np
        N_NODES = 6250
        N_EDGES = 100000
        DIM = 128
        N_HEADS = 8
        HEAD_DIM = DIM // N_HEADS
        LN_EPS = 1e-05
        NEG_SLOPE = 0.2

        def _gat_forward(x, src, dst, ln_gamma, ln_beta, W_in, b_in, W_u, b_u, W_v, W_ff, b_ff):
            mu = jnp.mean(x, axis=-1, keepdims=True)
            var = jnp.mean(jnp.square(x - mu), axis=-1, keepdims=True)
            x = (x - mu) * jax.lax.rsqrt(var + LN_EPS) * ln_gamma + ln_beta
            x = x @ W_in + b_in
            scores_u = x @ W_u + b_u
            scores_v = x @ W_v
            e = scores_u[src] + scores_v[dst]
            e = jnp.where(e >= 0, e, NEG_SLOPE * e)
            m = jax.ops.segment_max(e, dst, num_segments=N_NODES)
            ex = jnp.exp(e - m[dst])
            s = jax.ops.segment_sum(ex, dst, num_segments=N_NODES)
            probs = ex / s[dst]
            xh = x.reshape(N_NODES, HEAD_DIM, N_HEADS)
            msg = xh[src] * probs[:, None, :]
            agg = jax.ops.segment_sum(msg, dst, num_segments=N_NODES)
            out = agg.reshape(N_NODES, DIM)
            return out @ W_ff + b_ff
        return _gat_forward(x, src, dst, ln_gamma, ln_beta, W_in, b_in, W_u, b_u, W_v, W_ff, b_ff)

    def _L1_gnn_ref(x, edge_index, W, b, gamma, beta):
        import jax, jax.numpy as jnp
        import numpy as np
        N_NODES = 12500
        N_EDGES = 400000
        D_IN = 128
        D_OUT = 128
        BN_EPS = 1e-05
        N = x.shape[0]
        xw = x @ W
        loop = jnp.arange(N, dtype=edge_index.dtype)
        src = jnp.concatenate([edge_index[0], loop])
        dst = jnp.concatenate([edge_index[1], loop])
        deg = jax.ops.segment_sum(jnp.ones_like(dst, dtype=xw.dtype), dst, num_segments=N)
        dinv = jnp.where(deg > 0, jax.lax.rsqrt(deg), 0.0)
        norm = dinv[src] * dinv[dst]
        msg = xw[src] * norm[:, None]
        out = jax.ops.segment_sum(msg, dst, num_segments=N) + b
        mean = jnp.mean(out, axis=0)
        var = jnp.mean((out - mean) ** 2, axis=0)
        out = (out - mean) * jax.lax.rsqrt(var + BN_EPS) * gamma + beta
        return jax.nn.relu(out)

    def _L2_gnn_ref(x, src, dst, W1, as1, ad1, b1, W2, as2, ad2, b2):
        import jax, jax.numpy as jnp
        import numpy as np
        N = 6250
        E = 75000
        C = 128
        NEG_SLOPE = 0.2

        def _gat_layer(x, src, dst, W, a_src, a_dst, bias):
            h = x @ W
            alpha_s = h @ a_src
            alpha_d = h @ a_dst
            e = jax.nn.leaky_relu(alpha_s[src] + alpha_d[dst], NEG_SLOPE)
            m = jax.ops.segment_max(e, dst, num_segments=N)
            ex = jnp.exp(e - m[dst])
            denom = jax.ops.segment_sum(ex, dst, num_segments=N)
            coef = ex / denom[dst]
            out = jax.ops.segment_sum(h[src] * coef[:, None], dst, num_segments=N)
            return out + bias
        loops = jnp.arange(N, dtype=src.dtype)
        s = jnp.concatenate([src, loops])
        d = jnp.concatenate([dst, loops])
        h = _gat_layer(x, s, d, W1, as1, ad1, b1)
        h = jax.nn.relu(h)
        out = _gat_layer(h, s, d, W2, as2, ad2, b2)
        return out

    def _L3_gnn_ref(x, rbf_ij, d_gamma, phi_r_cut, pair_mask, idx_i, idx_j, rad_W1, rad_b1, rad_W2, rad_b2, sph_W1, sph_b1, sph_W2, sph_b2, Wq, Wk, Wv):
        import jax, jax.numpy as jnp
        import numpy as np
        N_ATOMS = 6250
        N_PAIRS = 100000
        F = 128
        K = 32
        N_L = 4
        H = 4
        DH = F // H
        silu = jax.nn.silu
        w = silu(rbf_ij @ rad_W1 + rad_b1) @ rad_W2 + rad_b2 + (silu(d_gamma @ sph_W1 + sph_b1) @ sph_W2 + sph_b2)
        n = x.shape[0]
        xh = x.reshape(n, H, DH)
        wh = w.reshape(-1, H, DH)
        q = jnp.einsum('nhd,hde->nhe', xh, Wq)
        k = jnp.einsum('nhd,hde->nhe', xh, Wk)
        alpha = (q[idx_i] * wh * k[idx_j]).sum(-1) / jnp.sqrt(jnp.float32(DH))
        alpha = alpha * (pair_mask * phi_r_cut)[:, None]
        v = jnp.einsum('nhd,hde->nhe', xh, Wv)
        agg = jax.ops.segment_sum(alpha[:, :, None] * v[idx_j], idx_i, num_segments=n)
        return agg.reshape(n, F)
    edge_index = jnp.stack([src, dst])
    h = jnp.maximum(_layernorm(x, axis=-1), 0.0)
    x = x + _L0_gnn_ref(h, src, dst, L0_gnn_ln_gamma, L0_gnn_ln_beta, L0_gnn_W_in, L0_gnn_b_in, L0_gnn_W_u, L0_gnn_b_u, L0_gnn_W_v, L0_gnn_W_ff, L0_gnn_b_ff)
    h = jnp.maximum(_layernorm(x, axis=-1), 0.0)
    x = x + _L1_gnn_ref(h, edge_index, L1_gnn_W, L1_gnn_b, L1_gnn_gamma, L1_gnn_beta)
    h = jnp.maximum(_layernorm(x, axis=-1), 0.0)
    x = x + _L2_gnn_ref(h, src, dst, L2_gnn_W1, L2_gnn_as1, L2_gnn_ad1, L2_gnn_b1, L2_gnn_W2, L2_gnn_as2, L2_gnn_ad2, L2_gnn_b2)
    h = jnp.maximum(_layernorm(x, axis=-1), 0.0)
    x = x + _L3_gnn_ref(h, edge_attr_32, edge_attr_4, edge_weight, edge_weight_n2, src, dst, L3_gnn_rad_W1, L3_gnn_rad_b1, L3_gnn_rad_W2, L3_gnn_rad_b2, L3_gnn_sph_W1, L3_gnn_sph_b1, L3_gnn_sph_W2, L3_gnn_sph_b2, L3_gnn_Wq, L3_gnn_Wk, L3_gnn_Wv)
    return x

_drawn_inputs = setup_inputs


def setup_inputs(seed=0):
    import zlib

    import numpy as np

    out = dict(_drawn_inputs(seed))
    spreads = {'L0_gnn_ln_gamma': (1.0, 0.2),
     'L0_gnn_ln_beta': (0.0, 0.1),
     'L1_gnn_b': (0.0, 2.0),
     'L1_gnn_gamma': (1.0, 0.2),
     'L1_gnn_beta': (0.0, 0.1),
     'L2_gnn_b1': (0.0, 0.1),
     'L2_gnn_b2': (0.0, 0.1),
     'L3_gnn_rad_b1': (0.0, 0.1),
     'L3_gnn_rad_b2': (0.0, 0.1),
     'L3_gnn_sph_b1': (0.0, 0.327),
     'L3_gnn_sph_b2': (0.0, 0.1)}
    factors = {'L0_gnn_b_in': 2.688,
     'L0_gnn_b_u': 31.702,
     'L2_gnn_as1': 5.875,
     'L2_gnn_ad1': 8.0,
     'L2_gnn_as2': 8.0,
     'L2_gnn_ad2': 8.0}
    for name, (base, spread) in spreads.items():
        noise = np.random.default_rng([zlib.crc32(name.encode()), seed]).standard_normal(out[name].shape)
        drawn = base * np.exp(spread * noise) if base else spread * noise
        out[name] = jnp.asarray(drawn.astype(out[name].dtype))
    for name, factor in factors.items():
        out[name] = (out[name] * factor).astype(out[name].dtype)
    return out
```

```python
from contextlib import ExitStack

import numpy as np

import concourse.bass as bass
from concourse import mybir

F32 = mybir.dt.float32
BF16 = mybir.dt.bfloat16
I32 = mybir.dt.int32
ALU = mybir.AluOpType
ACT = mybir.ActivationFunctionType
AX = mybir.AxisListType

N = 6250
E = 100000
D = 128
NT = 49
NB = 49
KB = 16
EB = 2048
EP = NB * EB
NP = NT * 128
TAIL = N - (NT - 1) * 128
BIG = 1.0e30
NOWHERE = 1000000
GROUPS = [(4 * g, min(4, NT - 4 * g)) for g in range(13)]


class Plan:

    def __init__(self, nc, ctx, name):
        self.nc, self.ctx, self.name = nc, ctx, name
        self.queues = {k: [] for k in ("sync", "gpsimd", "scalar", "vector", "tensor")}
        self.sems, self.counts, self.seen = {}, {}, {}

    def sem(self, key):
        if key not in self.sems:
            self.sems[key] = self.ctx.enter_context(self.nc.semaphore(f"{self.name}_{key}"))
            self.counts[key] = 0
        return self.sems[key]

    def _waits(self, eng, after):
        out, last = [], {}
        flat = [t for a in after if a for t in (a if isinstance(a, list) else [a])]
        for key, value in flat:
            last[key] = max(value, last.get(key, 0))
        for key, value in last.items():
            if self.seen.get((eng, key), 0) < value:
                self.seen[(eng, key)] = value
                out.append((self.sem(key), value))
        return out

    def op(self, eng, fn, after=()):
        sem = self.sem(eng)
        waits = self._waits(eng, after)
        self.counts[eng] += 1

        def emit(e):
            for s, v in waits:
                e.wait_ge(s, v)
            fn(e).then_inc(sem, 1)

        self.queues[eng].append(emit)
        return (eng, self.counts[eng])

    def dma(self, eng, slot, fn, after=()):
        sem = self.sem(slot)
        waits = self._waits(eng, after)
        self.counts[slot] += 16

        def emit(e):
            for s, v in waits:
                e.wait_ge(s, v)
            fn(e).then_inc(sem, 16)

        self.queues[eng].append(emit)
        return (slot, self.counts[slot])

    def raw(self, eng, fn, after=()):
        waits = self._waits(eng, after)

        def emit(e):
            for s, v in waits:
                e.wait_ge(s, v)
            fn(e)

        self.queues[eng].append(emit)

    def finish(self):
        for key, value in self.counts.items():
            if key not in self.queues:
                self.raw("sync", lambda e: None, [(key, value)])
        with self.nc.Block() as block:
            for eng, queue in self.queues.items():
                def run(e, queue=queue):
                    for emit in queue:
                        emit(e)

                on = {"sync": block.sync, "gpsimd": block.gpsimd, "scalar": block.scalar,
                      "vector": block.vector, "tensor": block.tensor}
                on[eng](run)


def row_bcast(ap, parts):
    return bass.AP(ap.tensor, ap.offset, [[0, parts], [1, ap.shape[0]]])


class Net:
    def __init__(self, nc, ctx, io):
        self.nc, self.ctx, self.io = nc, ctx, io
        sb = self.sb
        self.x = sb("x_res", [128, NT, 128])
        self.ident = sb("ident", [128, 128])
        self.iota = sb("iota", [128, 128])
        self.jt = sb("jt", [128, NT])
        self.tb = sb("tb", [128, NT])
        self.t0 = sb("t0", [1, NB + 1], I32)
        self.dinv = sb("dinv", [128, NT])
        self.srcS = sb("srcS", [128, NB * KB], I32)
        self.dstS = sb("dstS", [128, NB, KB])
        self.eps = sb("eps", [128, 1])
        self.tabs = {p: self.dram(f"tab{p}", (NP, w)) for p, w in
                     (("0", 136), ("1", 128), ("2", 129), ("3", 129), ("4", 128))}
        self.dstp = self.dram("dstp", (EP,), I32)
        self.srcp = self.dram("srcp", (EP,), I32)
        self.attr = self.dram("attrp", (36, EP))
        self.sums = [self.dram(f"sums{r}", (NP + 128, D)) for r in range(4)]
        self.gfr = self.dram("gfr", (2, NB, 128))

    def dram(self, name, shape, dt=F32):
        return self.nc.dram_tensor(name, shape, dt, kind="Internal").ap()

    def sb(self, name, shape, dt=F32, ctx=None):
        return (ctx or self.ctx).enter_context(self.nc.sbuf_tensor(name, shape, dt))

    def ps(self, name, shape, ctx):
        return ctx.enter_context(self.nc.psum_tensor(name, shape, F32))


def setup(net):
    nc, io = net.nc, net.io
    with ExitStack() as ctx:
        p = Plan(nc, net.ctx, "su")
        one = net.sb("su_one", [128, 128], ctx=ctx)
        padi = net.sb("su_padi", [1, 352], I32, ctx=ctx)
        zeroi = net.sb("su_zeroi", [1, 352], I32, ctx=ctx)
        padf = net.sb("su_padf", [36, 352], ctx=ctx)
        raw = net.sb("su_raw", [128, NB, KB], I32, ctx=ctx)
        t0f = net.sb("su_t0", [1, NB + 1], I32, ctx=ctx)
        a = p.op("vector", lambda e: e.memset(padi[:], NOWHERE))
        b = p.op("vector", lambda e: e.memset(zeroi[:], 0))
        c = p.op("vector", lambda e: e.memset(padf[:], 0.0))
        f = [p.dma("sync", "fill", lambda e: e.dma_start(net.dstp[E:EP].rearrange("(a n) -> a n", a=1), padi[:]), [a]),
             p.dma("sync", "fill", lambda e: e.dma_start(net.srcp[E:EP].rearrange("(a n) -> a n", a=1), zeroi[:]), [b]),
             p.dma("sync", "fill", lambda e: e.dma_start(net.dstp[0:E].rearrange("(a n) -> a n", a=16), io["dst"].rearrange("(a n) -> a n", a=16))),
             p.dma("sync", "fill", lambda e: e.dma_start(net.srcp[0:E].rearrange("(a n) -> a n", a=16), io["src"].rearrange("(a n) -> a n", a=16)))]
        p.dma("scalar", "attr", lambda e: e.dma_start(net.attr[:, E:EP], padf[:]), [c])
        p.dma("scalar", "attr", lambda e: e.dma_start(net.attr[0:32, 0:E], io["attr32T"]))
        p.dma("scalar", "attr", lambda e: e.dma_start(net.attr[32:36, 0:E], io["attr4T"]))
        l1 = p.dma("sync", "l1", lambda e: e.dma_start(raw[:], net.dstp.rearrange("(b p k) -> p b k", p=128, k=KB)), [f[-1]])
        p.dma("sync", "l2", lambda e: e.dma_start(net.srcS[:].rearrange("p (b k) -> p b k", k=KB), net.srcp.rearrange("(b p k) -> p b k", p=128, k=KB)), [f[-1]])
        l3 = p.dma("sync", "l3", lambda e: e.dma_start(t0f[0:1, 0:NB].rearrange("a (n o) -> a n o", o=1), net.dstp.rearrange("(b n) -> b n", n=EB)[:, 0:1].rearrange("(a b) o -> a b o", a=1), allow_slow_non_contiguous=True), [f[-1]])
        v = p.op("vector", lambda e: e.tensor_copy(net.dstS[:], raw[:]), [l1])
        v = p.op("vector", lambda e: e.tensor_scalar(net.t0[0:1, 0:NB], t0f[0:1, 0:NB], 7, None, ALU.arith_shift_right), [l3])
        v = p.op("vector", lambda e: e.memset(net.t0[0:1, 0:1], 0), [v])
        v = p.op("vector", lambda e: e.memset(net.t0[0:1, NB:NB + 1], NT - 1), [v])
        p.op("vector", lambda e: e.memset(net.eps[:], 1e-5))
        o = p.op("vector", lambda e: e.memset(one[:], 1.0))
        g = p.op("gpsimd", lambda e: e.affine_select(out=net.ident[:], in_=one[:], compare_op=ALU.is_equal, fill=0.0, base=0, pattern=[[-1, 128]], channel_multiplier=1), [o])
        p.op("gpsimd", lambda e: e.iota(net.iota[:], pattern=[[1, 128]], base=0, channel_multiplier=0, allow_small_or_imprecise_dtypes=True))
        p.op("gpsimd", lambda e: e.iota(net.jt[:], pattern=[[128, NT]], base=0, channel_multiplier=1, allow_small_or_imprecise_dtypes=True))
        p.op("gpsimd", lambda e: e.iota(net.tb[:], pattern=[[128, NT]], base=0, channel_multiplier=0, allow_small_or_imprecise_dtypes=True))
        z = p.op("vector", lambda e: e.memset(net.x[:, NT - 1, :], 0.0))
        zs = net.sb("su_zs", [128, 50 * 128], ctx=ctx)
        y = p.op("vector", lambda e: e.memset(zs[:], 0.0))
        for r in range(4):
            p.dma("scalar", "sums", lambda e, r=r: e.dma_start(net.sums[r].rearrange("(p t) c -> p (t c)", p=128), zs[:]), [y])
        p.dma("scalar", "x", lambda e: e.dma_start(net.x[:, 0:NT - 1, :], io["x"][0:(NT - 1) * 128, :].rearrange("(t p) c -> p t c", p=128)))
        p.dma("scalar", "x2", lambda e: e.dma_start(net.x[0:TAIL, NT - 1, :], io["x"][(NT - 1) * 128:N, :]), [z])
        p.finish()


def masks(net, ctx):
    m = {k: net.sb("m_" + k, [128, NB, KB], ctx=ctx) for k in ("MF", "MB", "FM", "LM", "isl")}
    nc = net.nc
    with ExitStack() as c2:
        p = Plan(nc, net.ctx, "mk")
        sh = net.sb("mk_sh", [128, 128], ctx=c2)
        sh2 = net.sb("mk_sh2", [128, 128], ctx=c2)
        one = net.sb("mk_one", [128, 128], ctx=c2)
        prev = net.sb("mk_prev", [128, NB, KB], ctx=c2)
        nxt = net.sb("mk_next", [128, NB, KB], ctx=c2)
        keep = net.sb("mk_keep", [128, NB, KB], ctx=c2)
        keep2 = net.sb("mk_keep2", [128, NB, KB], ctx=c2)
        sen = net.sb("mk_sen", [128, 2], ctx=c2)
        rows = net.sb("mk_rows", [NB, 2, 128], ctx=c2)
        pa = net.ps("mk_pa", [128, NB], c2)
        pb = net.ps("mk_pb", [128, NB], c2)
        pc = net.ps("mk_pc", [NB, 2, 128], c2)
        o = p.op("vector", lambda e: e.memset(one[:], 1.0))
        g1 = p.op("gpsimd", lambda e: e.affine_select(out=sh[:], in_=one[:], compare_op=ALU.is_equal, fill=0.0, base=1, pattern=[[-1, 128]], channel_multiplier=1), [o])
        g2 = p.op("gpsimd", lambda e: e.affine_select(out=sh2[:], in_=one[:], compare_op=ALU.is_equal, fill=0.0, base=-1, pattern=[[-1, 128]], channel_multiplier=1), [o])
        t1 = p.op("tensor", lambda e: e.matmul(pa[:], sh[:], net.dstS[:, :, KB - 1], start=True, stop=True), [g1])
        t2 = p.op("tensor", lambda e: e.matmul(pb[:], sh2[:], net.dstS[:, :, 0], start=True, stop=True), [g2])
        s1 = p.op("vector", lambda e: e.tensor_scalar(sen[:, 0:1], net.jt[:, 0:1], 0.0, -5.0, ALU.is_equal, ALU.mult))
        s2 = p.op("vector", lambda e: e.tensor_scalar(sen[:, 1:2], net.jt[:, 0:1], 127.0, -5.0, ALU.is_equal, ALU.mult))
        v1 = p.op("vector", lambda e: e.tensor_copy(prev[:, :, 1:KB], net.dstS[:, :, 0:KB - 1]))
        v2 = p.op("vector", lambda e: e.tensor_copy(nxt[:, :, 0:KB - 1], net.dstS[:, :, 1:KB]))
        v3 = p.op("vector", lambda e: e.tensor_scalar(prev[:, :, 0], pa[:], sen[:, 0:1], None, ALU.add), [t1, s2])
        v4 = p.op("vector", lambda e: e.tensor_scalar(nxt[:, :, KB - 1], pb[:], sen[:, 1:2], None, ALU.add), [t2])
        v5 = p.op("vector", lambda e: e.tensor_tensor(m["FM"][:], net.dstS[:], prev[:], ALU.not_equal), [v4])
        v6 = p.op("vector", lambda e: e.tensor_tensor(m["isl"][:], net.dstS[:], nxt[:], ALU.not_equal), [v4])
        k1 = p.op("vector", lambda e: e.memset(keep[:], 1.0))
        k1 = p.op("vector", lambda e: e.memset(keep[:, :, 0:1], 0.0), [k1])
        k2 = p.op("vector", lambda e: e.memset(keep2[:], 1.0))
        k2 = p.op("vector", lambda e: e.memset(keep2[:, :, KB - 1:KB], 0.0), [k2])
        a = p.op("vector", lambda e: e.tensor_scalar(m["MF"][:], m["FM"][:], -BIG, None, ALU.mult), [k2])
        a = p.op("vector", lambda e: e.memset(m["MF"][:, :, 0:1], -BIG), [a])
        a = p.op("vector", lambda e: e.tensor_scalar(m["MB"][:], m["isl"][:], -BIG, None, ALU.mult), [v6])
        a = p.op("vector", lambda e: e.memset(m["MB"][:, :, KB - 1:KB], -BIG), [a])

        def flat(t):
            return t[:].rearrange("p b k -> p (b k)")

        a1 = p.op("vector", lambda e: e.tensor_tensor_scan(flat(prev), flat(keep), flat(m["FM"]), 0.0, ALU.mult, ALU.max), [a])
        a2 = p.op("vector", lambda e: e.tensor_tensor_scan(flat(nxt)[:, ::-1], flat(keep2)[:, ::-1], flat(m["isl"])[:, ::-1], 0.0, ALU.mult, ALU.max), [a])
        a3 = p.op("vector", lambda e: e.tensor_scalar(m["FM"][:], prev[:], -BIG, None, ALU.mult), [a1])
        a4 = p.op("vector", lambda e: e.tensor_scalar(m["LM"][:], nxt[:], -BIG, None, ALU.mult), [a2])
        t3 = p.op("tensor", lambda e: e.matmul(pc[:, 0, :], m["FM"][:, :, KB - 1], net.ident[:], start=True, stop=True), [a3])
        t4 = p.op("tensor", lambda e: e.matmul(pc[:, 1, :], m["LM"][:, :, 0], net.ident[:], start=True, stop=True), [a4])
        v7 = p.op("vector", lambda e: e.tensor_copy(rows[:], pc[:]), [t3, t4])
        p.dma("sync", "gfr", lambda e: e.dma_start(net.gfr.rearrange("s b n -> b s n"), rows[:]), [v7])
        p.finish()
    return m


def layernorm(net, p, src, c2, name, after):
    st = net.sb(name + "_st", [128, NT, 6], ctx=c2)
    mv = net.sb(name + "_mv", [128, NT, 2], ctx=c2)
    rs = net.sb(name + "_rs", [128, NT], ctx=c2)
    nb = net.sb(name + "_nb", [128, NT], ctx=c2)
    for t in range(NT):
        a = p.op("vector", lambda e, t=t: e.bn_stats(st[:, t, :], src[:, t, :]), after[t] if isinstance(after, list) else after)
    for t in range(NT):
        a = p.op("vector", lambda e, t=t: e.bn_aggr(mv[:, t, :], st[:, t, :]), [a] if t == 0 else ())
    s = p.op("scalar", lambda e: e.activation(rs[:], mv[:, :, 1], ACT.Sqrt, bias=net.eps[:]), [a])
    r = p.op("vector", lambda e: e.reciprocal(rs[:], rs[:]), [s])
    n = p.op("vector", lambda e: e.scalar_tensor_tensor(nb[:], mv[:, :, 0], -1.0, rs[:], ALU.mult, ALU.mult), [r])
    return rs, nb, n


def nodes(net, kind, dinv=None):
    nc, io = net.nc, net.io
    nm = f"n{kind}"
    H = {0: 8, 1: 0, 2: 1, 3: 1, 4: 0}[kind]
    W = {0: 136, 1: 128, 2: 129, 3: 129, 4: 128}[kind]
    tab = net.tabs[str(kind)]
    with ExitStack() as c2:
        p = Plan(nc, net.ctx, nm)

        def load(name, shape, ap):
            t = net.sb(nm + name, shape, ctx=c2)
            return t, p.dma("sync", "w_" + name, lambda e: e.dma_start(t[:], ap))

        def col(ap):
            return ap.rearrange("(p o) -> p o", o=1)

        ready = []
        if kind == 0:
            Wm, k = load("W", [128, 128], io["L0_gnn_W_in"]); ready.append(k)
            Wa = net.sb(nm + "Wa", [128, 16], ctx=c2)
            ready.append(p.dma("sync", "w_a", lambda e: e.dma_start(Wa[:, 0:8], io["L0_gnn_W_u"])))
            ready.append(p.dma("sync", "w_a", lambda e: e.dma_start(Wa[:, 8:16], io["L0_gnn_W_v"])))
            gam, k = load("gam", [128, 1], col(io["L0_gnn_ln_gamma"])); ready.append(k)
            bet, k = load("bet", [128, 1], col(io["L0_gnn_ln_beta"])); ready.append(k)
            bcol, k = load("bcol", [128, 1], col(io["L0_gnn_b_in"])); ready.append(k)
            brow, k = load("brow", [128, 128], row_bcast(io["L0_gnn_b_in"], 128)); ready.append(k)
            burow, k = load("burow", [128, 8], row_bcast(io["L0_gnn_b_u"], 128)); ready.append(k)
        elif kind == 1:
            Wm, k = load("W", [128, 128], io["L1_gnn_W"]); ready.append(k)
        elif kind in (2, 3):
            s = str(kind - 1)
            Wm, k = load("W", [128, 128], io["L2_gnn_W" + s]); ready.append(k)
            Wa = net.sb(nm + "Wa", [128, 2], ctx=c2)
            ready.append(p.dma("sync", "w_a", lambda e: e.dma_start(Wa[:, 0:1], col(io["L2_gnn_as" + s]))))
            ready.append(p.dma("sync", "w_a", lambda e: e.dma_start(Wa[:, 1:2], col(io["L2_gnn_ad" + s]))))
        else:
            Wm = net.sb(nm + "W", [128, 384], ctx=c2)
            z = p.op("vector", lambda e: e.memset(Wm[:], 0.0))
            for j, w in enumerate(("Wq", "Wk", "Wv")):
                for h in range(4):
                    ready.append(p.dma("sync", "w_q", lambda e, j=j, w=w, h=h: e.dma_start(
                        Wm[32 * h:32 * h + 32, 128 * j + 32 * h:128 * j + 32 * h + 32], io["L3_gnn_" + w][h]), [z]))
        hn = net.sb(nm + "hn", [128, NT, 128], ctx=c2)
        if kind == 3:
            hsrc, hready = net.aux[:].rearrange("p (t c) -> p t c", c=128), [None] * NT
        else:
            rs, nb, n0 = layernorm(net, p, net.x, c2, nm + "l", ())
            hready = [p.op("scalar", lambda e, t=t: e.activation(hn[:, t, :], net.x[:, t, :], ACT.Relu, bias=nb[:, t:t + 1], scale=rs[:, t:t + 1]), [n0]) for t in range(NT)]
            if kind == 0:
                rs2, nb2, n2 = layernorm(net, p, hn, c2, nm + "m", [[x] for x in hready])
                hready = [p.op("scalar", lambda e, t=t: e.activation(hn[:, t, :], hn[:, t, :], ACT.Identity, bias=nb2[:, t:t + 1], scale=rs2[:, t:t + 1]), [n2]) for t in range(NT)]
            hsrc = hn
        hT = net.sb(nm + "hT", [128, 2, 512], ctx=c2)
        gT = net.sb(nm + "gT", [128, 2, 512], ctx=c2)
        TB = net.sb(nm + "TB", [128, 2, 4, W], ctx=c2)
        P1 = [net.ps(f"{nm}P1{i}", [128, 4, 128], c2) for i in range(2)]
        P2 = net.ps(nm + "P2", [128, 512], c2) if H else None
        P3 = [net.ps(f"{nm}P3{i}", [128, 512], c2) for i in range(3)]
        P4 = net.ps(nm + "P4", [128, 4, 16], c2) if H else None
        w = 2 * H
        accv = None if kind == 4 else net.acc[:, 0:NT * (128 + 2 * H + 2 if H else 128)].rearrange("p (t c) -> p t c", t=NT)
        stored = [None, None]
        free1, free3 = [None, None], [None, None, None]
        free2 = free4 = None
        hTfree, gTfree = [None, None], [None, None]
        n3 = 0
        sv = net.sv if H else None
        def group(g, t0, nt):
            nonlocal free2, free4, n3
            s = g % 2
            for j in range(nt):
                a = p.op("tensor", lambda e, j=j: e.transpose(P1[s][:, j, :], hsrc[:, t0 + j, :], net.ident[:]), [hready[t0 + j], free1[s]])
            L = nt * 128
            if kind == 0:
                ev = p.op("vector", lambda e: e.tensor_scalar(hT[:, s, 0:L], P1[s][:, 0:nt, :].rearrange("p a b -> p (a b)"), gam[:], bet[:], ALU.mult, ALU.add), [a, hTfree[s]] + ready)
            else:
                ev = p.op("vector", lambda e: e.tensor_copy(hT[:, s, 0:L], P1[s][:, 0:nt, :].rearrange("p a b -> p (a b)")), [a, hTfree[s]])
            free1[s] = ev
            if H:
                a = p.op("tensor", lambda e: e.matmul(P2[:, 0:L], Wm[:], hT[:, s, 0:L], start=True, stop=True), [ev, free2] + ready)
                if kind == 0:
                    e2 = p.op("scalar", lambda e: e.activation(gT[:, s, 0:L], P2[:, 0:L], ACT.Identity, bias=bcol[:]), [a, gTfree[s]] + ready)
                else:
                    e2 = p.op("scalar", lambda e: e.copy(gT[:, s, 0:L], P2[:, 0:L]), [a, gTfree[s]])
                free2 = e2
            fin = []
            if kind == 4:
                for j in range(nt):
                    b = n3 % 3
                    n3 += 1
                    a = p.op("tensor", lambda e, b=b, j=j: e.matmul(P3[b][:, 0:384], hT[:, s, 128 * j:128 * j + 128], Wm[:], start=True, stop=True), [ev, *(free3[b] or []), *ready])
                    eng = "scalar" if j % 2 else "vector"

                    def out(to, b, lo, hi, eng=eng):
                        return lambda e: (e.copy if eng == "scalar" else e.tensor_copy)(to, P3[b][:, lo:hi])

                    c = p.op(eng, out(TB[:, s, j, :], b, 0, 128), [a, stored[s]])
                    d = p.op(eng, out(net.kv[:, (t0 + j) * 256:(t0 + j + 1) * 256], b, 128, 384))
                    free3[b] = [c, d]
                    fin += [c, d]
                hTfree[s] = a
            else:
                b = n3 % 3
                n3 += 1
                for j in range(nt):
                    a = p.op("tensor", lambda e, j=j, b=b: e.matmul(P3[b][:, 128 * j:128 * j + 128], hT[:, s, 128 * j:128 * j + 128], Wm[:], start=True, stop=True), [ev, free3[b]] + ready)
                hTfree[s] = a
                src = P3[b][:, 0:L].rearrange("p (a c) -> p a c", c=128)
                if kind == 0:
                    c = p.op("vector", lambda e, src=src: e.tensor_tensor(TB[:, s, 0:nt, 0:128], src, brow[:].rearrange("p (a c) -> p a c", a=1).broadcast_to([128, nt, 128]), ALU.add), [a, stored[s]])
                elif kind == 1:
                    for j in range(nt):
                        c = p.op("vector", lambda e, b=b, j=j: e.tensor_scalar(TB[:, s, j, 0:128], P3[b][:, 128 * j:128 * j + 128], net.dinv[:, t0 + j:t0 + j + 1], None, ALU.mult), [a, stored[s]])
                    fin.append(p.op("scalar", lambda e: e.copy(accv[:, t0:t0 + nt, 0:128], TB[:, s, 0:nt, 0:128]), [c]))
                else:
                    c = p.op("vector", lambda e, src=src: e.tensor_copy(TB[:, s, 0:nt, 0:128], src), [a, stored[s]])
                    fin.append(p.op("scalar", lambda e: e.copy(accv[:, t0:t0 + nt, 0:128], TB[:, s, 0:nt, 0:128]), [c]))
                free3[b] = c
                fin.append(c)
                if H:
                    for j in range(nt):
                        a = p.op("tensor", lambda e, j=j: e.matmul(P4[:, j, 0:w], gT[:, s, 128 * j:128 * j + 128], Wa[:], start=True, stop=True), [e2, free4])
                    gTfree[s] = a
                    if kind == 0:
                        c = p.op("vector", lambda e: e.tensor_tensor(TB[:, s, 0:nt, 128:136], P4[:, 0:nt, 0:8], burow[:].rearrange("p (a c) -> p a c", a=1).broadcast_to([128, nt, 8]), ALU.add), [a])
                    else:
                        c = p.op("vector", lambda e: e.tensor_copy(TB[:, s, 0:nt, 128:129], P4[:, 0:nt, 0:1]), [a])
                    d = p.op("vector", lambda e: e.tensor_copy(sv[:, t0:t0 + nt, 0:H], P4[:, 0:nt, H:2 * H]), [a])
                    free4 = d
                    fin += [c, d]
                    if kind != 0:
                        d = p.op("vector", lambda e: e.tensor_tensor(accv[:, t0:t0 + nt, 129:130], TB[:, s, 0:nt, 128:129], sv[:, t0:t0 + nt, 0:1], ALU.add), [d])
                        d = p.op("vector", lambda e: e.scalar_tensor_tensor(accv[:, t0:t0 + nt, 129], accv[:, t0:t0 + nt, 129], 0.2, accv[:, t0:t0 + nt, 129], ALU.mult, ALU.max), [d])
                        fin.append(d)
            st = p.dma("sync", f"tab{s}", lambda e: e.dma_start(tab[t0 * 128:(t0 + nt) * 128, :].rearrange("(t q) c -> q t c", q=128), TB[:, s, 0:nt, :]), fin)
            stored[s] = st

        for g, (t0, nt) in enumerate(GROUPS):
            group(g, t0, nt)
        if kind == 0:
            p.op("vector", lambda e: e.memset(net.acc[:], 0.0))
            z = p.counts["vector"]
            p.op("vector", lambda e: e.memset(accv[:, :, 136:144], -BIG), [("vector", z)])
        if kind in (2, 3):
            p.op("vector", lambda e: e.memset(accv[:, :, 128:129], 1.0))
        p.finish()


def steps(e, t0, b, regs):
    if "hi" not in regs:
        regs["lo"] = e.value_load(t0[0:1, b:b + 1], min_val=0, max_val=NT - 1)
    else:
        regs["lo"] = regs["hi"]
    regs["hi"] = e.value_load(t0[0:1, b + 1:b + 2], min_val=0, max_val=NT - 1)
    return regs["lo"], regs["hi"]


def edges(net, kind, m=None):
    nc = net.nc
    nm = f"e{kind}"
    H = {0: 8, 1: 0, 2: 1, 3: 1}[kind]
    WT = {0: 136, 1: 128, 2: 129, 3: 129}[kind]
    W = 128 + 2 * H + 2 if H else 128
    R = 3 if H else 4
    tab = net.tabs[str(kind)]
    with ExitStack() as c2:
        p = Plan(nc, net.ctx, nm)
        G = [net.sb(f"{nm}G{i}", [128, KB, WT], ctx=c2) for i in range(R)]
        S = net.sb(nm + "S", [128, KB, 128], ctx=c2)
        dl = net.sb(nm + "dl", [128, KB], ctx=c2)
        PA = net.ps(nm + "PA", [128, W], c2)
        dum = net.sb(nm + "dum", [128, 1], ctx=c2)
        sa, sp_, sc = p.sem("aggv"), p.sem("aggp"), p.sem("aggs")
        for k in ("aggv", "aggp", "aggs"):
            del p.counts[k]
        KA = 1 + KB + {0: 1, 1: 8, 8: 10}[H]
        if H:
            MSG = [net.sb(f"{nm}M{i}", [128, KB, W], ctx=c2) for i in range(2)]
            ST = net.sb(nm + "ST", [128, EB], ctx=c2)
            DR = [net.sb(f"{nm}DR{i}", [128, EB], I32, ctx=c2) for i in range(2)]
            GR = [net.sb(f"{nm}GR{i}", [H, 2, 128], ctx=c2) for i in range(2)]
            zb = net.sb(nm + "zb", [128, 128], BF16, ctx=c2)
            EH = net.sb(nm + "EH", [128, H, KB], ctx=c2)
            FF = net.sb(nm + "FF", [128, H, KB], ctx=c2)
            BB = net.sb(nm + "BB", [128, H, KB], ctx=c2)
            T1 = net.sb(nm + "T1", [128, H, KB], ctx=c2)
            T2 = net.sb(nm + "T2", [128, H, KB], ctx=c2)
            MFH = net.sb(nm + "MFH", [128, H, KB], ctx=c2)
            MBH = net.sb(nm + "MBH", [128, H, KB], ctx=c2)
            RF = net.sb(nm + "RF", [H, 129], ctx=c2)
            RB = net.sb(nm + "RB", [H, 129], ctx=c2)
            sm = net.sb(nm + "sm", [128, 4 * H + 4], ctx=c2)
            ac = net.sb(nm + "ac", [128, 2 * H], ctx=c2)
            tmp = net.sb(nm + "tmp", [128, 136], ctx=c2)
            PX = net.ps(nm + "PX", [128, KB, H], c2)
            PT = [net.ps(f"{nm}PT{i}", [H, 128], c2) for i in range(2)]
            PC = net.ps(nm + "PC", [128, 2, H], c2)
            xv, xp = p.sem("expv"), p.sem("expp")
            del p.counts["expv"], p.counts["expp"]
            z1 = p.op("vector", lambda e: e.memset(zb[:], 0.0))
            for i in range(2):
                p.op("vector", lambda e, i=i: e.memset(MSG[i][:, :, W - 1:W], 1.0))
            z2 = p.op("vector", lambda e: e.memset(RF[:, 0:1], -BIG))
            z2 = p.op("vector", lambda e: e.memset(RB[:, 128:129], -BIG))
            p.raw("tensor", lambda e: e.sem_inc(xp, 1))
        regs = {k: {} for k in ("vector", "tensor", "scalar")}
        gfree = [None] * R
        drfree = [None, None]
        msgfree = [None, None]
        gtok = {}
        drtok = {}

        def gather(b):
            s = b % R
            for k in range(KB):
                gtok[b] = p.dma("gpsimd", f"g{s}", lambda e, k=k: e.indirect_dma_start(
                    G[s][:, k, :], None, tab, bass.IndirectOffsetOnAxis(net.srcS[:, b * KB + k:b * KB + k + 1], 0)), [gfree[s]])

        def load_rows(b):
            s = b % 2
            drtok[b] = [p.dma("sync", f"dr{s}", lambda e: e.dma_start(DR[s][:], row_bcast(net.dstp[b * EB:(b + 1) * EB], 128)), [drfree[s]]),
                        p.dma("sync", f"gr{s}", lambda e: e.dma_start(GR[s][:], bass.AP(net.gfr.tensor, net.gfr.offset + b * 128, [[0, H], [NB * 128, 2], [1, 128]])), [drfree[s]])]

        for b in range(min(R, NB)):
            gather(b)
        if H:
            load_rows(0)
            load_rows(1)
        for b in range(NB):
            g = G[b % R]
            for q in ("vector", "tensor") + (("scalar",) if H else ()):
                p.raw(q, lambda e, q=q, b=b: steps(e, net.t0, b, regs[q]))
            if H:
                dr, gr, M = DR[b % 2], GR[b % 2], MSG[b % 2]
                zz = p.op("tensor", lambda e: e.matmul(PX[:].rearrange("p k h -> p (k h)"), zb[:], zb[:, 0:KB * H], start=True, stop=False, skip_group_check=True), [z1, msgfree[(b + 1) % 2]])

                def expand_v(e, b=b, dr=dr):
                    lo, hi = regs["vector"]["lo"], regs["vector"]["hi"]
                    with e.Fori(lo, hi + 1) as t:
                        e.wait_ge(xp, t + (b + 1))
                        e.tensor_scalar(ST[:], dr[:], net.jt[:, bass.ds(t, 1)], None, ALU.is_equal).then_inc(xv, 1)

                def expand_p(e, b=b):
                    lo, hi = regs["tensor"]["lo"], regs["tensor"]["hi"]
                    with e.Fori(lo, hi + 1) as t:
                        e.wait_ge(xv, t + (b + 1))
                        for k in range(KB):
                            i = e.matmul(PX[:, k, :], ST[:, k:EB:KB], net.svf[:, bass.ds(t * 8, H)], start=False, stop=False, skip_group_check=True)
                        i.then_inc(xp, 1)

                p.raw("vector", expand_v, [drtok[b][0]])
                p.raw("tensor", expand_p)
                p.raw("vector", lambda e, b=b: e.wait_ge(xp, regs["vector"]["hi"] + (b + 2)))
                if H > 1:
                    p.op("scalar", lambda e, b=b: e.copy(MFH[:], m["MF"][:, b:b + 1, :].broadcast_to([128, H, KB])), [msgfree[(b + 1) % 2]])
                    mk = p.op("scalar", lambda e, b=b: e.copy(MBH[:], m["MB"][:, b:b + 1, :].broadcast_to([128, H, KB])))
                    mf, mb = MFH[:].rearrange("p h k -> p (h k)"), MBH[:].rearrange("p h k -> p (h k)")
                else:
                    mk = None
                    mf, mb = m["MF"][:, b, :], m["MB"][:, b, :]
                v = p.op("vector", lambda e, g=g: e.tensor_tensor(EH[:], g[:, :, 128:128 + H].rearrange("p k h -> p h k"), PX[:].rearrange("p k h -> p h k"), ALU.add), [gtok[b]])
                v = p.op("vector", lambda e: e.scalar_tensor_tensor(EH[:], EH[:], 0.2, EH[:], ALU.mult, ALU.max), [v])

                def fl(t):
                    return t[:].rearrange("p h k -> p (h k)")

                f1 = p.op("vector", lambda e, mf=mf: e.tensor_tensor_scan(fl(FF), mf, fl(EH), -BIG, ALU.add, ALU.max), [v, mk])
                f2 = p.op("vector", lambda e, mb=mb: e.tensor_tensor_scan(fl(BB)[:, ::-1], mb[:, ::-1], fl(EH)[:, ::-1], -BIG, ALU.add, ALU.max), [v, mk])
                t1 = p.op("tensor", lambda e: e.matmul(PT[0][:], FF[:, :, KB - 1], net.ident[:], start=True, stop=True), [f1])
                t2 = p.op("tensor", lambda e: e.matmul(PT[1][:], BB[:, :, 0], net.ident[:], start=True, stop=True), [f2])
                r1 = p.op("vector", lambda e, gr=gr: e.tensor_tensor_scan(RF[:, 1:129], gr[:, 0, :], PT[0][:], -BIG, ALU.add, ALU.max), [t1, z2, drtok[b][1]])
                r2 = p.op("vector", lambda e, gr=gr: e.tensor_tensor_scan(RB[:, 0:128][:, ::-1], gr[:, 1, :][:, ::-1], PT[1][:, ::-1], -BIG, ALU.add, ALU.max), [t2])
                drfree[b % 2] = r2
                c1 = p.op("tensor", lambda e: e.matmul(PC[:, 0, :], RF[:, 0:128], net.ident[0:H, 0:H], start=True, stop=True), [r1])
                c_ = p.op("tensor", lambda e: e.matmul(PC[:, 1, :], RB[:, 1:129], net.ident[0:H, 0:H], start=True, stop=True), [r2])
                v = p.op("vector", lambda e, b=b: e.tensor_tensor(T1[:], m["FM"][:, b:b + 1, :].broadcast_to([128, H, KB]), PC[:, 0, :].rearrange("p (h o) -> p h o", o=1).broadcast_to([128, H, KB]), ALU.add), [c_])
                v = p.op("vector", lambda e, b=b: e.tensor_tensor(T2[:], m["LM"][:, b:b + 1, :].broadcast_to([128, H, KB]), PC[:, 1, :].rearrange("p (h o) -> p h o", o=1).broadcast_to([128, H, KB]), ALU.add), [c_])
                v = p.op("vector", lambda e: e.tensor_tensor(T1[:], T1[:], FF[:], ALU.max), [v])
                v2 = p.op("vector", lambda e: e.tensor_tensor(T2[:], T2[:], BB[:], ALU.max), [v])
                v = p.op("vector", lambda e: e.tensor_tensor(T1[:], T1[:], T2[:], ALU.max), [v2])
                v3 = p.op("vector", lambda e: e.tensor_tensor(T2[:], EH[:], T1[:], ALU.subtract), [v])
                ex = p.op("scalar", lambda e, M=M: e.activation(M[:, :, 128:128 + H], T2[:].rearrange("p h k -> p k h"), ACT.Exp), [v3])
                il = p.op("scalar", lambda e, M=M, b=b: e.copy(M[:, :, 128 + 2 * H], m["isl"][:, b, :]))
                p.op("vector", lambda e, M=M, b=b: e.tensor_tensor(M[:, :, 128 + H:128 + 2 * H], T1[:].rearrange("p h k -> p k h"), m["isl"][:, b, :].rearrange("p (k o) -> p k o", o=1).broadcast_to([128, KB, H]), ALU.mult))
                if H > 1:
                    mm = p.op("vector", lambda e, M=M, g=g: e.tensor_tensor(
                        M[:, :, 0:128].rearrange("p k (d h) -> p k d h", h=H), g[:, :, 0:128].rearrange("p k (d h) -> p k d h", h=H),
                        M[:, :, 128:128 + H].rearrange("p k (o h) -> p k o h", o=1).broadcast_to([128, KB, 128 // H, H]), ALU.mult), [ex, il])
                else:
                    mm = p.op("vector", lambda e, M=M, g=g: e.tensor_tensor(
                        M[:, :, 0:128], g[:, :, 0:128], M[:, :, 128:129].broadcast_to([128, KB, 128]), ALU.mult), [ex, il])
                gfree[b % R] = mm
                rhs = [M[:, k, :] for k in range(KB)]
                if b + R < NB:
                    gather(b + R)
                if b + 2 < NB:
                    load_rows(b + 2)
                ready = [mm]
            else:
                rhs = [g[:, k, :] for k in range(KB)]
                ready = [gtok[b]]

            def agg_v(e, b=b):
                lo, hi = regs["vector"]["lo"], regs["vector"]["hi"]
                with e.Fori(lo, hi + 1) as t:
                    i = t + b
                    n = [0]

                    def done(ins, wait=True):
                        n[0] += 1
                        ins.then_inc(sa, 1)
                        if wait:
                            e.wait_ge(sa, i * KA + n[0])

                    done(e.tensor_scalar(dl[:], net.dstS[:, b, :], net.tb[:, bass.ds(t, 1)], None, ALU.subtract))
                    for k in range(KB):
                        done(e.tensor_scalar(S[:, k, :], net.iota[:], dl[:, k:k + 1], None, ALU.is_equal), False)
                    A = net.acc[:, bass.ds(t * W, W)]
                    e.wait_ge(sp_, i + 1)
                    if not H:
                        done(e.tensor_tensor(A, A, PA[:], ALU.add), False)
                    else:
                        mo = 128 + H
                        done(e.tensor_scalar(sm[:, 0:1], PA[:, mo + H:mo + H + 1], -1.0, BIG, ALU.add, ALU.mult))
                        done(e.tensor_scalar(sm[:, 4:4 + H], PA[:, mo:mo + H], sm[:, 0:1], None, ALU.add))
                        Am = net.acc[:, bass.ds(t * W + mo, H)]
                        done(e.tensor_tensor(sm[:, 4 + H:4 + 2 * H], Am, sm[:, 4:4 + H], ALU.max))
                        done(e.tensor_tensor(sm[:, 4 + 2 * H:4 + 3 * H], Am, sm[:, 4 + H:4 + 2 * H], ALU.subtract), False)
                        done(e.tensor_tensor(sm[:, 4 + 3 * H:4 + 4 * H], sm[:, 4:4 + H], sm[:, 4 + H:4 + 2 * H], ALU.subtract))
                        done(e.tensor_scalar(Am, sm[:, 4 + H:4 + 2 * H], 1.0, None, ALU.mult), False)
                        e.wait_ge(sc, i + 1)
                        nh = 128 // H + 1
                        An = net.acc[:, bass.ds(t * W, 128 + H)]
                        if H > 1:
                            An3 = An.rearrange("p (d h) -> p d h", h=H)
                            done(e.tensor_tensor(An3, An3, ac[:, 0:H].rearrange("p (o h) -> p o h", o=1).broadcast_to([128, nh, H]), ALU.mult), False)
                            done(e.tensor_tensor(tmp[:].rearrange("p (d h) -> p d h", h=H), PA[:, 0:128 + H].rearrange("p (d h) -> p d h", h=H), ac[:, H:2 * H].rearrange("p (o h) -> p o h", o=1).broadcast_to([128, nh, H]), ALU.mult))
                            done(e.tensor_tensor(An, An, tmp[:], ALU.add), False)
                        else:
                            done(e.tensor_scalar(An, An, ac[:, 0:1], None, ALU.mult))
                            done(e.scalar_tensor_tensor(An, PA[:, 0:129], ac[:, 1:2], An, ALU.mult, ALU.add), False)
                        Ac = net.acc[:, bass.ds(t * W + W - 1, 1)]
                        if kind == 0:
                            done(e.tensor_tensor(Ac, Ac, PA[:, W - 1:W], ALU.add), False)
                    assert n[0] == KA, (n[0], KA)
                    e.wait_ge(sa, i * KA + KA)

            def agg_p(e, b=b, rhs=rhs):
                lo, hi = regs["tensor"]["lo"], regs["tensor"]["hi"]
                with e.Fori(lo, hi + 1) as t:
                    i = t + b
                    for k in range(KB):
                        e.wait_ge(sa, i * KA + (2 + k))
                        ins = e.matmul(PA[:], S[:, k, :], rhs[k], start=(k == 0), stop=(k == KB - 1))
                    ins.then_inc(sp_, 1)

            def agg_s(e, b=b):
                lo, hi = regs["scalar"]["lo"], regs["scalar"]["hi"]
                with e.Fori(lo, hi + 1) as t:
                    i = t + b
                    e.wait_ge(sa, i * KA + (1 + KB + 5))
                    e.activation(ac[:], sm[:, 4 + 2 * H:4 + 4 * H], ACT.Exp).then_inc(sc, 1)

            p.raw("vector", agg_v)
            p.raw("tensor", agg_p, ready)
            if H:
                p.raw("scalar", agg_s)
            d = p.op("vector", lambda e: e.memset(dum[:], 0.0))
            if H:
                msgfree[b % 2] = d
            else:
                gfree[b % R] = d
                if b + R < NB:
                    gather(b + R)
        p.finish()


def final_attention(net, kind):
    nc, io = net.nc, net.io
    nm = f"f{kind}"
    H = 8 if kind == 0 else 1
    W = 128 + 2 * H + 2
    A = net.acc[:, 0:NT * W].rearrange("p (t c) -> p t c", t=NT)
    with ExitStack() as c2:
        p = Plan(nc, net.ctx, nm)
        rd = net.sb(nm + "rd", [128, NT, H], ctx=c2)
        r2 = net.sb(nm + "r2", [128, NT, H], ctx=c2)
        bias = net.sb(nm + "b", [128, 128], ctx=c2)
        bname = {0: "L0_gnn_b_ff", 2: "L2_gnn_b1", 3: "L2_gnn_b2"}[kind]
        lb = p.dma("sync", "b", lambda e: e.dma_start(bias[:], row_bcast(io[bname], 128)))
        v = p.op("vector", lambda e: e.tensor_scalar(r2[:], A[:, :, 128:128 + H], 0.0, None, ALU.is_equal))
        v = p.op("vector", lambda e: e.tensor_tensor(rd[:], r2[:], A[:, :, 128:128 + H], ALU.add), [v])
        v = p.op("vector", lambda e: e.reciprocal(rd[:], rd[:]), [v])
        if kind != 0:
            o = net.sb(nm + "o", [128, NT, 128], ctx=c2)
            for t in range(NT):
                p.op("vector", lambda e, t=t: e.scalar_tensor_tensor(o[:, t, :], A[:, t, 0:128], rd[:, t, :], bias[:], ALU.mult, ALU.add), [v, lb])
            last = ("vector", p.counts["vector"])
            if kind == 2:
                p.op("scalar", lambda e: e.activation(net.aux[:], o[:].rearrange("p t c -> p (t c)"), ACT.Relu), [last])
            else:
                p.op("vector", lambda e: e.tensor_tensor(net.x[:], net.x[:], o[:], ALU.add), [last])
            p.finish()
            return
        Wf = net.sb(nm + "Wf", [128, 128], ctx=c2)
        lw = p.dma("sync", "w", lambda e: e.dma_start(Wf[:], io["L0_gnn_W_ff"]))
        o = net.sb(nm + "o", [128, 3, 128], ctx=c2)
        oT = net.sb(nm + "oT", [128, 3, 128], ctx=c2)
        P1 = [net.ps(f"{nm}p{i}", [128, 128], c2) for i in range(3)]
        P2 = [net.ps(f"{nm}q{i}", [128, 128], c2) for i in range(3)]
        dg = net.sb(nm + "dg", [128, NT], ctx=c2)
        c = p.op("vector", lambda e: e.tensor_scalar(dg[:], A[:, :, W - 1], 1.0, None, ALU.add))
        c = p.op("scalar", lambda e: e.activation(dg[:], dg[:], ACT.Sqrt), [c])
        p.op("vector", lambda e: e.reciprocal(net.dinv[:], dg[:]), [c])
        xb = None
        for t in range(NT):
            xb = p.op("gpsimd", lambda e, t=t: e.tensor_tensor(net.x[:, t, :], net.x[:, t, :], bias[:], ALU.add), [lb])
        free = [[None] * 3 for _ in range(3)]
        free3 = [None] * 3
        for t in range(NT):
            s = t % 3
            a = p.op("vector", lambda e, t=t, s=s: e.tensor_tensor(o[:, s, :].rearrange("p (d h) -> p d h", h=8), A[:, t, 0:128].rearrange("p (d h) -> p d h", h=8), rd[:, t:t + 1, :].broadcast_to([128, 16, 8]), ALU.mult), [v, free[0][s]])
            b = p.op("tensor", lambda e, s=s: e.transpose(P1[s][:], o[:, s, :], net.ident[:]), [a, free[1][s]])
            free[0][s] = b
            c = p.op("scalar", lambda e, s=s: e.copy(oT[:, s, :], P1[s][:]), [b, free[2][s]])
            free[1][s] = c
            d = p.op("tensor", lambda e, s=s: e.matmul(P2[s][:], oT[:, s, :], Wf[:], start=True, stop=True), [c, lw, free3[s]])
            free[2][s] = d
            f = p.op("vector", lambda e, t=t, s=s: e.tensor_tensor(net.x[:, t, :], net.x[:, t, :], P2[s][:], ALU.add), [d, xb])
            free3[s] = f
        p.finish()


def final_conv(net):
    nc, io = net.nc, net.io
    A = net.acc[:, 0:NT * 128].rearrange("p (t c) -> p t c", t=NT)
    with ExitStack() as c2:
        p = Plan(nc, net.ctx, "f1")
        rows = net.sb("f1r", [128, 3, 128], ctx=c2)
        lb = [p.dma("sync", "b", lambda e, j=j, n=n: e.dma_start(rows[:, j, :], row_bcast(io[n], 128)))
              for j, n in enumerate(("L1_gnn_b", "L1_gnn_gamma", "L1_gnn_beta"))][-1]
        ones = net.sb("f1o", [128, 2, 128], ctx=c2)
        cm = net.sb("f1c", [128, 1], ctx=c2)
        mean = net.sb("f1m", [128, 128], ctx=c2)
        sq = net.sb("f1s", [128, NT, 128], ctx=c2)
        PM = net.ps("f1pm", [128, 128], c2)
        PV = net.ps("f1pv", [128, 128], c2)
        o = p.op("vector", lambda e: e.memset(ones[:, 0, :], 1.0))
        o = p.op("vector", lambda e: e.tensor_scalar(cm[:], net.jt[:, 0:1], float(TAIL), None, ALU.is_lt), [o])
        o = p.op("vector", lambda e: e.tensor_scalar(ones[:, 1, :], ones[:, 0, :], cm[:], None, ALU.mult), [o])
        for t in range(NT):
            a = p.op("vector", lambda e, t=t: e.scalar_tensor_tensor(A[:, t, :], A[:, t, :], net.dinv[:, t:t + 1], rows[:, 0, :], ALU.mult, ALU.add), [lb])
            q = p.op("tensor", lambda e, t=t: e.matmul(PM[:], ones[:, int(t == NT - 1), :], A[:, t, :], start=(t == 0), stop=(t == NT - 1)), [a, o])
        v = p.op("vector", lambda e: e.tensor_scalar(mean[:], PM[:], 1.0 / N, None, ALU.mult), [q])
        for t in range(NT):
            a = p.op("vector", lambda e, t=t: e.tensor_tensor(A[:, t, :], A[:, t, :], mean[:], ALU.subtract), [v])
            s = p.op("scalar", lambda e, t=t: e.activation(sq[:, t, :], A[:, t, :], ACT.Square), [a])
            q = p.op("tensor", lambda e, t=t: e.matmul(PV[:], ones[:, int(t == NT - 1), :], sq[:, t, :], start=(t == 0), stop=(t == NT - 1)), [s])
        s = p.op("scalar", lambda e: e.activation(mean[:], PV[:], ACT.Sqrt, bias=net.eps[:], scale=1.0 / N), [q])
        v = p.op("vector", lambda e: e.reciprocal(mean[:], mean[:]), [s])
        v = p.op("vector", lambda e: e.tensor_tensor(mean[:], mean[:], rows[:, 1, :], ALU.mult), [v])
        v = p.op("vector", lambda e: e.tensor_tensor(A, A, mean[:].rearrange("p (o c) -> p o c", o=1).broadcast_to([128, NT, 128]), ALU.mult), [v])
        v = p.op("vector", lambda e: e.tensor_tensor(A, A, rows[:, 2:3, :].broadcast_to([128, NT, 128]), ALU.add), [v])
        v = p.op("vector", lambda e: e.scalar_tensor_tensor(net.x[:].rearrange("p t c -> p (t c)"), net.acc[:, 0:NT * 128], 0.0, net.x[:].rearrange("p t c -> p (t c)"), ALU.max, ALU.add), [v])
        p.finish()


def pairs(net):
    nc, io = net.nc, net.io
    nm = "pr"
    R, RA, KH, EH, NH = 3, 4, 8, 1024, 98
    tab = net.tabs["4"]
    with ExitStack() as c2:
        p = Plan(nc, net.ctx, nm)
        sb = lambda n, s, dt=F32: net.sb(nm + n, s, dt, ctx=c2)
        pm, srcF = sb("pm", [128, 784]), sb("srcF", [128, 784])
        srcC = sb("srcC", [128, 784], I32)
        t0h = sb("t0h", [1, NH + 1], I32)
        G = [sb(f"G{i}", [128, KH, 128]) for i in range(R)]
        MSG = sb("MSG", [128, KH, 128])
        OUT = [sb(f"OUT{i}", [128, KH, 128]) for i in range(2)]
        EQ = [sb(f"EQ{i}", [128, KH, 128]) for i in range(2)]
        ST = sb("ST", [128, EH])
        DR = [sb(f"DR{i}", [128, EH], I32) for i in range(2)]
        SR = [sb(f"SR{i}", [128, EH], I32) for i in range(2)]
        EA = [sb(f"EA{i}", [36, EH]) for i in range(2)]
        hr, hs = sb("hr", [128, 2, 512]), sb("hs", [128, 2, 512])
        w1 = sb("w1", [36, 128])
        w2 = sb("w2", [128, 2, 128])
        b1 = sb("b1", [128, 2])
        b2 = sb("b2", [128, 2, 128])
        bb = sb("bb", [128, 4, 128])
        zb = sb("zb", [128, 512], BF16)
        low = sb("low", [128, 128])
        one = sb("one", [128, 128])
        u = sb("u", [128, 512])
        al = sb("al", [128, 16])
        cnt = sb("cnt", [128, KH])
        junk = sb("junk", [128, 128])
        ti = sb("ti", [128, KH])
        trash = sb("trash", [128, 1])
        idx = [sb(f"idx{i}", [128, KH], I32) for i in range(3)]
        dum = sb("dum", [128, 1])
        PQ = net.ps(nm + "PQ", [128, KH, 256], c2)
        PH = [net.ps(f"{nm}PH{i}", [128, 512], c2) for i in range(2)]
        PW = net.ps(nm + "PW", [128, 512], c2)
        PS = net.ps(nm + "PS", [128, 4, 128], c2)
        xv, xp = p.sem("expv"), p.sem("expp")
        for k in ("expv", "expp"):
            del p.counts[k]
        with ExitStack() as c3:
            rw = net.sb(nm + "rw", [112, 7, 128], I32, ctx=c3)
            rf = net.sb(nm + "rf", [112, 7, 128], ctx=c3)
            rg = net.sb(nm + "rg", [112, 7, 128], ctx=c3)

            def turn(ready, out, last):
                for j in range(7):
                    q = p.op("tensor", lambda e, j=j: e.transpose(PH[0][:, 0:112], rf[:, j, :], net.ident[0:112, 0:112]), [ready, last])
                    last = p.op("vector", lambda e, j=j: e.tensor_copy(out[:, 112 * j:112 * j + 112], PH[0][:, 0:112]), [q])
                return last

            l = p.dma("sync", "rw", lambda e: e.dma_start(rw[:], net.srcp.rearrange("(j q n) -> q j n", q=112, n=128)))
            v = p.op("vector", lambda e: e.tensor_copy(rf[:], rw[:]), [l])
            v = turn(v, srcF, None)
            v = p.op("vector", lambda e: e.tensor_copy(srcC[:], srcF[:]), [v])
            v = p.op("vector", lambda e: e.memset(rf[:], 0.0), [("tensor", p.counts["tensor"])])
            v2 = p.op("vector", lambda e: e.memset(rg[:], 0.0))
            ls = []
            for tgt, n in ((rf, "edge_weight"), (rg, "edge_weight_n2")):
                a = io[n]
                ls.append(p.dma("sync", "ph", lambda e, tgt=tgt, a=a: e.dma_start(tgt[:, 0:6, :], a[0:672 * 128].rearrange("(j q n) -> q j n", q=112, n=128)), [v, v2]))
                ls.append(p.dma("sync", "ph", lambda e, tgt=tgt, a=a: e.dma_start(tgt[0:109, 6, :], a[672 * 128:781 * 128].rearrange("(q n) -> q n", n=128))))
                ls.append(p.dma("sync", "ph", lambda e, tgt=tgt, a=a: e.dma_start(tgt[109:110, 6, 0:32], a[781 * 128:E].rearrange("(q n) -> q n", q=1))))
            v = p.op("vector", lambda e: e.scalar_tensor_tensor(rf[:], rf[:], float(1.0 / np.sqrt(np.float32(32.0))), rg[:], ALU.mult, ALU.mult), ls)
            v = turn(v, pm, v)
        l = p.dma("sync", "t0", lambda e: e.dma_start(t0h[0:1, 0:NH].rearrange("a (n o) -> a n o", o=1), net.dstp.rearrange("(b n) -> b n", n=EH)[:, 0:1].rearrange("(a b) o -> a b o", a=1), allow_slow_non_contiguous=True))
        v = p.op("vector", lambda e: e.tensor_scalar(t0h[0:1, 0:NH], t0h[0:1, 0:NH], 7, None, ALU.arith_shift_right), [l])
        v = p.op("vector", lambda e: e.memset(t0h[0:1, 0:1], 0), [v])
        tready = p.op("vector", lambda e: e.memset(t0h[0:1, NH:NH + 1], NT - 1), [v])
        ready = [p.dma("scalar", "w", lambda e: e.dma_start(w1[0:32, :], io["L3_gnn_rad_W1"])),
                 p.dma("scalar", "w", lambda e: e.dma_start(w1[32:36, :], io["L3_gnn_sph_W1"]))]
        for j, n in enumerate(("rad", "sph")):
            ready.append(p.dma("scalar", "w", lambda e, j=j, n=n: e.dma_start(w2[:, j, :], io[f"L3_gnn_{n}_W2"])))
            ready.append(p.dma("scalar", "w", lambda e, j=j, n=n: e.dma_start(b1[:, j:j + 1], io[f"L3_gnn_{n}_b1"].rearrange("(p o) -> p o", o=1))))
            ready.append(p.dma("scalar", "w", lambda e, j=j, n=n: e.dma_start(b2[:, j, :], row_bcast(io[f"L3_gnn_{n}_b2"], 128))))
        v = p.op("vector", lambda e: e.tensor_tensor(bb[:], b2[:, 0:1, :].broadcast_to([128, 4, 128]), b2[:, 1:2, :].broadcast_to([128, 4, 128]), ALU.add), ready)
        v = p.op("vector", lambda e: e.memset(zb[:], 0.0), [v])
        v = p.op("vector", lambda e: e.memset(one[:], 1.0), [v])
        z1 = p.op("vector", lambda e: e.tensor_scalar(trash[:], net.jt[:, 0:1], float(NP), None, ALU.add), [v])
        lo_ = p.op("gpsimd", lambda e: e.affine_select(out=low[:], in_=one[:], compare_op=ALU.is_gt, fill=0.0, base=0, pattern=[[-1, 128]], channel_multiplier=1), [z1])
        p.raw("tensor", lambda e: e.sem_inc(xp, 1))
        regs = {k: {} for k in ("vector", "tensor")}
        gfree, gtok, rtok, etok = [None] * R, {}, {}, {}
        rfree, eafree = [None, None], [None, None]
        scat = {}

        def gather(b, after=()):
            s = b % R
            for k in range(KH):
                gtok[b] = p.dma("gpsimd", f"g{s}", lambda e, k=k: e.indirect_dma_start(
                    G[s][:, k, :], None, tab, bass.IndirectOffsetOnAxis(srcC[:, b * KH + k:b * KH + k + 1], 0)), [gfree[s], *after])

        def load(b):
            s = b % 2
            rtok[b] = [p.dma("sync", f"dr{s}", lambda e: e.dma_start(DR[s][:], row_bcast(net.dstp[b * EH:(b + 1) * EH], 128)), [rfree[s]]),
                       p.dma("sync", f"sr{s}", lambda e: e.dma_start(SR[s][:], row_bcast(net.srcp[b * EH:(b + 1) * EH], 128)), [rfree[s]])]
            etok[b] = p.dma("sync", f"ea{s}", lambda e: e.dma_start(EA[s][:], net.attr[:, b * EH:(b + 1) * EH]), [eafree[s]])

        for b in range(R):
            gather(b, [z1])
        load(0)
        load(1)
        phf, hf, psf = [None, None], [None, None], [None, None]
        pwf = pqf = msgf = None
        outf, eqf = [None, None], [None, None]
        turns = 0
        for b in range(NH):
            g, sr, dr, ea, out, eq, ix = G[b % R], SR[b % 2], DR[b % 2], EA[b % 2], OUT[b % 2], EQ[b % 2], idx[b % 3]
            for q in ("vector", "tensor"):
                p.raw(q, lambda e, q=q, b=b: steps(e, t0h, b, regs[q]), [tready])
            for j in range(4):
                p.op("tensor", lambda e, j=j: e.matmul(PQ[:, 2 * j:2 * j + 2, :].rearrange("p a c -> p (a c)"), zb[:, 0:128], zb[:], start=True, stop=False, skip_group_check=True), [z1, pqf])

            def expand_v(e, b=b, dr=dr):
                lo, hi = regs["vector"]["lo"], regs["vector"]["hi"]
                with e.Fori(lo, hi + 1) as t:
                    e.wait_ge(xp, t + (b + 1))
                    e.tensor_scalar(ST[:], dr[:], net.jt[:, bass.ds(t, 1)], None, ALU.is_equal).then_inc(xv, 1)

            def expand_p(e, b=b):
                lo, hi = regs["tensor"]["lo"], regs["tensor"]["hi"]
                with e.Fori(lo, hi + 1) as t:
                    e.wait_ge(xv, t + (b + 1))
                    for k in range(KH):
                        i = e.matmul(PQ[:, k, :], ST[:, k * 128:k * 128 + 128], net.kv[:, bass.ds(t * 256, 256)], start=False, stop=False, skip_group_check=True)
                    i.then_inc(xp, 1)

            p.raw("vector", expand_v, [rtok[b][0]])
            p.raw("tensor", expand_p)
            for k in range(KH):
                c = slice(128 * k, 128 * k + 128)
                col = srcF[:, b * KH + k:b * KH + k + 1]
                v = p.op("vector", lambda e, c=c, k=k, col=col, sr=sr, eq=eq: e.tensor_scalar(eq[:, k, :], sr[:, c], col, None, ALU.is_equal), [rtok[b][1], eqf[b % 2]])
            for k in range(KH):
                v = p.op("vector", lambda e, k=k, eq=eq: e.scalar_tensor_tensor(junk[:], eq[:, k, :], 1.0, low[:], ALU.mult, ALU.mult, accum_out=cnt[:, k:k + 1]), [v, lo_])
            sc = srcF[:, b * KH:b * KH + KH]
            v = p.op("vector", lambda e: e.tensor_scalar(cnt[:], cnt[:], 0.5, None, ALU.is_gt), [v])
            w = p.op("vector", lambda e, sc=sc: e.tensor_scalar(ti[:], sc, -1.0, trash[:], ALU.mult, ALU.add))
            v = p.op("vector", lambda e: e.tensor_tensor(ti[:], ti[:], cnt[:], ALU.mult), [w])
            ixr = p.op("vector", lambda e, ix=ix, sc=sc: e.tensor_tensor(ix[:], ti[:], sc, ALU.add), [v, scat.get(b - 3)])
            p.raw("vector", lambda e, b=b: e.wait_ge(xp, regs["vector"]["hi"] + (b + 2)))
            rfree[b % 2] = p.op("vector", lambda e: e.memset(dum[:], 0.0))
            for j in range(2):
                c = slice(512 * j, 512 * j + 512)
                a1 = p.op("tensor", lambda e, c=c, ea=ea: e.matmul(PH[0][:], w1[0:32, :], ea[0:32, c], start=True, stop=True), [etok[b], phf[0], *ready])
                a2 = p.op("tensor", lambda e, c=c, ea=ea: e.matmul(PH[1][:], w1[32:36, :], ea[32:36, c], start=True, stop=True), [phf[1]])
                eafree[b % 2] = a2
                phf[0] = p.op("scalar", lambda e, j=j: e.activation(hr[:, j, :], PH[0][:], ACT.Silu, bias=b1[:, 0:1]), [a1, hf[j], *ready])
                phf[1] = p.op("scalar", lambda e, j=j: e.activation(hs[:, j, :], PH[1][:], ACT.Silu, bias=b1[:, 1:2]), [a2])
                for k in range(4):
                    q = slice(128 * k, 128 * k + 128)
                    p.op("tensor", lambda e, q=q, j=j: e.matmul(PW[:, q], hr[:, j, q], w2[:, 0, :], start=True, stop=False, skip_group_check=True), [phf[1], pwf])
                    hf[j] = p.op("tensor", lambda e, q=q, j=j: e.matmul(PW[:, q], hs[:, j, q], w2[:, 1, :], start=False, stop=True, skip_group_check=True))
                u4 = u[:].rearrange("p (a c) -> p a c", c=128)
                v = p.op("vector", lambda e: e.tensor_tensor(u[:], PW[:], bb[:].rearrange("p a c -> p (a c)"), ALU.add), [hf[j]])
                pwf = v
                v = p.op("vector", lambda e, j=j, u4=u4: e.tensor_tensor(u4, u4, PQ[:, 4 * j:4 * j + 4, 0:128], ALU.mult), [v])
                v = p.op("vector", lambda e, j=j, g=g, u4=u4: e.tensor_tensor(u4, u4, g[:, 4 * j:4 * j + 4, :], ALU.mult), [v, gtok[b]])
                gfree[b % R] = v
                v = p.op("vector", lambda e: e.tensor_reduce(al[:], u[:].rearrange("p (a c) -> p a c", c=32), AX.X, ALU.add), [v])
                v = p.op("vector", lambda e, b=b, j=j: e.tensor_tensor(al[:].rearrange("p (a h) -> p a h", h=4), al[:].rearrange("p (a h) -> p a h", h=4), pm[:, b * KH + 4 * j:b * KH + 4 * j + 4].rearrange("p (a o) -> p a o", o=1).broadcast_to([128, 4, 4]), ALU.mult), [v])
                v = p.op("vector", lambda e, j=j: e.tensor_tensor(
                    MSG[:, 4 * j:4 * j + 4, :].rearrange("p a (h c) -> p a h c", c=32), PQ[:, 4 * j:4 * j + 4, 128:256].rearrange("p a (h c) -> p a h c", c=32),
                    al[:].rearrange("p (a h o) -> p a h o", h=4, o=1).broadcast_to([128, 4, 4, 32]), ALU.mult), [v, msgf])
                pqf = v
                for k in range(4):
                    q = p.op("tensor", lambda e, k=k, j=j, eq=eq: e.matmul(PS[:, k, :], eq[:, 4 * j + k, :], MSG[:, 4 * j + k, :], start=True, stop=True), [v, psf[0]])
                eqf[b % 2] = q
                msgf = q
                psf[0] = p.op("scalar", lambda e, j=j, out=out: e.copy(out[:, 4 * j:4 * j + 4, :], PS[:]), [q, scat.get(b - 2)])
            if b + 2 < NH:
                load(b + 2)
            for k in range(KH):
                r = turns % RA
                turns += 1
                prev = [(f"s{r}", p.counts[f"s{r}"])] if f"s{r}" in p.counts else []
                tok = p.dma("gpsimd", f"s{r}", lambda e, k=k, r=r, out=out, ix=ix: e.indirect_dma_start(
                    net.sums[r], bass.IndirectOffsetOnAxis(ix[:, k:k + 1], 0), out[:, k, :], None, compute_op=ALU.add), [psf[0], ixr, *prev])
                scat.setdefault(b, [])
                scat[b] = tok if k == 0 else scat[b]
                scat[(b, k)] = tok
            scat[b] = [scat[(b, k)] for k in range(KH - RA, KH)]
            if b + R < NH:
                gather(b + R)
        last = [(f"s{r}", p.counts[f"s{r}"]) for r in range(RA)]
        L = [G[0], G[1], G[2], OUT[0]]
        done = ("vector", p.counts["vector"])
        lf = [None] * RA
        for t0 in range(0, NT, 8):
            n = min(8, NT - t0)
            for r in range(RA):
                ld = p.dma("sync", f"ld{r}", lambda e, r=r, t0=t0, n=n: e.dma_start(L[r][:, 0:n, :], net.sums[r][t0 * 128:(t0 + n) * 128, :].rearrange("(t q) c -> q t c", q=128)), [*last, done, lf[r]])
                lf[r] = p.op("vector", lambda e, r=r, t0=t0, n=n: e.tensor_tensor(net.x[:, t0:t0 + n, :], net.x[:, t0:t0 + n, :], L[r][:, 0:n, :], ALU.add), [ld, ("vector", p.counts["vector"])])
        a = lf[RA - 1]
        p.dma("sync", "out", lambda e: e.dma_start(io["out"][0:(NT - 1) * 128, :].rearrange("(t q) c -> q t c", q=128), net.x[:, 0:NT - 1, :]), [a])
        p.dma("sync", "out", lambda e: e.dma_start(io["out"][(NT - 1) * 128:N, :], net.x[0:TAIL, NT - 1, :]), [a])
        p.finish()


def build(nc, io):
    with ExitStack() as ctx:
        net = Net(nc, ctx, io)
        setup(net)
        with ExitStack() as c2:
            net.sv = net.sb("sv", [128, NT, 8], ctx=c2)
            net.svf = net.sv[:].rearrange("p t h -> p (t h)")
            net.acc = net.sb("acc", [128, NT * 146], ctx=c2)
            net.aux = net.sb("aux", [128, NT * 128], ctx=c2)
            m = masks(net, c2)
            nodes(net, 0)
            edges(net, 0, m)
            final_attention(net, 0)
            nodes(net, 1)
            edges(net, 1)
            final_conv(net)
            for kind in (2, 3):
                nodes(net, kind)
                edges(net, kind, m)
                final_attention(net, kind)
        net.kv = net.sb("kv", [128, NT * 256])
        nodes(net, 4)
        pairs(net)


FLOATS = ["x", "edge_weight", "edge_weight_n2", "L0_gnn_ln_gamma", "L0_gnn_ln_beta", "L0_gnn_W_in", "L0_gnn_b_in",
          "L0_gnn_W_u", "L0_gnn_b_u", "L0_gnn_W_v", "L0_gnn_W_ff", "L0_gnn_b_ff", "L1_gnn_W", "L1_gnn_b",
          "L1_gnn_gamma", "L1_gnn_beta", "L2_gnn_W1", "L2_gnn_as1", "L2_gnn_ad1", "L2_gnn_b1", "L2_gnn_W2",
          "L2_gnn_as2", "L2_gnn_ad2", "L2_gnn_b2", "L3_gnn_rad_W1", "L3_gnn_rad_b1", "L3_gnn_rad_W2",
          "L3_gnn_rad_b2", "L3_gnn_sph_W1", "L3_gnn_sph_b1", "L3_gnn_sph_W2", "L3_gnn_sph_b2", "L3_gnn_Wq",
          "L3_gnn_Wk", "L3_gnn_Wv"]


def kernel(**inputs):
    import numpy as _np
    import concourse.bacc as _bacc
    from concourse import mybir as _mybir
    from concourse.bass_utils import run_bass_kernel_spmd as _run

    nc = _bacc.Bacc("TRN2", target_bir_lowering=False, num_devices=1)
    arrays = {n: _np.ascontiguousarray(inputs[n]) for n in FLOATS + ["src", "dst"]}
    arrays["attr32T"] = _np.ascontiguousarray(_np.asarray(inputs["edge_attr_32"]).T)
    arrays["attr4T"] = _np.ascontiguousarray(_np.asarray(inputs["edge_attr_4"]).T)
    maps, io = {}, {}
    for n, a in arrays.items():
        maps[f"in_{n}"] = a
        io[n] = nc.dram_tensor(f"in_{n}", a.shape, _mybir.dt.from_np(a.dtype), kind="ExternalInput").ap()
    io["out"] = nc.dram_tensor("out_x", (N, D), _mybir.dt.float32, kind="ExternalOutput").ap()
    build(nc, io)
    r = _run(nc, [maps], core_ids=[0])
    return r.results[0]["out_x"]
```

```python
from contextlib import ExitStack

import numpy as np

import concourse.bass as bass
from concourse import mybir

F32 = mybir.dt.float32
BF16 = mybir.dt.bfloat16
I32 = mybir.dt.int32
ALU = mybir.AluOpType
ACT = mybir.ActivationFunctionType
AX = mybir.AxisListType

N = 6250
E = 100000
D = 128
NT = 49
NB = 49
KB = 16
EB = 2048
EP = NB * EB
NP = NT * 128
TAIL = N - (NT - 1) * 128
BIG = 1.0e30
NOWHERE = 1000000
GROUPS = [(4 * g, min(4, NT - 4 * g)) for g in range(13)]


class Plan:

    def __init__(self, nc, ctx, name):
        self.nc, self.ctx, self.name = nc, ctx, name
        self.queues = {k: [] for k in ("sync", "gpsimd", "scalar", "vector", "tensor")}
        self.sems, self.counts, self.seen = {}, {}, {}

    def sem(self, key):
        if key not in self.sems:
            self.sems[key] = self.ctx.enter_context(self.nc.semaphore(f"{self.name}_{key}"))
            self.counts[key] = 0
        return self.sems[key]

    def _waits(self, eng, after):
        out, last = [], {}
        flat = [t for a in after if a for t in (a if isinstance(a, list) else [a])]
        for key, value in flat:
            last[key] = max(value, last.get(key, 0))
        for key, value in last.items():
            if self.seen.get((eng, key), 0) < value:
                self.seen[(eng, key)] = value
                out.append((self.sem(key), value))
        return out

    def op(self, eng, fn, after=()):
        sem = self.sem(eng)
        waits = self._waits(eng, after)
        self.counts[eng] += 1

        def emit(e):
            for s, v in waits:
                e.wait_ge(s, v)
            fn(e).then_inc(sem, 1)

        self.queues[eng].append(emit)
        return (eng, self.counts[eng])

    def dma(self, eng, slot, fn, after=()):
        sem = self.sem(slot)
        waits = self._waits(eng, after)
        self.counts[slot] += 16

        def emit(e):
            for s, v in waits:
                e.wait_ge(s, v)
            fn(e).then_inc(sem, 16)

        self.queues[eng].append(emit)
        return (slot, self.counts[slot])

    def raw(self, eng, fn, after=()):
        waits = self._waits(eng, after)

        def emit(e):
            for s, v in waits:
                e.wait_ge(s, v)
            fn(e)

        self.queues[eng].append(emit)

    def finish(self):
        for key, value in self.counts.items():
            if key not in self.queues:
                self.raw("sync", lambda e: None, [(key, value)])
        with self.nc.Block() as block:
            for eng, queue in self.queues.items():
                def run(e, queue=queue):
                    for emit in queue:
                        emit(e)

                on = {"sync": block.sync, "gpsimd": block.gpsimd, "scalar": block.scalar,
                      "vector": block.vector, "tensor": block.tensor}
                on[eng](run)


def row_bcast(ap, parts):
    return bass.AP(ap.tensor, ap.offset, [[0, parts], [1, ap.shape[0]]])


class Net:
    def __init__(self, nc, ctx, io):
        self.nc, self.ctx, self.io = nc, ctx, io
        sb = self.sb
        self.x = sb("x_res", [128, NT, 128])
        self.ident = sb("ident", [128, 128])
        self.iota = sb("iota", [128, 128])
        self.jt = sb("jt", [128, NT])
        self.tb = sb("tb", [128, NT])
        self.t0 = sb("t0", [1, NB + 1], I32)
        self.dinv = sb("dinv", [128, NT])
        self.srcS = sb("srcS", [128, NB * KB], I32)
        self.dstS = sb("dstS", [128, NB, KB])
        self.eps = sb("eps", [128, 1])
        self.tabs = {p: self.dram(f"tab{p}", (NP, w)) for p, w in
                     (("0", 136), ("1", 128), ("2", 129), ("3", 129), ("4", 128))}
        self.dstp = self.dram("dstp", (EP,), I32)
        self.srcp = self.dram("srcp", (EP,), I32)
        self.attr = self.dram("attrp", (36, EP))
        self.sums = [self.dram(f"sums{r}", (NP + 128, D)) for r in range(4)]
        self.gfr = self.dram("gfr", (2, NB, 128))

    def dram(self, name, shape, dt=F32):
        return self.nc.dram_tensor(name, shape, dt, kind="Internal").ap()

    def sb(self, name, shape, dt=F32, ctx=None):
        return (ctx or self.ctx).enter_context(self.nc.sbuf_tensor(name, shape, dt))

    def ps(self, name, shape, ctx):
        return ctx.enter_context(self.nc.psum_tensor(name, shape, F32))


def setup(net):
    nc, io = net.nc, net.io
    with ExitStack() as ctx:
        p = Plan(nc, net.ctx, "su")
        one = net.sb("su_one", [128, 128], ctx=ctx)
        padi = net.sb("su_padi", [1, 352], I32, ctx=ctx)
        zeroi = net.sb("su_zeroi", [1, 352], I32, ctx=ctx)
        padf = net.sb("su_padf", [36, 352], ctx=ctx)
        raw = net.sb("su_raw", [128, NB, KB], I32, ctx=ctx)
        t0f = net.sb("su_t0", [1, NB + 1], I32, ctx=ctx)
        a = p.op("vector", lambda e: e.memset(padi[:], NOWHERE))
        b = p.op("vector", lambda e: e.memset(zeroi[:], 0))
        c = p.op("vector", lambda e: e.memset(padf[:], 0.0))
        f = [p.dma("sync", "fill", lambda e: e.dma_start(net.dstp[E:EP].rearrange("(a n) -> a n", a=1), padi[:]), [a]),
             p.dma("sync", "fill", lambda e: e.dma_start(net.srcp[E:EP].rearrange("(a n) -> a n", a=1), zeroi[:]), [b]),
             p.dma("sync", "fill", lambda e: e.dma_start(net.dstp[0:E].rearrange("(a n) -> a n", a=16), io["dst"].rearrange("(a n) -> a n", a=16))),
             p.dma("sync", "fill", lambda e: e.dma_start(net.srcp[0:E].rearrange("(a n) -> a n", a=16), io["src"].rearrange("(a n) -> a n", a=16)))]
        p.dma("scalar", "attr", lambda e: e.dma_start(net.attr[:, E:EP], padf[:]), [c])
        p.dma("scalar", "attr", lambda e: e.dma_start(net.attr[0:32, 0:E], io["attr32T"]))
        p.dma("scalar", "attr", lambda e: e.dma_start(net.attr[32:36, 0:E], io["attr4T"]))
        l1 = p.dma("sync", "l1", lambda e: e.dma_start(raw[:], net.dstp.rearrange("(b p k) -> p b k", p=128, k=KB)), [f[-1]])
        p.dma("sync", "l2", lambda e: e.dma_start(net.srcS[:].rearrange("p (b k) -> p b k", k=KB), net.srcp.rearrange("(b p k) -> p b k", p=128, k=KB)), [f[-1]])
        l3 = p.dma("sync", "l3", lambda e: e.dma_start(t0f[0:1, 0:NB].rearrange("a (n o) -> a n o", o=1), net.dstp.rearrange("(b n) -> b n", n=EB)[:, 0:1].rearrange("(a b) o -> a b o", a=1), allow_slow_non_contiguous=True), [f[-1]])
        v = p.op("vector", lambda e: e.tensor_copy(net.dstS[:], raw[:]), [l1])
        v = p.op("vector", lambda e: e.tensor_scalar(net.t0[0:1, 0:NB], t0f[0:1, 0:NB], 7, None, ALU.arith_shift_right), [l3])
        v = p.op("vector", lambda e: e.memset(net.t0[0:1, 0:1], 0), [v])
        v = p.op("vector", lambda e: e.memset(net.t0[0:1, NB:NB + 1], NT - 1), [v])
        p.op("vector", lambda e: e.memset(net.eps[:], 1e-5))
        o = p.op("vector", lambda e: e.memset(one[:], 1.0))
        g = p.op("gpsimd", lambda e: e.affine_select(out=net.ident[:], in_=one[:], compare_op=ALU.is_equal, fill=0.0, base=0, pattern=[[-1, 128]], channel_multiplier=1), [o])
        p.op("gpsimd", lambda e: e.iota(net.iota[:], pattern=[[1, 128]], base=0, channel_multiplier=0, allow_small_or_imprecise_dtypes=True))
        p.op("gpsimd", lambda e: e.iota(net.jt[:], pattern=[[128, NT]], base=0, channel_multiplier=1, allow_small_or_imprecise_dtypes=True))
        p.op("gpsimd", lambda e: e.iota(net.tb[:], pattern=[[128, NT]], base=0, channel_multiplier=0, allow_small_or_imprecise_dtypes=True))
        z = p.op("vector", lambda e: e.memset(net.x[:, NT - 1, :], 0.0))
        zs = net.sb("su_zs", [128, 50 * 128], ctx=ctx)
        y = p.op("vector", lambda e: e.memset(zs[:], 0.0))
        for r in range(4):
            p.dma("scalar", "sums", lambda e, r=r: e.dma_start(net.sums[r].rearrange("(p t) c -> p (t c)", p=128), zs[:]), [y])
        p.dma("scalar", "x", lambda e: e.dma_start(net.x[:, 0:NT - 1, :], io["x"][0:(NT - 1) * 128, :].rearrange("(t p) c -> p t c", p=128)))
        p.dma("scalar", "x2", lambda e: e.dma_start(net.x[0:TAIL, NT - 1, :], io["x"][(NT - 1) * 128:N, :]), [z])
        p.finish()


def masks(net, ctx):
    m = {k: net.sb("m_" + k, [128, NB, KB], ctx=ctx) for k in ("MF", "MB", "FM", "LM", "isl")}
    nc = net.nc
    with ExitStack() as c2:
        p = Plan(nc, net.ctx, "mk")
        sh = net.sb("mk_sh", [128, 128], ctx=c2)
        sh2 = net.sb("mk_sh2", [128, 128], ctx=c2)
        one = net.sb("mk_one", [128, 128], ctx=c2)
        prev = net.sb("mk_prev", [128, NB, KB], ctx=c2)
        nxt = net.sb("mk_next", [128, NB, KB], ctx=c2)
        keep = net.sb("mk_keep", [128, NB, KB], ctx=c2)
        keep2 = net.sb("mk_keep2", [128, NB, KB], ctx=c2)
        sen = net.sb("mk_sen", [128, 2], ctx=c2)
        rows = net.sb("mk_rows", [NB, 2, 128], ctx=c2)
        pa = net.ps("mk_pa", [128, NB], c2)
        pb = net.ps("mk_pb", [128, NB], c2)
        pc = net.ps("mk_pc", [NB, 2, 128], c2)
        o = p.op("vector", lambda e: e.memset(one[:], 1.0))
        g1 = p.op("gpsimd", lambda e: e.affine_select(out=sh[:], in_=one[:], compare_op=ALU.is_equal, fill=0.0, base=1, pattern=[[-1, 128]], channel_multiplier=1), [o])
        g2 = p.op("gpsimd", lambda e: e.affine_select(out=sh2[:], in_=one[:], compare_op=ALU.is_equal, fill=0.0, base=-1, pattern=[[-1, 128]], channel_multiplier=1), [o])
        t1 = p.op("tensor", lambda e: e.matmul(pa[:], sh[:], net.dstS[:, :, KB - 1], start=True, stop=True), [g1])
        t2 = p.op("tensor", lambda e: e.matmul(pb[:], sh2[:], net.dstS[:, :, 0], start=True, stop=True), [g2])
        s1 = p.op("vector", lambda e: e.tensor_scalar(sen[:, 0:1], net.jt[:, 0:1], 0.0, -5.0, ALU.is_equal, ALU.mult))
        s2 = p.op("vector", lambda e: e.tensor_scalar(sen[:, 1:2], net.jt[:, 0:1], 127.0, -5.0, ALU.is_equal, ALU.mult))
        v1 = p.op("vector", lambda e: e.tensor_copy(prev[:, :, 1:KB], net.dstS[:, :, 0:KB - 1]))
        v2 = p.op("vector", lambda e: e.tensor_copy(nxt[:, :, 0:KB - 1], net.dstS[:, :, 1:KB]))
        v3 = p.op("vector", lambda e: e.tensor_scalar(prev[:, :, 0], pa[:], sen[:, 0:1], None, ALU.add), [t1, s2])
        v4 = p.op("vector", lambda e: e.tensor_scalar(nxt[:, :, KB - 1], pb[:], sen[:, 1:2], None, ALU.add), [t2])
        v5 = p.op("vector", lambda e: e.tensor_tensor(m["FM"][:], net.dstS[:], prev[:], ALU.not_equal), [v4])
        v6 = p.op("vector", lambda e: e.tensor_tensor(m["isl"][:], net.dstS[:], nxt[:], ALU.not_equal), [v4])
        k1 = p.op("vector", lambda e: e.memset(keep[:], 1.0))
        k1 = p.op("vector", lambda e: e.memset(keep[:, :, 0:1], 0.0), [k1])
        k2 = p.op("vector", lambda e: e.memset(keep2[:], 1.0))
        k2 = p.op("vector", lambda e: e.memset(keep2[:, :, KB - 1:KB], 0.0), [k2])
        a = p.op("vector", lambda e: e.tensor_scalar(m["MF"][:], m["FM"][:], -BIG, None, ALU.mult), [k2])
        a = p.op("vector", lambda e: e.memset(m["MF"][:, :, 0:1], -BIG), [a])
        a = p.op("vector", lambda e: e.tensor_scalar(m["MB"][:], m["isl"][:], -BIG, None, ALU.mult), [v6])
        a = p.op("vector", lambda e: e.memset(m["MB"][:, :, KB - 1:KB], -BIG), [a])

        def flat(t):
            return t[:].rearrange("p b k -> p (b k)")

        a1 = p.op("vector", lambda e: e.tensor_tensor_scan(flat(prev), flat(keep), flat(m["FM"]), 0.0, ALU.mult, ALU.max), [a])
        a2 = p.op("vector", lambda e: e.tensor_tensor_scan(flat(nxt)[:, ::-1], flat(keep2)[:, ::-1], flat(m["isl"])[:, ::-1], 0.0, ALU.mult, ALU.max), [a])
        a3 = p.op("vector", lambda e: e.tensor_scalar(m["FM"][:], prev[:], -BIG, None, ALU.mult), [a1])
        a4 = p.op("vector", lambda e: e.tensor_scalar(m["LM"][:], nxt[:], -BIG, None, ALU.mult), [a2])
        t3 = p.op("tensor", lambda e: e.matmul(pc[:, 0, :], m["FM"][:, :, KB - 1], net.ident[:], start=True, stop=True), [a3])
        t4 = p.op("tensor", lambda e: e.matmul(pc[:, 1, :], m["LM"][:, :, 0], net.ident[:], start=True, stop=True), [a4])
        v7 = p.op("vector", lambda e: e.tensor_copy(rows[:], pc[:]), [t3, t4])
        p.dma("sync", "gfr", lambda e: e.dma_start(net.gfr.rearrange("s b n -> b s n"), rows[:]), [v7])
        p.finish()
    return m


def layernorm(net, p, src, c2, name, after):
    st = net.sb(name + "_st", [128, NT, 6], ctx=c2)
    mv = net.sb(name + "_mv", [128, NT, 2], ctx=c2)
    rs = net.sb(name + "_rs", [128, NT], ctx=c2)
    nb = net.sb(name + "_nb", [128, NT], ctx=c2)
    for t in range(NT):
        a = p.op("vector", lambda e, t=t: e.bn_stats(st[:, t, :], src[:, t, :]), after[t] if isinstance(after, list) else after)
    for t in range(NT):
        a = p.op("vector", lambda e, t=t: e.bn_aggr(mv[:, t, :], st[:, t, :]), [a] if t == 0 else ())
    s = p.op("scalar", lambda e: e.activation(rs[:], mv[:, :, 1], ACT.Sqrt, bias=net.eps[:]), [a])
    r = p.op("vector", lambda e: e.reciprocal(rs[:], rs[:]), [s])
    n = p.op("vector", lambda e: e.scalar_tensor_tensor(nb[:], mv[:, :, 0], -1.0, rs[:], ALU.mult, ALU.mult), [r])
    return rs, nb, n


def nodes(net, kind, dinv=None):
    nc, io = net.nc, net.io
    nm = f"n{kind}"
    H = {0: 8, 1: 0, 2: 1, 3: 1, 4: 0}[kind]
    W = {0: 136, 1: 128, 2: 129, 3: 129, 4: 128}[kind]
    tab = net.tabs[str(kind)]
    with ExitStack() as c2:
        p = Plan(nc, net.ctx, nm)

        def load(name, shape, ap):
            t = net.sb(nm + name, shape, ctx=c2)
            return t, p.dma("sync", "w_" + name, lambda e: e.dma_start(t[:], ap))

        def col(ap):
            return ap.rearrange("(p o) -> p o", o=1)

        ready = []
        if kind == 0:
            Wm, k = load("W", [128, 128], io["L0_gnn_W_in"]); ready.append(k)
            Wa = net.sb(nm + "Wa", [128, 16], ctx=c2)
            ready.append(p.dma("sync", "w_a", lambda e: e.dma_start(Wa[:, 0:8], io["L0_gnn_W_u"])))
            ready.append(p.dma("sync", "w_a", lambda e: e.dma_start(Wa[:, 8:16], io["L0_gnn_W_v"])))
            gam, k = load("gam", [128, 1], col(io["L0_gnn_ln_gamma"])); ready.append(k)
            bet, k = load("bet", [128, 1], col(io["L0_gnn_ln_beta"])); ready.append(k)
            bcol, k = load("bcol", [128, 1], col(io["L0_gnn_b_in"])); ready.append(k)
            brow, k = load("brow", [128, 128], row_bcast(io["L0_gnn_b_in"], 128)); ready.append(k)
            burow, k = load("burow", [128, 8], row_bcast(io["L0_gnn_b_u"], 128)); ready.append(k)
        elif kind == 1:
            Wm, k = load("W", [128, 128], io["L1_gnn_W"]); ready.append(k)
        elif kind in (2, 3):
            s = str(kind - 1)
            Wm, k = load("W", [128, 128], io["L2_gnn_W" + s]); ready.append(k)
            Wa = net.sb(nm + "Wa", [128, 2], ctx=c2)
            ready.append(p.dma("sync", "w_a", lambda e: e.dma_start(Wa[:, 0:1], col(io["L2_gnn_as" + s]))))
            ready.append(p.dma("sync", "w_a", lambda e: e.dma_start(Wa[:, 1:2], col(io["L2_gnn_ad" + s]))))
        else:
            Wm = net.sb(nm + "W", [128, 384], ctx=c2)
            z = p.op("vector", lambda e: e.memset(Wm[:], 0.0))
            for j, w in enumerate(("Wq", "Wk", "Wv")):
                for h in range(4):
                    ready.append(p.dma("sync", "w_q", lambda e, j=j, w=w, h=h: e.dma_start(
                        Wm[32 * h:32 * h + 32, 128 * j + 32 * h:128 * j + 32 * h + 32], io["L3_gnn_" + w][h]), [z]))
        hn = net.sb(nm + "hn", [128, NT, 128], ctx=c2)
        if kind == 3:
            hsrc, hready = net.aux[:].rearrange("p (t c) -> p t c", c=128), [None] * NT
        else:
            rs, nb, n0 = layernorm(net, p, net.x, c2, nm + "l", ())
            hready = [p.op("scalar", lambda e, t=t: e.activation(hn[:, t, :], net.x[:, t, :], ACT.Relu, bias=nb[:, t:t + 1], scale=rs[:, t:t + 1]), [n0]) for t in range(NT)]
            if kind == 0:
                rs2, nb2, n2 = layernorm(net, p, hn, c2, nm + "m", [[x] for x in hready])
                hready = [p.op("scalar", lambda e, t=t: e.activation(hn[:, t, :], hn[:, t, :], ACT.Identity, bias=nb2[:, t:t + 1], scale=rs2[:, t:t + 1]), [n2]) for t in range(NT)]
            hsrc = hn
        hT = net.sb(nm + "hT", [128, 2, 512], ctx=c2)
        gT = net.sb(nm + "gT", [128, 2, 512], ctx=c2)
        TB = net.sb(nm + "TB", [128, 2, 4, W], ctx=c2)
        P1 = [net.ps(f"{nm}P1{i}", [128, 4, 128], c2) for i in range(2)]
        P2 = net.ps(nm + "P2", [128, 512], c2) if H else None
        P3 = [net.ps(f"{nm}P3{i}", [128, 512], c2) for i in range(3)]
        P4 = net.ps(nm + "P4", [128, 4, 16], c2) if H else None
        w = 2 * H
        accv = None if kind == 4 else net.acc[:, 0:NT * {0: 146, 1: 128, 2: 130, 3: 130}[kind]].rearrange("p (t c) -> p t c", t=NT)
        stored = [None, None]
        free1, free3 = [None, None], [None, None, None]
        free2 = free4 = None
        hTfree, gTfree = [None, None], [None, None]
        n3 = 0
        sv = net.sv if H else None
        def group(g, t0, nt):
            nonlocal free2, free4, n3
            s = g % 2
            for j in range(nt):
                a = p.op("tensor", lambda e, j=j: e.transpose(P1[s][:, j, :], hsrc[:, t0 + j, :], net.ident[:]), [hready[t0 + j], free1[s]])
            L = nt * 128
            if kind == 0:
                ev = p.op("vector", lambda e: e.tensor_scalar(hT[:, s, 0:L], P1[s][:, 0:nt, :].rearrange("p a b -> p (a b)"), gam[:], bet[:], ALU.mult, ALU.add), [a, hTfree[s]] + ready)
            else:
                ev = p.op("vector", lambda e: e.tensor_copy(hT[:, s, 0:L], P1[s][:, 0:nt, :].rearrange("p a b -> p (a b)")), [a, hTfree[s]])
            free1[s] = ev
            if H:
                a = p.op("tensor", lambda e: e.matmul(P2[:, 0:L], Wm[:], hT[:, s, 0:L], start=True, stop=True), [ev, free2] + ready)
                if kind == 0:
                    e2 = p.op("scalar", lambda e: e.activation(gT[:, s, 0:L], P2[:, 0:L], ACT.Identity, bias=bcol[:]), [a, gTfree[s]] + ready)
                else:
                    e2 = p.op("scalar", lambda e: e.copy(gT[:, s, 0:L], P2[:, 0:L]), [a, gTfree[s]])
                free2 = e2
            fin = []
            if kind == 4:
                for j in range(nt):
                    b = n3 % 3
                    n3 += 1
                    a = p.op("tensor", lambda e, b=b, j=j: e.matmul(P3[b][:, 0:384], hT[:, s, 128 * j:128 * j + 128], Wm[:], start=True, stop=True), [ev, *(free3[b] or []), *ready])
                    eng = "scalar" if j % 2 else "vector"

                    def out(to, b, lo, hi, eng=eng):
                        return lambda e: (e.copy if eng == "scalar" else e.tensor_copy)(to, P3[b][:, lo:hi])

                    c = p.op(eng, out(TB[:, s, j, :], b, 0, 128), [a, stored[s]])
                    d = p.op(eng, out(net.kv[:, (t0 + j) * 256:(t0 + j + 1) * 256], b, 128, 384))
                    free3[b] = [c, d]
                    fin += [c, d]
                hTfree[s] = a
            else:
                b = n3 % 3
                n3 += 1
                for j in range(nt):
                    a = p.op("tensor", lambda e, j=j, b=b: e.matmul(P3[b][:, 128 * j:128 * j + 128], hT[:, s, 128 * j:128 * j + 128], Wm[:], start=True, stop=True), [ev, free3[b]] + ready)
                hTfree[s] = a
                src = P3[b][:, 0:L].rearrange("p (a c) -> p a c", c=128)
                if kind == 0:
                    c = p.op("vector", lambda e, src=src: e.tensor_tensor(TB[:, s, 0:nt, 0:128], src, brow[:].rearrange("p (a c) -> p a c", a=1).broadcast_to([128, nt, 128]), ALU.add), [a, stored[s]])
                elif kind == 1:
                    for j in range(nt):
                        c = p.op("vector", lambda e, b=b, j=j: e.tensor_scalar(TB[:, s, j, 0:128], P3[b][:, 128 * j:128 * j + 128], net.dinv[:, t0 + j:t0 + j + 1], None, ALU.mult), [a, stored[s]])
                    fin.append(p.op("scalar", lambda e: e.copy(accv[:, t0:t0 + nt, 0:128], TB[:, s, 0:nt, 0:128]), [c]))
                else:
                    c = p.op("vector", lambda e, src=src: e.tensor_copy(TB[:, s, 0:nt, 0:128], src), [a, stored[s]])
                    fin.append(p.op("scalar", lambda e: e.copy(accv[:, t0:t0 + nt, 0:128], TB[:, s, 0:nt, 0:128]), [c]))
                free3[b] = c
                fin.append(c)
                if H:
                    for j in range(nt):
                        a = p.op("tensor", lambda e, j=j: e.matmul(P4[:, j, 0:w], gT[:, s, 128 * j:128 * j + 128], Wa[:], start=True, stop=True), [e2, free4])
                    gTfree[s] = a
                    if kind == 0:
                        c = p.op("vector", lambda e: e.tensor_tensor(TB[:, s, 0:nt, 128:136], P4[:, 0:nt, 0:8], burow[:].rearrange("p (a c) -> p a c", a=1).broadcast_to([128, nt, 8]), ALU.add), [a])
                    else:
                        c = p.op("vector", lambda e: e.tensor_copy(TB[:, s, 0:nt, 128:129], P4[:, 0:nt, 0:1]), [a])
                    d = p.op("vector", lambda e: e.tensor_copy(sv[:, t0:t0 + nt, 0:H], P4[:, 0:nt, H:2 * H]), [a])
                    free4 = d
                    fin += [c, d]
                    if kind != 0:
                        d = p.op("vector", lambda e: e.tensor_tensor(accv[:, t0:t0 + nt, 129:130], TB[:, s, 0:nt, 128:129], sv[:, t0:t0 + nt, 0:1], ALU.add), [d])
                        d = p.op("vector", lambda e: e.scalar_tensor_tensor(accv[:, t0:t0 + nt, 129], accv[:, t0:t0 + nt, 129], 0.2, accv[:, t0:t0 + nt, 129], ALU.mult, ALU.max), [d])
                        fin.append(d)
            st = p.dma("sync", f"tab{s}", lambda e: e.dma_start(tab[t0 * 128:(t0 + nt) * 128, :].rearrange("(t q) c -> q t c", q=128), TB[:, s, 0:nt, :]), fin)
            stored[s] = st

        for g, (t0, nt) in enumerate(GROUPS):
            group(g, t0, nt)
        if kind == 0:
            p.op("vector", lambda e: e.memset(net.acc[:], 0.0))
            z = p.counts["vector"]
            p.op("vector", lambda e: e.memset(accv[:, :, 136:144], -BIG), [("vector", z)])
        if kind in (2, 3):
            p.op("vector", lambda e: e.memset(accv[:, :, 128:129], 1.0))
        p.finish()


def edges(net, kind, m=None):
    nc = net.nc
    nm = f"e{kind}"
    H = {0: 8, 1: 0, 2: 1, 3: 1}[kind]
    WT = {0: 136, 1: 128, 2: 129, 3: 129}[kind]
    W = {0: 146, 1: 128, 2: 130, 3: 130}[kind]
    R = {0: 3, 1: 4, 2: 4, 3: 4}[kind]
    tab = net.tabs[str(kind)]
    with ExitStack() as c2:
        p = Plan(nc, net.ctx, nm)
        G = [net.sb(f"{nm}G{i}", [128, KB, max(WT, W) if H < 8 else WT], ctx=c2) for i in range(R)]
        S = [net.sb(f"{nm}S{i}", [128, KB, 128], ctx=c2) for i in range(2)]
        dl = net.sb(nm + "dl", [128, KB], ctx=c2)
        PA = net.ps(nm + "PA", [128, W], c2)
        PS = net.sb(nm + "PS", [128, W], ctx=c2)
        dum = net.sb(nm + "dum", [128, 1], ctx=c2)
        sa, sp, sc = p.sem("aggv"), p.sem("aggp"), p.sem("aggs")
        for k in ("aggv", "aggp", "aggs"):
            del p.counts[k]
        P1N = {0: 0, 1: 9, 8: 6}[H]
        P2N = {0: 1, 1: 2, 8: 4}[H]
        KA = P1N + 1 + KB + P2N
        CA = 2 if H else 1
        z0 = p.op("vector", lambda e: e.memset(PA[:], 0.0))
        if H:
            ST = [net.sb(f"{nm}ST{i}", [128, EB], BF16, ctx=c2) for i in range(2)]
            svb = net.sb(nm + "svb", [128, 3, NT * 8], BF16, ctx=c2)
            svr = net.sb(nm + "svr", [128, NT * 8], ctx=c2)
            DR = [net.sb(f"{nm}DR{i}", [128, EB], I32, ctx=c2) for i in range(2)]
            GR = [net.sb(f"{nm}GR{i}", [H, 2, 128], ctx=c2) for i in range(2)]
            EH, FF, BB, T1, T2 = [net.sb(nm + x, [128, H, KB], ctx=c2) for x in ("EH", "FF", "BB", "T1", "T2")]
            RF = net.sb(nm + "RF", [H, 129], ctx=c2)
            RB = net.sb(nm + "RB", [H, 129], ctx=c2)
            sm = net.sb(nm + "sm", [128, 16 + 4 * H], ctx=c2)
            ac = net.sb(nm + "ac", [128, 2 * H], ctx=c2)
            PX = net.ps(nm + "PX", [128, KB, H], c2)
            PT = [net.ps(f"{nm}PT{i}", [H, 128], c2) for i in range(2)]
            PC = net.ps(nm + "PC", [128, 2, H], c2)
            xv, xp = p.sem("expv"), p.sem("expp")
            del p.counts["expv"], p.counts["expp"]
            z1 = p.op("vector", lambda e: e.tensor_copy(svb[:, 0, :], net.svf))
            z1 = p.op("vector", lambda e: e.tensor_tensor(svr[:], net.svf, svb[:, 0, :], ALU.subtract), [z1])
            z1 = p.op("vector", lambda e: e.tensor_copy(svb[:, 1, :], svr[:]), [z1])
            z1 = p.op("vector", lambda e: e.tensor_tensor(svr[:], svr[:], svb[:, 1, :], ALU.subtract), [z1])
            z1 = p.op("vector", lambda e: e.tensor_copy(svb[:, 2, :], svr[:]), [z1])
            z2 = p.op("vector", lambda e: e.memset(RF[:, 0:1], -BIG))
            z2 = p.op("vector", lambda e: e.memset(RB[:, 128:129], -BIG))
            p.raw("tensor", lambda e: e.sem_inc(xp, 1))
        if H == 8:
            MSG = [net.sb(f"{nm}M{i}", [128, KB, W], ctx=c2) for i in range(2)]
            MFH, MBH = [net.sb(nm + x, [128, H, KB], ctx=c2) for x in ("MFH", "MBH")]
            tmp = net.sb(nm + "tmp", [128, 136], ctx=c2)
            for i in range(2):
                z2 = p.op("vector", lambda e, i=i: e.memset(MSG[i][:, :, W - 1:W], 1.0))
        if H == 1:
            EX = [net.sb(f"{nm}EX{i}", [128, KB], ctx=c2) for i in range(2)]
        p.raw("tensor", lambda e: e.sem_inc(sp, KB))
        p.raw("vector", lambda e: e.sem_inc(sa, 1))
        hi = {k: {} for k in ("vector", "tensor", "scalar")}
        gfree, drfree, grfree = [None] * R, [None, None], [None, None]
        gtok, drtok, grtok, ready, rhs, scale = {}, {}, {}, {}, {}, {}
        last = {"scan": None, "EH": None}

        def gather(b):
            s = b % R
            for k in range(KB):
                gtok[b] = p.dma("gpsimd", f"g{s}", lambda e, k=k: e.indirect_dma_start(
                    G[s][:, k, 0:WT], None, tab, bass.IndirectOffsetOnAxis(net.srcS[:, b * KB + k:b * KB + k + 1], 0)), [gfree[s]])

        def load_dst(b):
            s = b % 2
            drtok[b] = p.dma("sync", f"dr{s}", lambda e: e.dma_start(DR[s][:], row_bcast(net.dstp[b * EB:(b + 1) * EB], 128)), [drfree[s]])

        def load_runs(b):
            s = b % 2
            grtok[b] = p.dma("sync", f"gr{s}", lambda e: e.dma_start(GR[s][:], bass.AP(net.gfr.tensor, net.gfr.offset + b * 128, [[0, H], [NB * 128, 2], [1, 128]])), [grfree[s]])

        def load_tile(b):
            for q in ("vector", "tensor", "scalar"):
                def emit(e, q=q):
                    hi[q][b] = e.value_load(net.t0[0:1, b:b + 1], min_val=0, max_val=NT - 1)
                p.raw(q, emit)

        def released(b):
            gfree[b % R] = p.op("vector", lambda e: e.memset(dum[:], 0.0))
            if b + R < NB:
                gather(b + R)

        def expand(b):
            dr = DR[b % 2]

            def one_v(e, st, t):
                e.tensor_scalar(st[:], dr[:], net.jt[:, bass.ds(t, 1)], None, ALU.is_equal).then_inc(xv, 1)

            def expand_v(e):
                lo, up = hi["vector"][b], hi["vector"][b + 1]
                if b:
                    e.wait_ge(xp, hi["vector"][b - 1] + (b + 1))
                one_v(e, ST[0], lo)
                with e.If(lo < up):
                    with e.Fori(lo + 1, up + 1) as t:
                        e.wait_ge(xp, t + b + (t > lo + 1))
                        one_v(e, ST[1], t)

            def one_p(e, st, t, first):
                e.wait_ge(xv, t + (b + 1))
                for k in range(KB):
                    for j in range(3):
                        i = e.matmul(PX[:, k, :], st[:, k:EB:KB], svb[:, j, bass.ds(t * 8, H)], start=first and k + j == 0, stop=False, skip_group_check=True)
                i.then_inc(xp, 1)

            def expand_p(e):
                lo, up = hi["tensor"][b], hi["tensor"][b + 1]
                one_p(e, ST[0], lo, True)
                with e.If(lo < up):
                    with e.Fori(lo + 1, up + 1) as t:
                        one_p(e, ST[1], t, False)

            p.raw("vector", expand_v, [drtok[b], z1])
            p.raw("tensor", expand_p, [z1, last["EH"]])

        def fl(t):
            return t[:].rearrange("p h k -> p (h k)")

        def copy_masks(b):
            if H > 1:
                p.op("scalar", lambda e: e.copy(MFH[:], m["MF"][:, b:b + 1, :].broadcast_to([128, H, KB])), [last["scan"]])
                last["mask"] = p.op("scalar", lambda e: e.copy(MBH[:], m["MB"][:, b:b + 1, :].broadcast_to([128, H, KB])))

        def scan(b):
            g = G[b % R]
            mf, mb = (fl(MFH), fl(MBH)) if H > 1 else (m["MF"][:, b, :], m["MB"][:, b, :])
            mk = last.get("mask")
            p.raw("vector", lambda e: e.wait_ge(xp, hi["vector"][b + 1] + (b + 2)))
            v = p.op("vector", lambda e: e.tensor_tensor(EH[:], g[:, :, 128:128 + H].rearrange("p k h -> p h k"), PX[:].rearrange("p k h -> p h k"), ALU.add), [gtok[b]])
            last["EH"] = drfree[b % 2] = v
            if b + 2 < NB:
                load_dst(b + 2)
            v = p.op("vector", lambda e: e.scalar_tensor_tensor(EH[:], EH[:], 0.2, EH[:], ALU.mult, ALU.max), [v])
            f1 = p.op("vector", lambda e: e.tensor_tensor_scan(fl(FF), mf, fl(EH), -BIG, ALU.add, ALU.max), [v, mk])
            f2 = p.op("vector", lambda e: e.tensor_tensor_scan(fl(BB)[:, ::-1], mb[:, ::-1], fl(EH)[:, ::-1], -BIG, ALU.add, ALU.max), [v, mk])
            last["scan"] = f2
            last["turned"] = turned = []
            t1 = p.op("tensor", lambda e: e.matmul(PT[0][:], FF[:, :, KB - 1], net.ident[:], start=True, stop=True), [f1])
            t2 = p.op("tensor", lambda e: e.matmul(PT[1][:], BB[:, :, 0], net.ident[:], start=True, stop=True), [f2])
            turned += [t1, t2]

        def scan_across(b):
            gr = GR[b % 2]
            t1, t2 = last["turned"]
            r1 = p.op("vector", lambda e: e.tensor_tensor_scan(RF[:, 1:129], gr[:, 0, :], PT[0][:], -BIG, ALU.add, ALU.max), [t1, z2, grtok[b]])
            r2 = p.op("vector", lambda e: e.tensor_tensor_scan(RB[:, 0:128][:, ::-1], gr[:, 1, :][:, ::-1], PT[1][:, ::-1], -BIG, ALU.add, ALU.max), [t2])
            grfree[b % 2] = r2
            if b + 2 < NB:
                load_runs(b + 2)
            p.op("tensor", lambda e: e.matmul(PC[:, 0, :], RF[:, 0:128], net.ident[0:H, 0:H], start=True, stop=True), [r1])
            last["across"] = p.op("tensor", lambda e: e.matmul(PC[:, 1, :], RB[:, 1:129], net.ident[0:H, 0:H], start=True, stop=True), [r2])

        def weigh(b):
            g, c_ = G[b % R], last["across"]
            if H == 1:
                v = p.op("vector", lambda e: e.scalar_tensor_tensor(T1[:, 0, :], m["FM"][:, b, :], PC[:, 0, :], FF[:, 0, :], ALU.add, ALU.max), [c_])
                v = p.op("vector", lambda e: e.scalar_tensor_tensor(T2[:, 0, :], m["LM"][:, b, :], PC[:, 1, :], BB[:, 0, :], ALU.add, ALU.max), [c_])
            else:
                v = p.op("vector", lambda e: e.tensor_tensor(T1[:], m["FM"][:, b:b + 1, :].broadcast_to([128, H, KB]), PC[:, 0, :].rearrange("p (h o) -> p h o", o=1).broadcast_to([128, H, KB]), ALU.add), [c_])
                w = p.op("vector", lambda e: e.tensor_tensor(T2[:], m["LM"][:, b:b + 1, :].broadcast_to([128, H, KB]), PC[:, 1, :].rearrange("p (h o) -> p h o", o=1).broadcast_to([128, H, KB]), ALU.add), [c_])
                v = p.op("vector", lambda e: e.tensor_tensor(T1[:], T1[:], FF[:], ALU.max), [v])
                v = p.op("vector", lambda e: e.tensor_tensor(T2[:], T2[:], BB[:], ALU.max), [w])
            v = p.op("vector", lambda e: e.tensor_tensor(T1[:], T1[:], T2[:], ALU.max), [v])
            v = p.op("vector", lambda e: e.tensor_tensor(T2[:], EH[:], T1[:], ALU.subtract), [v])
            if H == 1:
                x = EX[b % 2]
                ex = p.op("scalar", lambda e: e.activation(x[:], T2[:, 0, :], ACT.Exp), [v])
                p.op("vector", lambda e: e.memset(g[:, :, 128:129], 1.0))
                v = p.op("vector", lambda e: e.tensor_copy(g[:, :, 129], T1[:, 0, :]))
                ready[b], rhs[b], scale[b] = [v, ex], [g[:, k, 0:W] for k in range(KB)], x
            else:
                M = MSG[b % 2]
                ex = p.op("scalar", lambda e: e.activation(M[:, :, 128:128 + H], T2[:].rearrange("p h k -> p k h"), ACT.Exp), [v])
                il = p.op("scalar", lambda e: e.copy(M[:, :, 128 + 2 * H], m["isl"][:, b, :]))
                p.op("vector", lambda e: e.tensor_tensor(M[:, :, 128 + H:128 + 2 * H], T1[:].rearrange("p h k -> p k h"), m["isl"][:, b, :].rearrange("p (k o) -> p k o", o=1).broadcast_to([128, KB, H]), ALU.mult))
                v = p.op("vector", lambda e: e.tensor_tensor(
                    M[:, :, 0:128].rearrange("p k (d h) -> p k d h", h=H), g[:, :, 0:128].rearrange("p k (d h) -> p k d h", h=H),
                    M[:, :, 128:128 + H].rearrange("p k (o h) -> p k o h", o=1).broadcast_to([128, KB, 128 // H, H]), ALU.mult), [ex, il])
                gfree[b % R] = v
                if b + R < NB:
                    gather(b + R)
                ready[b], rhs[b], scale[b] = [v], [M[:, k, :] for k in range(KB)], None

        def merge_1(e, i, n, at):
            e.wait_ge(sc, i * CA + 1)

            def done(ins, wait=True):
                n[0] += 1
                ins.then_inc(sa, 1)
                if wait:
                    e.wait_ge(sa, i * KA + (n[0] + 1))

            if not H:
                return
            Am = net.acc[:, bass.ds(at * W + 128 + H, H)]
            Mb, mx, d1, d2 = [sm[:, 16 + H * q:16 + H * q + H] for q in range(4)]
            d12 = sm[:, 16 + 2 * H:16 + 4 * H]
            if H == 8:
                done(e.tensor_scalar(sm[:, 0:1], PS[:, 144:145], -1.0, BIG, ALU.add, ALU.mult))
                done(e.tensor_scalar(Mb, PS[:, 136:144], sm[:, 0:1], None, ALU.add))
            else:
                done(e.tensor_scalar(sm[:, 0:1], PS[:, 128:129], 0.0, None, ALU.is_equal))
                done(e.tensor_tensor(sm[:, 1:2], PS[:, 128:129], sm[:, 0:1], ALU.add))
                done(e.reciprocal(sm[:, 2:3], sm[:, 1:2]))
                done(e.tensor_tensor(sm[:, 3:4], PS[:, 129:130], sm[:, 2:3], ALU.mult))
                done(e.scalar_tensor_tensor(Mb, sm[:, 0:1], -BIG, sm[:, 3:4], ALU.mult, ALU.add))
            done(e.tensor_tensor(mx, Am, Mb, ALU.max))
            done(e.tensor_tensor(d1, Am, mx, ALU.subtract), False)
            done(e.tensor_tensor(d2, Mb, mx, ALU.subtract))
            done(e.tensor_scalar(Am, mx, 1.0, None, ALU.mult), False)
            assert n[0] == P1N

        def merge_2(e, i, n, at):
            def done(ins, wait=True):
                n[0] += 1
                ins.then_inc(sa, 1)
                if wait:
                    e.wait_ge(sa, i * KA + (n[0] + 1))

            if not H:
                A = net.acc[:, bass.ds(at * W, W)]
                done(e.tensor_tensor(A, A, PS[:], ALU.add), False)
                return
            e.wait_ge(sc, i * CA + 2)
            An = net.acc[:, bass.ds(at * W, 128 + H)]
            if H > 1:
                An3 = An.rearrange("p (d h) -> p d h", h=H)
                nh = 128 // H + 1
                done(e.tensor_tensor(An3, An3, ac[:, 0:H].rearrange("p (o h) -> p o h", o=1).broadcast_to([128, nh, H]), ALU.mult), False)
                done(e.tensor_tensor(tmp[:].rearrange("p (d h) -> p d h", h=H), PS[:, 0:128 + H].rearrange("p (d h) -> p d h", h=H), ac[:, H:2 * H].rearrange("p (o h) -> p o h", o=1).broadcast_to([128, nh, H]), ALU.mult))
                done(e.tensor_tensor(An, An, tmp[:], ALU.add), False)
                Ac = net.acc[:, bass.ds(at * W + W - 1, 1)]
                done(e.tensor_tensor(Ac, Ac, PS[:, W - 1:W], ALU.add), False)
            else:
                done(e.tensor_scalar(An, An, ac[:, 0:1], None, ALU.mult))
                done(e.scalar_tensor_tensor(An, PS[:, 0:129], ac[:, 1:2], An, ALU.mult, ALU.add), False)

        def merge_exp(e, i):
            e.wait_ge(sa, i * KA + P1N)
            e.activation(ac[:], sm[:, 16 + 2 * H:16 + 4 * H], ACT.Exp).then_inc(sc, 1)

        def copy_sums(e, i):
            e.wait_ge(sp, i * KB + KB)
            e.wait_ge(sa, i * KA + 1)
            e.copy(PS[:], PA[:]).then_inc(sc, 1)
            if H:
                merge_exp(e, i)

        def step_v(e, b, t, s, at, free):
            i, n = t + b, [0]
            merge_1(e, i, n, at)
            e.tensor_scalar(dl[:], net.dstS[:, b, :], net.tb[:, bass.ds(t, 1)], None, ALU.subtract).then_inc(sa, 1)
            e.wait_ge(sa, i * KA + (P1N + 2))
            if free is not None:
                e.wait_ge(sp, free)
            for k in range(KB):
                if scale[b] is None:
                    x = e.tensor_scalar(s[:, k, :], net.iota[:], dl[:, k:k + 1], None, ALU.is_equal)
                else:
                    x = e.tensor_scalar(s[:, k, :], net.iota[:], dl[:, k:k + 1], scale[b][:, k:k + 1], ALU.is_equal, ALU.mult)
                x.then_inc(sa, 1)
            n[0] += 1 + KB
            merge_2(e, i, n, at)
            assert n[0] == KA, n

        def step_p(e, b, t, s):
            i = t + b
            e.wait_ge(sc, i * CA + 1)
            for k in range(KB):
                if k % 4 == 0:
                    e.wait_ge(sa, i * KA + (P1N + 2 + k + 4))
                e.matmul(PA[:], s[:, k, :], rhs[b][k], start=(k == 0), stop=(k == KB - 1)).then_inc(sp, 1)

        def first_step(b):
            def free(e):
                return (hi["vector"][b - 1] + (b - 1)) * KB + 2 * KB if b else None

            p.raw("vector", lambda e: step_v(e, b, hi["vector"][b], S[0], hi["vector"][b], free(e)), ready[b])
            p.raw("tensor", lambda e: step_p(e, b, hi["tensor"][b], S[0]), ready[b])
            p.raw("scalar", lambda e: copy_sums(e, hi["scalar"][b] + b))

        def other_steps(b):
            def on(q, body):
                def emit(e):
                    lo, up = hi[q][b], hi[q][b + 1]
                    with e.If(lo < up):
                        with e.Fori(lo + 1, up + 1) as t:
                            body(e, lo, t)
                p.raw(q, emit)

            on("vector", lambda e, lo, t: step_v(e, b, t, S[1], t - 1, (t + b) * KB + (t > lo + 1) * KB))
            on("tensor", lambda e, lo, t: step_p(e, b, t, S[1]))
            on("scalar", lambda e, lo, t: copy_sums(e, t + b))

        for b in range(min(R, NB)):
            gather(b)
        for b in range(3):
            load_tile(b)
        p.raw("scalar", lambda e: None, [z0])
        if H:
            for b in range(2):
                load_dst(b)
                load_runs(b)
            copy_masks(0)
            expand(0)
            scan(0)
            expand(1)
            scan_across(0)
            weigh(0)
        for b in range(NB):
            if b + 3 <= NB:
                load_tile(b + 3)
            more = H and b + 1 < NB
            if more:
                copy_masks(b + 1)
            if not H:
                ready[b], rhs[b], scale[b] = [gtok[b]], [G[b % R][:, k, 0:W] for k in range(KB)], None
            first_step(b)
            if b and H < 8:
                released(b - 1)
            if more:
                scan(b + 1)
            if H and b + 2 < NB:
                expand(b + 2)
            if more:
                scan_across(b + 1)
            other_steps(b)
            if more:
                weigh(b + 1)
        steps, n, n2 = NB + NT - 1, [0], [P1N]
        p.raw("scalar", lambda e: copy_sums(e, steps))
        p.raw("vector", lambda e: merge_1(e, steps, n, NT - 1))
        p.raw("vector", lambda e: merge_2(e, steps, n2, NT - 1))
        p.finish()


def final_attention(net, kind):
    nc, io = net.nc, net.io
    nm = f"f{kind}"
    H = 8 if kind == 0 else 1
    W = 146 if kind == 0 else 130
    A = net.acc[:, 0:NT * W].rearrange("p (t c) -> p t c", t=NT)
    with ExitStack() as c2:
        p = Plan(nc, net.ctx, nm)
        rd = net.sb(nm + "rd", [128, NT, H], ctx=c2)
        r2 = net.sb(nm + "r2", [128, NT, H], ctx=c2)
        bias = net.sb(nm + "b", [128, 128], ctx=c2)
        bname = {0: "L0_gnn_b_ff", 2: "L2_gnn_b1", 3: "L2_gnn_b2"}[kind]
        lb = p.dma("sync", "b", lambda e: e.dma_start(bias[:], row_bcast(io[bname], 128)))
        v = p.op("vector", lambda e: e.tensor_scalar(r2[:], A[:, :, 128:128 + H], 0.0, None, ALU.is_equal))
        v = p.op("vector", lambda e: e.tensor_tensor(rd[:], r2[:], A[:, :, 128:128 + H], ALU.add), [v])
        v = p.op("vector", lambda e: e.reciprocal(rd[:], rd[:]), [v])
        if kind != 0:
            o = net.sb(nm + "o", [128, NT, 128], ctx=c2)
            for t in range(NT):
                p.op("vector", lambda e, t=t: e.scalar_tensor_tensor(o[:, t, :], A[:, t, 0:128], rd[:, t, :], bias[:], ALU.mult, ALU.add), [v, lb])
            last = ("vector", p.counts["vector"])
            if kind == 2:
                p.op("scalar", lambda e: e.activation(net.aux[:], o[:].rearrange("p t c -> p (t c)"), ACT.Relu), [last])
            else:
                p.op("vector", lambda e: e.tensor_tensor(net.x[:], net.x[:], o[:], ALU.add), [last])
            p.finish()
            return
        Wf = net.sb(nm + "Wf", [128, 128], ctx=c2)
        lw = p.dma("sync", "w", lambda e: e.dma_start(Wf[:], io["L0_gnn_W_ff"]))
        o = net.sb(nm + "o", [128, 3, 128], ctx=c2)
        oT = net.sb(nm + "oT", [128, 3, 128], ctx=c2)
        P1 = [net.ps(f"{nm}p{i}", [128, 128], c2) for i in range(3)]
        P2 = [net.ps(f"{nm}q{i}", [128, 128], c2) for i in range(3)]
        dg = net.sb(nm + "dg", [128, NT], ctx=c2)
        c = p.op("vector", lambda e: e.tensor_scalar(dg[:], A[:, :, W - 1], 1.0, None, ALU.add))
        c = p.op("scalar", lambda e: e.activation(dg[:], dg[:], ACT.Sqrt), [c])
        p.op("vector", lambda e: e.reciprocal(net.dinv[:], dg[:]), [c])
        xb = None
        for t in range(NT):
            xb = p.op("gpsimd", lambda e, t=t: e.tensor_tensor(net.x[:, t, :], net.x[:, t, :], bias[:], ALU.add), [lb])
        free = [[None] * 3 for _ in range(3)]
        free3 = [None] * 3
        for t in range(NT):
            s = t % 3
            a = p.op("vector", lambda e, t=t, s=s: e.tensor_tensor(o[:, s, :].rearrange("p (d h) -> p d h", h=8), A[:, t, 0:128].rearrange("p (d h) -> p d h", h=8), rd[:, t:t + 1, :].broadcast_to([128, 16, 8]), ALU.mult), [v, free[0][s]])
            b = p.op("tensor", lambda e, s=s: e.transpose(P1[s][:], o[:, s, :], net.ident[:]), [a, free[1][s]])
            free[0][s] = b
            c = p.op("scalar", lambda e, s=s: e.copy(oT[:, s, :], P1[s][:]), [b, free[2][s]])
            free[1][s] = c
            d = p.op("tensor", lambda e, s=s: e.matmul(P2[s][:], oT[:, s, :], Wf[:], start=True, stop=True), [c, lw, free3[s]])
            free[2][s] = d
            f = p.op("vector", lambda e, t=t, s=s: e.tensor_tensor(net.x[:, t, :], net.x[:, t, :], P2[s][:], ALU.add), [d, xb])
            free3[s] = f
        p.finish()


def final_conv(net):
    nc, io = net.nc, net.io
    A = net.acc[:, 0:NT * 128].rearrange("p (t c) -> p t c", t=NT)
    with ExitStack() as c2:
        p = Plan(nc, net.ctx, "f1")
        rows = net.sb("f1r", [128, 3, 128], ctx=c2)
        lb = [p.dma("sync", "b", lambda e, j=j, n=n: e.dma_start(rows[:, j, :], row_bcast(io[n], 128)))
              for j, n in enumerate(("L1_gnn_b", "L1_gnn_gamma", "L1_gnn_beta"))][-1]
        ones = net.sb("f1o", [128, 2, 128], ctx=c2)
        cm = net.sb("f1c", [128, 1], ctx=c2)
        mean = net.sb("f1m", [128, 128], ctx=c2)
        sq = net.sb("f1s", [128, NT, 128], ctx=c2)
        PM = net.ps("f1pm", [128, 128], c2)
        PV = net.ps("f1pv", [128, 128], c2)
        o = p.op("vector", lambda e: e.memset(ones[:, 0, :], 1.0))
        o = p.op("vector", lambda e: e.tensor_scalar(cm[:], net.jt[:, 0:1], float(TAIL), None, ALU.is_lt), [o])
        o = p.op("vector", lambda e: e.tensor_scalar(ones[:, 1, :], ones[:, 0, :], cm[:], None, ALU.mult), [o])
        for t in range(NT):
            a = p.op("vector", lambda e, t=t: e.scalar_tensor_tensor(A[:, t, :], A[:, t, :], net.dinv[:, t:t + 1], rows[:, 0, :], ALU.mult, ALU.add), [lb])
            q = p.op("tensor", lambda e, t=t: e.matmul(PM[:], ones[:, int(t == NT - 1), :], A[:, t, :], start=(t == 0), stop=(t == NT - 1)), [a, o])
        v = p.op("vector", lambda e: e.tensor_scalar(mean[:], PM[:], 1.0 / N, None, ALU.mult), [q])
        for t in range(NT):
            a = p.op("vector", lambda e, t=t: e.tensor_tensor(A[:, t, :], A[:, t, :], mean[:], ALU.subtract), [v])
            s = p.op("scalar", lambda e, t=t: e.activation(sq[:, t, :], A[:, t, :], ACT.Square), [a])
            q = p.op("tensor", lambda e, t=t: e.matmul(PV[:], ones[:, int(t == NT - 1), :], sq[:, t, :], start=(t == 0), stop=(t == NT - 1)), [s])
        s = p.op("scalar", lambda e: e.activation(mean[:], PV[:], ACT.Sqrt, bias=net.eps[:], scale=1.0 / N), [q])
        v = p.op("vector", lambda e: e.reciprocal(mean[:], mean[:]), [s])
        v = p.op("vector", lambda e: e.tensor_tensor(mean[:], mean[:], rows[:, 1, :], ALU.mult), [v])
        v = p.op("vector", lambda e: e.tensor_tensor(A, A, mean[:].rearrange("p (o c) -> p o c", o=1).broadcast_to([128, NT, 128]), ALU.mult), [v])
        v = p.op("vector", lambda e: e.tensor_tensor(A, A, rows[:, 2:3, :].broadcast_to([128, NT, 128]), ALU.add), [v])
        v = p.op("vector", lambda e: e.scalar_tensor_tensor(net.x[:].rearrange("p t c -> p (t c)"), net.acc[:, 0:NT * 128], 0.0, net.x[:].rearrange("p t c -> p (t c)"), ALU.max, ALU.add), [v])
        p.finish()


def pairs(net):
    nc, io = net.nc, net.io
    nm = "pr"
    R, RA, KH, EH, NH = 8, 4, 4, 512, 196
    tab = net.tabs["4"]
    with ExitStack() as c2:
        p = Plan(nc, net.ctx, nm)
        sb = lambda n, s, dt=F32: net.sb(nm + n, s, dt, ctx=c2)
        pm, srcF = sb("pm", [128, 784]), sb("srcF", [128, 784])
        srcC = sb("srcC", [128, 784], I32)
        t0h = sb("t0h", [1, NH + 1], I32)
        G = [sb(f"G{i}", [128, KH, 128]) for i in range(R)]
        MSG = [sb(f"MSG{i}", [128, KH, 128]) for i in range(2)]
        OUT = [sb(f"OUT{i}", [128, KH, 128]) for i in range(3)]
        EQ = [sb(f"EQ{i}", [128, KH, 128]) for i in range(3)]
        ST = sb("ST", [128, EH])
        DR = [sb(f"DR{i}", [128, EH], I32) for i in range(3)]
        SR = [sb(f"SR{i}", [128, EH], I32) for i in range(3)]
        EA = [sb(f"EA{i}", [36, EH]) for i in range(3)]
        hr, hs = sb("hr", [128, 2, 512]), sb("hs", [128, 2, 512])
        w1 = sb("w1", [36, 128])
        w2 = sb("w2", [128, 2, 128])
        b1 = sb("b1", [128, 2])
        b2 = sb("b2", [128, 2, 128])
        bb = sb("bb", [128, 4, 128])
        low = sb("low", [128, 128])
        one = sb("one", [128, 128])
        u = sb("u", [128, 512])
        al = sb("al", [128, 16])
        cnt = sb("cnt", [128, KH])
        junk = sb("junk", [128, 128])
        ti = sb("ti", [128, KH])
        trash = sb("trash", [128, 1])
        idx = [sb(f"idx{i}", [128, KH], I32) for i in range(4)]
        PQ = [net.ps(f"{nm}PQ{i}", [128, KH, 256], c2) for i in range(2)]
        PH = [net.ps(f"{nm}PH{i}", [128, 512], c2) for i in range(2)]
        PW = net.ps(nm + "PW", [128, 512], c2)
        PS = net.ps(nm + "PS", [128, 4, 128], c2)
        xv, xp = p.sem("expv"), p.sem("expp")
        for k in ("expv", "expp"):
            del p.counts[k]
        with ExitStack() as c3:
            rw = net.sb(nm + "rw", [112, 7, 128], I32, ctx=c3)
            rf = net.sb(nm + "rf", [112, 7, 128], ctx=c3)
            rg = net.sb(nm + "rg", [112, 7, 128], ctx=c3)

            def turn(ready, out, last):
                for j in range(7):
                    q = p.op("tensor", lambda e, j=j: e.transpose(PH[0][:, 0:112], rf[:, j, :], net.ident[0:112, 0:112]), [ready, last])
                    last = p.op("vector", lambda e, j=j: e.tensor_copy(out[:, 112 * j:112 * j + 112], PH[0][:, 0:112]), [q])
                return last

            l = p.dma("sync", "rw", lambda e: e.dma_start(rw[:], net.srcp.rearrange("(j q n) -> q j n", q=112, n=128)))
            v = p.op("vector", lambda e: e.tensor_copy(rf[:], rw[:]), [l])
            v = turn(v, srcF, None)
            v = p.op("vector", lambda e: e.tensor_copy(srcC[:], srcF[:]), [v])
            v = p.op("vector", lambda e: e.memset(rf[:], 0.0), [("tensor", p.counts["tensor"])])
            v2 = p.op("vector", lambda e: e.memset(rg[:], 0.0))
            ls = []
            for tgt, n in ((rf, "edge_weight"), (rg, "edge_weight_n2")):
                a = io[n]
                ls.append(p.dma("sync", "ph", lambda e, tgt=tgt, a=a: e.dma_start(tgt[:, 0:6, :], a[0:672 * 128].rearrange("(j q n) -> q j n", q=112, n=128)), [v, v2]))
                ls.append(p.dma("sync", "ph", lambda e, tgt=tgt, a=a: e.dma_start(tgt[0:109, 6, :], a[672 * 128:781 * 128].rearrange("(q n) -> q n", n=128))))
                ls.append(p.dma("sync", "ph", lambda e, tgt=tgt, a=a: e.dma_start(tgt[109:110, 6, 0:32], a[781 * 128:E].rearrange("(q n) -> q n", q=1))))
            v = p.op("vector", lambda e: e.scalar_tensor_tensor(rf[:], rf[:], float(1.0 / np.sqrt(np.float32(32.0))), rg[:], ALU.mult, ALU.mult), ls)
            v = turn(v, pm, v)
        l = p.dma("sync", "t0", lambda e: e.dma_start(t0h[0:1, 0:NH].rearrange("a (n o) -> a n o", o=1), net.dstp.rearrange("(b n) -> b n", n=EH)[:, 0:1].rearrange("(a b) o -> a b o", a=1), allow_slow_non_contiguous=True))
        v = p.op("vector", lambda e: e.tensor_scalar(t0h[0:1, 0:NH], t0h[0:1, 0:NH], 7, None, ALU.arith_shift_right), [l])
        v = p.op("vector", lambda e: e.memset(t0h[0:1, 0:1], 0), [v])
        tready = p.op("vector", lambda e: e.memset(t0h[0:1, NH:NH + 1], NT - 1), [v])
        ready = [p.dma("scalar", "w", lambda e: e.dma_start(w1[0:32, :], io["L3_gnn_rad_W1"])),
                 p.dma("scalar", "w", lambda e: e.dma_start(w1[32:36, :], io["L3_gnn_sph_W1"]))]
        for j, n in enumerate(("rad", "sph")):
            ready.append(p.dma("scalar", "w", lambda e, j=j, n=n: e.dma_start(w2[:, j, :], io[f"L3_gnn_{n}_W2"])))
            ready.append(p.dma("scalar", "w", lambda e, j=j, n=n: e.dma_start(b1[:, j:j + 1], io[f"L3_gnn_{n}_b1"].rearrange("(p o) -> p o", o=1))))
            ready.append(p.dma("scalar", "w", lambda e, j=j, n=n: e.dma_start(b2[:, j, :], row_bcast(io[f"L3_gnn_{n}_b2"], 128))))
        v = p.op("vector", lambda e: e.tensor_tensor(bb[:], b2[:, 0:1, :].broadcast_to([128, 4, 128]), b2[:, 1:2, :].broadcast_to([128, 4, 128]), ALU.add), ready)
        v = p.op("vector", lambda e: e.memset(one[:], 1.0), [v])
        z1 = p.op("vector", lambda e: e.tensor_scalar(trash[:], net.jt[:, 0:1], float(NP), None, ALU.add), [v])
        lo_ = p.op("gpsimd", lambda e: e.affine_select(out=low[:], in_=one[:], compare_op=ALU.is_gt, fill=0.0, base=0, pattern=[[-1, 128]], channel_multiplier=1), [z1])
        p.raw("tensor", lambda e: e.sem_inc(xp, 1))
        hi = {"vector": {}, "tensor": {}}
        gfree, gtok, rtok, etok = [None] * R, {}, {}, {}
        rfree, eafree = [None] * 3, [None] * 3
        phf, hf, pqf, msgf, eqf = [None] * 2, [None] * 2, [None] * 2, [None] * 2, [None] * 3
        psf = pwf = None
        hid, ixr, msg, scat = {}, {}, {}, {}

        def gather(b, after=()):
            s = b % R
            for k in range(KH):
                gtok[b] = p.dma("gpsimd", f"g{s}", lambda e, k=k: e.indirect_dma_start(
                    G[s][:, k, :], None, tab, bass.IndirectOffsetOnAxis(srcC[:, b * KH + k:b * KH + k + 1], 0)), [gfree[s], *after])

        def load(b):
            s = b % 3
            rtok[b] = [p.dma("sync", f"dr{s}", lambda e: e.dma_start(DR[s][:], row_bcast(net.dstp[b * EH:(b + 1) * EH], 128)), [rfree[s]]),
                       p.dma("sync", f"sr{s}", lambda e: e.dma_start(SR[s][:], row_bcast(net.srcp[b * EH:(b + 1) * EH], 128)), [rfree[s]])]
            etok[b] = p.dma("sync", f"ea{s}", lambda e: e.dma_start(EA[s][:], net.attr[:, b * EH:(b + 1) * EH]), [eafree[s]])

        def load_tile(b):
            for q in ("vector", "tensor"):
                def emit(e, q=q):
                    hi[q][b] = e.value_load(t0h[0:1, b:b + 1], min_val=0, max_val=NT - 1)
                p.raw(q, emit, [tready])

        def expand(b):
            dr, pq = DR[b % 3], PQ[b % 2]

            def one_v(e, t):
                e.wait_ge(xp, t + (b + 1))
                e.tensor_scalar(ST[:], dr[:], net.jt[:, bass.ds(t, 1)], None, ALU.is_equal).then_inc(xv, 1)

            def one_p(e, t, first):
                e.wait_ge(xv, t + (b + 1))
                for k in range(KH):
                    i = e.matmul(pq[:, k, :], ST[:, k * 128:k * 128 + 128], net.kv[:, bass.ds(t * 256, 256)], start=first and k % 2 == 0, stop=False, skip_group_check=True)
                i.then_inc(xp, 1)

            def expand_v(e):
                one_v(e, hi["vector"][b])
                with e.If(hi["vector"][b] < hi["vector"][b + 1]):
                    with e.Fori(hi["vector"][b] + 1, hi["vector"][b + 1] + 1) as t:
                        one_v(e, t)

            def expand_p(e):
                one_p(e, hi["tensor"][b], True)
                with e.If(hi["tensor"][b] < hi["tensor"][b + 1]):
                    with e.Fori(hi["tensor"][b] + 1, hi["tensor"][b + 1] + 1) as t:
                        one_p(e, t, False)

            p.raw("vector", expand_v, [rtok[b][0]])
            p.raw("tensor", expand_p, [pqf[b % 2]])

        def hidden(b):
            ea, h = EA[b % 3], b % 2
            a1 = p.op("tensor", lambda e: e.matmul(PH[0][:], w1[0:32, :], ea[0:32, :], start=True, stop=True), [etok[b], phf[0], *ready])
            a2 = p.op("tensor", lambda e: e.matmul(PH[1][:], w1[32:36, :], ea[32:36, :], start=True, stop=True), [phf[1]])
            eafree[b % 3] = a2
            phf[0] = p.op("scalar", lambda e: e.activation(hr[:, h, :], PH[0][:], ACT.Silu, bias=b1[:, 0:1]), [a1, hf[h], *ready])
            phf[1] = hid[b] = p.op("scalar", lambda e: e.activation(hs[:, h, :], PH[1][:], ACT.Silu, bias=b1[:, 1:2]), [a2])

        def equal(b):
            sr, eq, ix = SR[b % 3], EQ[b % 3], idx[b % 4]
            for k in range(KH):
                c = slice(128 * k, 128 * k + 128)
                v = p.op("vector", lambda e, c=c, k=k: e.tensor_scalar(eq[:, k, :], sr[:, c], srcF[:, b * KH + k:b * KH + k + 1], None, ALU.is_equal), [rtok[b][1], eqf[b % 3]])
            rfree[b % 3] = v
            for k in range(KH):
                v = p.op("vector", lambda e, k=k: e.scalar_tensor_tensor(junk[:], eq[:, k, :], 1.0, low[:], ALU.mult, ALU.mult, accum_out=cnt[:, k:k + 1]), [v, lo_])
            sc = srcF[:, b * KH:b * KH + KH]
            v = p.op("vector", lambda e: e.tensor_scalar(cnt[:], cnt[:], 0.5, None, ALU.is_gt), [v])
            w = p.op("vector", lambda e: e.tensor_scalar(ti[:], sc, -1.0, trash[:], ALU.mult, ALU.add))
            v = p.op("vector", lambda e: e.tensor_tensor(ti[:], ti[:], cnt[:], ALU.mult), [w])
            ixr[b] = p.op("vector", lambda e: e.tensor_tensor(ix[:], ti[:], sc, ALU.add), [v, scat.get(b - 4)])

        def filters(b):
            h = b % 2
            for k in range(KH):
                q = slice(128 * k, 128 * k + 128)
                p.op("tensor", lambda e, q=q: e.matmul(PW[:, q], hr[:, h, q], w2[:, 0, :], start=True, stop=False, skip_group_check=True), [hid[b], pwf])
                hf[h] = p.op("tensor", lambda e, q=q: e.matmul(PW[:, q], hs[:, h, q], w2[:, 1, :], start=False, stop=True, skip_group_check=True))

        def weigh(b):
            nonlocal pwf
            g, pq, ms = G[b % R], PQ[b % 2], MSG[b % 2]
            u4 = u[:].rearrange("p (a c) -> p a c", c=128)
            a3 = al[:].rearrange("p (a h) -> p a h", h=4)
            pwf = p.op("vector", lambda e: e.tensor_tensor(u[:], PW[:], bb[:].rearrange("p a c -> p (a c)"), ALU.add), [hf[b % 2]])
            p.raw("vector", lambda e: e.wait_ge(xp, hi["vector"][b + 1] + (b + 2)))
            v = p.op("vector", lambda e: e.tensor_tensor(u4, u4, pq[:, :, 0:128], ALU.mult), [pwf])
            gfree[b % R] = v = p.op("vector", lambda e: e.tensor_tensor(u4, u4, g[:], ALU.mult), [v, gtok[b]])
            v = p.op("vector", lambda e: e.tensor_reduce(al[:], u[:].rearrange("p (a c) -> p a c", c=32), AX.X, ALU.add), [v])
            v = p.op("vector", lambda e: e.tensor_tensor(a3, a3, pm[:, b * KH:b * KH + KH].rearrange("p (a o) -> p a o", o=1).broadcast_to([128, KH, 4]), ALU.mult), [v])
            pqf[b % 2] = msg[b] = p.op("vector", lambda e: e.tensor_tensor(
                ms[:].rearrange("p a (h c) -> p a h c", c=32), pq[:, :, 128:256].rearrange("p a (h c) -> p a h c", c=32),
                al[:].rearrange("p (a h o) -> p a h o", h=4, o=1).broadcast_to([128, KH, 4, 32]), ALU.mult), [v, msgf[b % 2]])

        def add(b):
            nonlocal psf
            eq, ms, out, ix = EQ[b % 3], MSG[b % 2], OUT[b % 3], idx[b % 4]
            for k in range(KH):
                q = p.op("tensor", lambda e, k=k: e.matmul(PS[:, k, :], eq[:, k, :], ms[:, k, :], start=True, stop=True), [msg[b], psf])
            eqf[b % 3] = msgf[b % 2] = q
            psf = p.op("scalar", lambda e: e.copy(out[:], PS[:]), [q, scat.get(b - 3)])
            scat[b] = [p.dma("gpsimd", f"s{k}", lambda e, k=k: e.indirect_dma_start(
                net.sums[k], bass.IndirectOffsetOnAxis(ix[:, k:k + 1], 0), out[:, k, :], None, compute_op=ALU.add),
                [psf, ixr[b], *([scat[b - 1][k]] if b else [])]) for k in range(RA)]
            if b + R < NH:
                gather(b + R)

        for b in range(R):
            gather(b, [z1])
        for b in range(3):
            load(b)
        load_tile(0)
        load_tile(1)
        hidden(0)
        expand(0)
        equal(0)
        for b in range(NH):
            if b + 1 < NH:
                load_tile(b + 2)
                hidden(b + 1)
            filters(b)
            if b + 1 < NH:
                expand(b + 1)
            weigh(b)
            if b + 1 < NH:
                equal(b + 1)
            if b:
                add(b - 1)
            if b + 3 < NH:
                load(b + 3)
        add(NH - 1)
        last = [(f"s{r}", p.counts[f"s{r}"]) for r in range(RA)]
        L = [G[0:RA], G[RA:2 * RA]]
        done = ("vector", p.counts["vector"])
        lf = [[None] * RA for _ in range(2)]
        slots = [f"{n}{i}" for n in ("dr", "sr", "ea") for i in range(3)]
        for j, t0 in enumerate(range(0, NT, KH)):
            n, s = min(KH, NT - t0), j % 2
            for r in range(RA):
                ld = p.dma("sync", slots[s * RA + r], lambda e, r=r, s=s, t0=t0, n=n: e.dma_start(L[s][r][:, 0:n, :], net.sums[r][t0 * 128:(t0 + n) * 128, :].rearrange("(t q) c -> q t c", q=128)), [*last, done, lf[s][r]])
                a = lf[s][r] = p.op("vector", lambda e, r=r, s=s, t0=t0, n=n: e.tensor_tensor(net.x[:, t0:t0 + n, :], net.x[:, t0:t0 + n, :], L[s][r][:, 0:n, :], ALU.add), [ld, ("vector", p.counts["vector"])])
        p.dma("sync", "out", lambda e: e.dma_start(io["out"][0:(NT - 1) * 128, :].rearrange("(t q) c -> q t c", q=128), net.x[:, 0:NT - 1, :]), [a])
        p.dma("sync", "out", lambda e: e.dma_start(io["out"][(NT - 1) * 128:N, :], net.x[0:TAIL, NT - 1, :]), [a])
        p.finish()


def build(nc, io):
    with ExitStack() as ctx:
        net = Net(nc, ctx, io)
        setup(net)
        with ExitStack() as c2:
            net.sv = net.sb("sv", [128, NT, 8], ctx=c2)
            net.svf = net.sv[:].rearrange("p t h -> p (t h)")
            net.acc = net.sb("acc", [128, NT * 146], ctx=c2)
            net.aux = net.sb("aux", [128, NT * 128], ctx=c2)
            m = masks(net, c2)
            nodes(net, 0)
            edges(net, 0, m)
            final_attention(net, 0)
            nodes(net, 1)
            edges(net, 1)
            final_conv(net)
            for kind in (2, 3):
                nodes(net, kind)
                edges(net, kind, m)
                final_attention(net, kind)
        net.kv = net.sb("kv", [128, NT * 256])
        nodes(net, 4)
        pairs(net)


FLOATS = ["x", "edge_weight", "edge_weight_n2", "L0_gnn_ln_gamma", "L0_gnn_ln_beta", "L0_gnn_W_in", "L0_gnn_b_in",
          "L0_gnn_W_u", "L0_gnn_b_u", "L0_gnn_W_v", "L0_gnn_W_ff", "L0_gnn_b_ff", "L1_gnn_W", "L1_gnn_b",
          "L1_gnn_gamma", "L1_gnn_beta", "L2_gnn_W1", "L2_gnn_as1", "L2_gnn_ad1", "L2_gnn_b1", "L2_gnn_W2",
          "L2_gnn_as2", "L2_gnn_ad2", "L2_gnn_b2", "L3_gnn_rad_W1", "L3_gnn_rad_b1", "L3_gnn_rad_W2",
          "L3_gnn_rad_b2", "L3_gnn_sph_W1", "L3_gnn_sph_b1", "L3_gnn_sph_W2", "L3_gnn_sph_b2", "L3_gnn_Wq",
          "L3_gnn_Wk", "L3_gnn_Wv"]


def kernel(**inputs):
    import numpy as _np
    import concourse.bacc as _bacc
    from concourse import mybir as _mybir
    from concourse.bass_utils import run_bass_kernel_spmd as _run

    nc = _bacc.Bacc("TRN2", target_bir_lowering=False, num_devices=1)
    arrays = {n: _np.ascontiguousarray(inputs[n]) for n in FLOATS + ["src", "dst"]}
    arrays["attr32T"] = _np.ascontiguousarray(_np.asarray(inputs["edge_attr_32"]).T)
    arrays["attr4T"] = _np.ascontiguousarray(_np.asarray(inputs["edge_attr_4"]).T)
    maps, io = {}, {}
    for n, a in arrays.items():
        maps[f"in_{n}"] = a
        io[n] = nc.dram_tensor(f"in_{n}", a.shape, _mybir.dt.from_np(a.dtype), kind="ExternalInput").ap()
    io["out"] = nc.dram_tensor("out_x", (N, D), _mybir.dt.float32, kind="ExternalOutput").ap()
    build(nc, io)
    r = _run(nc, [maps], core_ids=[0])
    return r.results[0]["out_x"]
```

```python
from contextlib import ExitStack

import numpy as np

import concourse.bass as bass
from concourse import mybir

F32 = mybir.dt.float32
BF16 = mybir.dt.bfloat16
I32 = mybir.dt.int32
ALU = mybir.AluOpType
ACT = mybir.ActivationFunctionType
AX = mybir.AxisListType

N = 6250
E = 100000
D = 128
NT = 49
NB = 49
KB = 16
EB = 2048
EP = NB * EB
NP = NT * 128
TAIL = N - (NT - 1) * 128
BIG = 1.0e30
NOWHERE = 1000000
GROUPS = [(4 * g, min(4, NT - 4 * g)) for g in range(13)]


class Plan:

    def __init__(self, nc, ctx, name):
        self.nc, self.ctx, self.name = nc, ctx, name
        self.queues = {k: [] for k in ("sync", "gpsimd", "scalar", "vector", "tensor")}
        self.sems, self.counts, self.seen = {}, {}, {}

    def sem(self, key):
        if key not in self.sems:
            self.sems[key] = self.ctx.enter_context(self.nc.semaphore(f"{self.name}_{key}"))
            self.counts[key] = 0
        return self.sems[key]

    def _waits(self, eng, after):
        out, last = [], {}
        flat = [t for a in after if a for t in (a if isinstance(a, list) else [a])]
        for key, value in flat:
            last[key] = max(value, last.get(key, 0))
        for key, value in last.items():
            if self.seen.get((eng, key), 0) < value:
                self.seen[(eng, key)] = value
                out.append((self.sem(key), value))
        return out

    def op(self, eng, fn, after=()):
        sem = self.sem(eng)
        waits = self._waits(eng, after)
        self.counts[eng] += 1

        def emit(e):
            for s, v in waits:
                e.wait_ge(s, v)
            fn(e).then_inc(sem, 1)

        self.queues[eng].append(emit)
        return (eng, self.counts[eng])

    def dma(self, eng, slot, fn, after=()):
        sem = self.sem(slot)
        waits = self._waits(eng, after)
        self.counts[slot] += 16

        def emit(e):
            for s, v in waits:
                e.wait_ge(s, v)
            fn(e).then_inc(sem, 16)

        self.queues[eng].append(emit)
        return (slot, self.counts[slot])

    def raw(self, eng, fn, after=()):
        waits = self._waits(eng, after)

        def emit(e):
            for s, v in waits:
                e.wait_ge(s, v)
            fn(e)

        self.queues[eng].append(emit)

    def finish(self):
        for key, value in self.counts.items():
            if key not in self.queues:
                self.raw("sync", lambda e: None, [(key, value)])
        with self.nc.Block() as block:
            for eng, queue in self.queues.items():
                def run(e, queue=queue):
                    for emit in queue:
                        emit(e)

                on = {"sync": block.sync, "gpsimd": block.gpsimd, "scalar": block.scalar,
                      "vector": block.vector, "tensor": block.tensor}
                on[eng](run)


def row_bcast(ap, parts):
    return bass.AP(ap.tensor, ap.offset, [[0, parts], [1, ap.shape[0]]])


class Net:
    def __init__(self, nc, ctx, io):
        self.nc, self.ctx, self.io = nc, ctx, io
        sb = self.sb
        self.x = sb("x_res", [128, NT, 128])
        self.ident = sb("ident", [128, 128])
        self.iota = sb("iota", [128, 128])
        self.jt = sb("jt", [128, NT])
        self.tb = sb("tb", [128, NT])
        self.t0 = sb("t0", [1, NB + 1], I32)
        self.dinv = sb("dinv", [128, NT])
        self.srcS = sb("srcS", [128, NB * KB], I32)
        self.dstS = sb("dstS", [128, NB, KB])
        self.eps = sb("eps", [128, 1])
        self.tabs = {p: self.dram(f"tab{p}", (NP, w)) for p, w in
                     (("0", 136), ("1", 128), ("2", 129), ("3", 129), ("4", 128))}
        self.dstp = self.dram("dstp", (EP,), I32)
        self.srcp = self.dram("srcp", (EP,), I32)
        self.attr = self.dram("attrp", (36, EP))
        self.sums = [self.dram(f"sums{r}", (NP + 128, D)) for r in range(2)]
        self.srcc = self.dram("srcc", (128, 784), I32)
        self.cols = self.dram("cols", (2, 128, 784))
        self.gfr = self.dram("gfr", (2, NB, 128))

    def dram(self, name, shape, dt=F32):
        return self.nc.dram_tensor(name, shape, dt, kind="Internal").ap()

    def sb(self, name, shape, dt=F32, ctx=None):
        return (ctx or self.ctx).enter_context(self.nc.sbuf_tensor(name, shape, dt))

    def ps(self, name, shape, ctx):
        return ctx.enter_context(self.nc.psum_tensor(name, shape, F32))


def setup(net):
    nc, io = net.nc, net.io
    with ExitStack() as ctx:
        p = Plan(nc, net.ctx, "su")
        one = net.sb("su_one", [128, 128], ctx=ctx)
        padi = net.sb("su_padi", [1, 352], I32, ctx=ctx)
        zeroi = net.sb("su_zeroi", [1, 352], I32, ctx=ctx)
        padf = net.sb("su_padf", [36, 352], ctx=ctx)
        raw = net.sb("su_raw", [128, NB, KB], I32, ctx=ctx)
        t0f = net.sb("su_t0", [1, NB + 1], I32, ctx=ctx)
        a = p.op("vector", lambda e: e.memset(padi[:], NOWHERE))
        b = p.op("vector", lambda e: e.memset(zeroi[:], 0))
        c = p.op("vector", lambda e: e.memset(padf[:], 0.0))
        f = [p.dma("sync", "fill", lambda e: e.dma_start(net.dstp[E:EP].rearrange("(a n) -> a n", a=1), padi[:]), [a]),
             p.dma("sync", "fill", lambda e: e.dma_start(net.srcp[E:EP].rearrange("(a n) -> a n", a=1), zeroi[:]), [b]),
             p.dma("sync", "fill", lambda e: e.dma_start(net.dstp[0:E].rearrange("(a n) -> a n", a=16), io["dst"].rearrange("(a n) -> a n", a=16))),
             p.dma("sync", "fill", lambda e: e.dma_start(net.srcp[0:E].rearrange("(a n) -> a n", a=16), io["src"].rearrange("(a n) -> a n", a=16)))]
        l1 = p.dma("sync", "l1", lambda e: e.dma_start(raw[:], net.dstp.rearrange("(b p k) -> p b k", p=128, k=KB)), [f[-1]])
        p.dma("sync", "l2", lambda e: e.dma_start(net.srcS[:].rearrange("p (b k) -> p b k", k=KB), net.srcp.rearrange("(b p k) -> p b k", p=128, k=KB)), [f[-1]])
        l3 = p.dma("sync", "l3", lambda e: e.dma_start(t0f[0:1, 0:NB].rearrange("a (n o) -> a n o", o=1), net.dstp.rearrange("(b n) -> b n", n=EB)[:, 0:1].rearrange("(a b) o -> a b o", a=1), allow_slow_non_contiguous=True), [f[-1]])
        v = p.op("vector", lambda e: e.tensor_copy(net.dstS[:], raw[:]), [l1])
        v = p.op("vector", lambda e: e.tensor_scalar(net.t0[0:1, 0:NB], t0f[0:1, 0:NB], 7, None, ALU.arith_shift_right), [l3])
        v = p.op("vector", lambda e: e.memset(net.t0[0:1, 0:1], 0), [v])
        v = p.op("vector", lambda e: e.memset(net.t0[0:1, NB:NB + 1], NT - 1), [v])
        p.op("vector", lambda e: e.memset(net.eps[:], 1e-5))
        o = p.op("vector", lambda e: e.memset(one[:], 1.0))
        g = p.op("gpsimd", lambda e: e.affine_select(out=net.ident[:], in_=one[:], compare_op=ALU.is_equal, fill=0.0, base=0, pattern=[[-1, 128]], channel_multiplier=1), [o])
        p.op("gpsimd", lambda e: e.iota(net.iota[:], pattern=[[1, 128]], base=0, channel_multiplier=0, allow_small_or_imprecise_dtypes=True))
        p.op("gpsimd", lambda e: e.iota(net.jt[:], pattern=[[128, NT]], base=0, channel_multiplier=1, allow_small_or_imprecise_dtypes=True))
        p.op("gpsimd", lambda e: e.iota(net.tb[:], pattern=[[128, NT]], base=0, channel_multiplier=0, allow_small_or_imprecise_dtypes=True))
        z = p.op("vector", lambda e: e.memset(net.x[:, NT - 1, :], 0.0))
        p.dma("scalar", "x", lambda e: e.dma_start(net.x[:, 0:NT - 1, :], io["x"][0:(NT - 1) * 128, :].rearrange("(t p) c -> p t c", p=128)))
        p.dma("scalar", "x", lambda e: e.dma_start(net.x[0:TAIL, NT - 1, :], io["x"][(NT - 1) * 128:N, :]), [z])
        p.dma("scalar", "x", lambda e: e.dma_start(net.attr[:, E:EP], padf[:]), [c])
        p.finish()


def masks(net, ctx):
    m = {k: net.sb("m_" + k, [128, NB, KB], ctx=ctx) for k in ("MF", "MB", "FM", "LM", "isl")}
    nc = net.nc
    with ExitStack() as c2:
        p = Plan(nc, net.ctx, "mk")
        sh = net.sb("mk_sh", [128, 128], ctx=c2)
        sh2 = net.sb("mk_sh2", [128, 128], ctx=c2)
        one = net.sb("mk_one", [128, 128], ctx=c2)
        prev = net.sb("mk_prev", [128, NB, KB], ctx=c2)
        nxt = net.sb("mk_next", [128, NB, KB], ctx=c2)
        keep = net.sb("mk_keep", [128, NB, KB], ctx=c2)
        keep2 = net.sb("mk_keep2", [128, NB, KB], ctx=c2)
        sen = net.sb("mk_sen", [128, 2], ctx=c2)
        rows = net.sb("mk_rows", [NB, 2, 128], ctx=c2)
        pa = net.ps("mk_pa", [128, NB], c2)
        pb = net.ps("mk_pb", [128, NB], c2)
        pc = net.ps("mk_pc", [NB, 2, 128], c2)
        o = p.op("vector", lambda e: e.memset(one[:], 1.0))
        g1 = p.op("gpsimd", lambda e: e.affine_select(out=sh[:], in_=one[:], compare_op=ALU.is_equal, fill=0.0, base=1, pattern=[[-1, 128]], channel_multiplier=1), [o])
        g2 = p.op("gpsimd", lambda e: e.affine_select(out=sh2[:], in_=one[:], compare_op=ALU.is_equal, fill=0.0, base=-1, pattern=[[-1, 128]], channel_multiplier=1), [o])
        t1 = p.op("tensor", lambda e: e.matmul(pa[:], sh[:], net.dstS[:, :, KB - 1], start=True, stop=True), [g1])
        t2 = p.op("tensor", lambda e: e.matmul(pb[:], sh2[:], net.dstS[:, :, 0], start=True, stop=True), [g2])
        s1 = p.op("vector", lambda e: e.tensor_scalar(sen[:, 0:1], net.jt[:, 0:1], 0.0, -5.0, ALU.is_equal, ALU.mult))
        s2 = p.op("vector", lambda e: e.tensor_scalar(sen[:, 1:2], net.jt[:, 0:1], 127.0, -5.0, ALU.is_equal, ALU.mult))
        v1 = p.op("vector", lambda e: e.tensor_copy(prev[:, :, 1:KB], net.dstS[:, :, 0:KB - 1]))
        v2 = p.op("vector", lambda e: e.tensor_copy(nxt[:, :, 0:KB - 1], net.dstS[:, :, 1:KB]))
        v3 = p.op("vector", lambda e: e.tensor_scalar(prev[:, :, 0], pa[:], sen[:, 0:1], None, ALU.add), [t1, s2])
        v4 = p.op("vector", lambda e: e.tensor_scalar(nxt[:, :, KB - 1], pb[:], sen[:, 1:2], None, ALU.add), [t2])
        v5 = p.op("vector", lambda e: e.tensor_tensor(m["FM"][:], net.dstS[:], prev[:], ALU.not_equal), [v4])
        v6 = p.op("vector", lambda e: e.tensor_tensor(m["isl"][:], net.dstS[:], nxt[:], ALU.not_equal), [v4])
        k1 = p.op("vector", lambda e: e.memset(keep[:], 1.0))
        k1 = p.op("vector", lambda e: e.memset(keep[:, :, 0:1], 0.0), [k1])
        k2 = p.op("vector", lambda e: e.memset(keep2[:], 1.0))
        k2 = p.op("vector", lambda e: e.memset(keep2[:, :, KB - 1:KB], 0.0), [k2])
        a = p.op("vector", lambda e: e.tensor_scalar(m["MF"][:], m["FM"][:], -BIG, None, ALU.mult), [k2])
        a = p.op("vector", lambda e: e.memset(m["MF"][:, :, 0:1], -BIG), [a])
        a = p.op("vector", lambda e: e.tensor_scalar(m["MB"][:], m["isl"][:], -BIG, None, ALU.mult), [v6])
        a = p.op("vector", lambda e: e.memset(m["MB"][:, :, KB - 1:KB], -BIG), [a])

        def flat(t):
            return t[:].rearrange("p b k -> p (b k)")

        a1 = p.op("vector", lambda e: e.tensor_tensor_scan(flat(prev), flat(keep), flat(m["FM"]), 0.0, ALU.mult, ALU.max), [a])
        a2 = p.op("vector", lambda e: e.tensor_tensor_scan(flat(nxt)[:, ::-1], flat(keep2)[:, ::-1], flat(m["isl"])[:, ::-1], 0.0, ALU.mult, ALU.max), [a])
        a3 = p.op("vector", lambda e: e.tensor_scalar(m["FM"][:], prev[:], -BIG, None, ALU.mult), [a1])
        a4 = p.op("vector", lambda e: e.tensor_scalar(m["LM"][:], nxt[:], -BIG, None, ALU.mult), [a2])
        t3 = p.op("tensor", lambda e: e.matmul(pc[:, 0, :], m["FM"][:, :, KB - 1], net.ident[:], start=True, stop=True), [a3])
        t4 = p.op("tensor", lambda e: e.matmul(pc[:, 1, :], m["LM"][:, :, 0], net.ident[:], start=True, stop=True), [a4])
        v7 = p.op("vector", lambda e: e.tensor_copy(rows[:], pc[:]), [t3, t4])
        p.dma("sync", "gfr", lambda e: e.dma_start(net.gfr.rearrange("s b n -> b s n"), rows[:]), [v7])
        p.finish()
    return m


class LayerNorm:

    def __init__(self, net, p, src, c2, name):
        self.net, self.p, self.src = net, p, src
        self.st = net.sb(name + "_st", [128, NT, 6], ctx=c2)
        self.mv = net.sb(name + "_mv", [128, NT, 2], ctx=c2)
        self.rs = net.sb(name + "_rs", [128, NT], ctx=c2)
        self.nb = net.sb(name + "_nb", [128, NT], ctx=c2)

    def part(self, lo, hi, after):
        net, p, st, mv, rs, nb = self.net, self.p, self.st, self.mv, self.rs, self.nb
        for t in range(lo, hi):
            a = p.op("vector", lambda e, t=t: e.bn_stats(st[:, t, :], self.src[:, t, :]), [after[t]])
        for t in range(lo, hi):
            a = p.op("vector", lambda e, t=t: e.bn_aggr(mv[:, t, :], st[:, t, :]), [a] if t == lo else ())
        s = p.op("scalar", lambda e: e.activation(rs[:, lo:hi], mv[:, lo:hi, 1], ACT.Sqrt, bias=net.eps[:]), [a])
        r = p.op("vector", lambda e: e.reciprocal(rs[:, lo:hi], rs[:, lo:hi]), [s])
        return p.op("vector", lambda e: e.scalar_tensor_tensor(nb[:, lo:hi], mv[:, lo:hi, 0], -1.0, rs[:, lo:hi], ALU.mult, ALU.mult), [r])


def nodes(net, kind):
    nc, io = net.nc, net.io
    nm = f"n{kind}"
    H = {0: 8, 1: 0, 2: 1, 3: 1, 4: 0}[kind]
    W = {0: 136, 1: 128, 2: 129, 3: 129, 4: 128}[kind]
    tab = net.tabs[str(kind)]
    with ExitStack() as c2:
        p = Plan(nc, net.ctx, nm)

        def load(name, shape, ap):
            t = net.sb(nm + name, shape, ctx=c2)
            return t, p.dma("sync", "w", lambda e: e.dma_start(t[:], ap))

        def col(ap):
            return ap.rearrange("(p o) -> p o", o=1)

        ready = []
        if kind == 0:
            Wm, k = load("W", [128, 128], io["L0_gnn_W_in"]); ready.append(k)
            Wa = net.sb(nm + "Wa", [128, 16], ctx=c2)
            ready.append(p.dma("sync", "w", lambda e: e.dma_start(Wa[:, 0:8], io["L0_gnn_W_u"])))
            ready.append(p.dma("sync", "w", lambda e: e.dma_start(Wa[:, 8:16], io["L0_gnn_W_v"])))
            gam, k = load("gam", [128, 1], col(io["L0_gnn_ln_gamma"])); ready.append(k)
            bet, k = load("bet", [128, 1], col(io["L0_gnn_ln_beta"])); ready.append(k)
            bcol, k = load("bcol", [128, 1], col(io["L0_gnn_b_in"])); ready.append(k)
            brow, k = load("brow", [128, 128], row_bcast(io["L0_gnn_b_in"], 128)); ready.append(k)
            burow, k = load("burow", [128, 8], row_bcast(io["L0_gnn_b_u"], 128)); ready.append(k)
        elif kind == 1:
            Wm, k = load("W", [128, 128], io["L1_gnn_W"]); ready.append(k)
        elif kind in (2, 3):
            s = str(kind - 1)
            Wm, k = load("W", [128, 128], io["L2_gnn_W" + s]); ready.append(k)
            Wa = net.sb(nm + "Wa", [128, 2], ctx=c2)
            ready.append(p.dma("sync", "w", lambda e: e.dma_start(Wa[:, 0:1], col(io["L2_gnn_as" + s]))))
            ready.append(p.dma("sync", "w", lambda e: e.dma_start(Wa[:, 1:2], col(io["L2_gnn_ad" + s]))))
        else:
            Wm = net.sb(nm + "W", [128, 384], ctx=c2)
            z = p.op("vector", lambda e: e.memset(Wm[:], 0.0))
            for j, w in enumerate(("Wq", "Wk", "Wv")):
                for h in range(4):
                    ready.append(p.dma("sync", "w", lambda e, j=j, w=w, h=h: e.dma_start(
                        Wm[32 * h:32 * h + 32, 128 * j + 32 * h:128 * j + 32 * h + 32], io["L3_gnn_" + w][h]), [z]))
        hn = net.sb(nm + "hn", [128, NT, 128], ctx=c2)
        if kind == 3:
            hsrc, hready = net.aux[:].rearrange("p (t c) -> p t c", c=128), [None] * NT
        else:
            ln = LayerNorm(net, p, net.x, c2, nm + "l")
            ln2 = LayerNorm(net, p, hn, c2, nm + "m") if kind == 0 else None
            hsrc, hready = hn, [None] * NT

        def normalise(lo, hi):
            if kind == 3:
                return
            n = ln.part(lo, hi, hready)
            for t in range(lo, hi):
                hready[t] = p.op("scalar", lambda e, t=t: e.activation(hn[:, t, :], net.x[:, t, :], ACT.Relu, bias=ln.nb[:, t:t + 1], scale=ln.rs[:, t:t + 1]), [n])

        def normalise_again(lo, hi):
            if kind != 0:
                return
            n = ln2.part(lo, hi, hready)
            for t in range(lo, hi):
                hready[t] = p.op("scalar", lambda e, t=t: e.activation(hn[:, t, :], hn[:, t, :], ACT.Identity, bias=ln2.nb[:, t:t + 1], scale=ln2.rs[:, t:t + 1]), [n])

        hT = net.sb(nm + "hT", [128, 3, 512], ctx=c2)
        gT = net.sb(nm + "gT", [128, 3, 512], ctx=c2)
        TB = net.sb(nm + "TB", [128, 3, 4, W], ctx=c2)
        P1 = [net.ps(f"{nm}P1{i}", [128, 4, 128], c2) for i in range(2)]
        P2 = net.ps(nm + "P2", [128, 512], c2) if H else None
        P3 = [net.ps(f"{nm}P3{i}", [128, 512], c2) for i in range(3)]
        P4 = net.ps(nm + "P4", [128, 4, 16], c2) if H else None
        w = 2 * H
        accv = None if kind == 4 else net.acc[:, 0:NT * {0: 146, 1: 128, 2: 130, 3: 130}[kind]].rearrange("p (t c) -> p t c", t=NT)
        stored, hTfree, gTfree = [None] * 3, [None] * 3, [None] * 3
        free1, free3 = [None, None], [None, None, None]
        free2 = free4 = None
        evac, scored = {}, {}
        fin = {g: [] for g in range(len(GROUPS))}
        n3 = 0
        sv = net.sv if H else None

        def turn(g):
            (t0, nt), s, L = GROUPS[g], g % 3, GROUPS[g][1] * 128
            P = P1[g % 2]
            for j in range(nt):
                a = p.op("tensor", lambda e, j=j: e.transpose(P[:, j, :], hsrc[:, t0 + j, :], net.ident[:]), [hready[t0 + j], free1[g % 2]])
            flat = P[:, 0:nt, :].rearrange("p a b -> p (a b)")
            if kind == 0:
                ev = p.op("vector", lambda e: e.tensor_scalar(hT[:, s, 0:L], flat, gam[:], bet[:], ALU.mult, ALU.add), [a, *(hTfree[s] or []), *ready])
            else:
                ev = p.op("vector", lambda e: e.tensor_copy(hT[:, s, 0:L], flat), [a, *(hTfree[s] or [])])
            free1[g % 2] = evac[g] = ev

        def multiply(g):
            nonlocal free2, n3
            (t0, nt), s, L = GROUPS[g], g % 3, GROUPS[g][1] * 128
            hTfree[s] = []
            if H:
                a = p.op("tensor", lambda e: e.matmul(P2[:, 0:L], Wm[:], hT[:, s, 0:L], start=True, stop=True), [evac[g], free2] + ready)
                hTfree[s].append(a)
                if kind == 0:
                    free2 = p.op("scalar", lambda e: e.activation(gT[:, s, 0:L], P2[:, 0:L], ACT.Identity, bias=bcol[:]), [a, gTfree[s]] + ready)
                else:
                    free2 = p.op("scalar", lambda e: e.copy(gT[:, s, 0:L], P2[:, 0:L]), [a, gTfree[s]])
                scored[g] = free2
            if kind == 4:
                for j in range(nt):
                    b = n3 % 3
                    n3 += 1
                    a = p.op("tensor", lambda e, b=b, j=j: e.matmul(P3[b][:, 0:384], hT[:, s, 128 * j:128 * j + 128], Wm[:], start=True, stop=True), [evac[g], *(free3[b] or []), *ready])
                    eng = "scalar" if j % 2 else "vector"

                    def out(to, b, lo, hi, eng=eng):
                        return lambda e: (e.copy if eng == "scalar" else e.tensor_copy)(to, P3[b][:, lo:hi])

                    c = p.op(eng, out(TB[:, s, j, :], b, 0, 128), [a, stored[s]])
                    d = p.op(eng, out(net.kv[:, (t0 + j) * 256:(t0 + j + 1) * 256], b, 128, 384))
                    free3[b] = [c, d]
                    fin[g] += [c, d]
                hTfree[s].append(a)
                return
            b = n3 % 3
            n3 += 1
            for j in range(nt):
                a = p.op("tensor", lambda e, j=j: e.matmul(P3[b][:, 128 * j:128 * j + 128], hT[:, s, 128 * j:128 * j + 128], Wm[:], start=True, stop=True), [evac[g], free3[b]] + ready)
            hTfree[s].append(a)
            src = P3[b][:, 0:L].rearrange("p (a c) -> p a c", c=128)
            if kind == 0:
                c = p.op("vector", lambda e: e.tensor_tensor(TB[:, s, 0:nt, 0:128], src, brow[:].rearrange("p (a c) -> p a c", a=1).broadcast_to([128, nt, 128]), ALU.add), [a, stored[s]])
            elif kind == 1:
                c = p.op("vector", lambda e: e.tensor_tensor(TB[:, s, 0:nt, 0:128], src, net.dinv[:, t0:t0 + nt].rearrange("p (t o) -> p t o", o=1).broadcast_to([128, nt, 128]), ALU.mult), [a, stored[s]])
            else:
                c = p.op("vector", lambda e: e.tensor_copy(TB[:, s, 0:nt, 0:128], src), [a, stored[s]])
            if kind != 0:
                fin[g].append(p.op("scalar", lambda e: e.copy(accv[:, t0:t0 + nt, 0:128], TB[:, s, 0:nt, 0:128]), [c]))
            free3[b] = c
            fin[g].append(c)

        def store(g):
            nonlocal free4
            (t0, nt), s = GROUPS[g], g % 3
            if H:
                for j in range(nt):
                    a = p.op("tensor", lambda e, j=j: e.matmul(P4[:, j, 0:w], gT[:, s, 128 * j:128 * j + 128], Wa[:], start=True, stop=True), [scored[g], free4])
                gTfree[s] = a
                if kind == 0:
                    c = p.op("vector", lambda e: e.tensor_tensor(TB[:, s, 0:nt, 128:136], P4[:, 0:nt, 0:8], burow[:].rearrange("p (a c) -> p a c", a=1).broadcast_to([128, nt, 8]), ALU.add), [a])
                else:
                    c = p.op("vector", lambda e: e.tensor_copy(TB[:, s, 0:nt, 128:129], P4[:, 0:nt, 0:1]), [a])
                free4 = d = p.op("vector", lambda e: e.tensor_copy(sv[:, t0:t0 + nt, 0:H], P4[:, 0:nt, H:2 * H]), [a])
                fin[g] += [c, d]
                if kind != 0:
                    d = p.op("vector", lambda e: e.tensor_tensor(accv[:, t0:t0 + nt, 129:130], TB[:, s, 0:nt, 128:129], sv[:, t0:t0 + nt, 0:1], ALU.add), [d])
                    d = p.op("vector", lambda e: e.scalar_tensor_tensor(accv[:, t0:t0 + nt, 129], accv[:, t0:t0 + nt, 129], 0.2, accv[:, t0:t0 + nt, 129], ALU.mult, ALU.max), [d])
                    fin[g].append(d)
            stored[s] = p.dma("sync", f"tab{s}", lambda e: e.dma_start(tab[t0 * 128:(t0 + nt) * 128, :].rearrange("(t q) c -> q t c", q=128), TB[:, s, 0:nt, :]), fin[g])

        if kind == 0:
            z = p.op("gpsimd", lambda e: e.memset(net.acc[:], 0.0))
            p.op("gpsimd", lambda e: e.memset(accv[:, :, 136:144], -BIG), [z])
        if kind in (2, 3):
            p.op("gpsimd", lambda e: e.memset(accv[:, :, 128:129], 1.0))
        ends = [(t0, t0 + nt) for t0, nt in GROUPS]
        ahead = 3
        for g in range(ahead):
            normalise(*ends[g])
            if g:
                normalise_again(*ends[g - 1])
        for g in range(len(GROUPS)):
            if g + ahead < len(GROUPS):
                normalise(*ends[g + ahead])
            if g + ahead - 1 < len(GROUPS):
                normalise_again(*ends[g + ahead - 1])
            turn(g)
            if g >= 1:
                multiply(g - 1)
            if g >= 2:
                store(g - 2)
        multiply(len(GROUPS) - 1)
        store(len(GROUPS) - 2)
        store(len(GROUPS) - 1)
        p.finish()


def columns(net, p, c2):
    io = net.io
    rw = net.sb("co_rw", [112, 7, 128], I32, ctx=c2)
    rf = net.sb("co_rf", [112, 7, 128], ctx=c2)
    rg = net.sb("co_rg", [112, 7, 128], ctx=c2)
    out = net.sb("co_out", [128, 2, 784], ctx=c2)
    srcc = net.sb("co_src", [128, 784], I32, ctx=c2)
    P = net.ps("co_P", [128, 112], c2)

    def turn(ready, i, last):
        for j in range(7):
            q = p.op("tensor", lambda e, j=j: e.transpose(P[:], rf[:, j, :], net.ident[0:112, 0:112]), [ready, last])
            last = p.op("vector", lambda e, j=j: e.tensor_copy(out[:, i, 112 * j:112 * j + 112], P[:]), [q])
        return q, last

    l = p.dma("sync", "rw", lambda e: e.dma_start(rw[:], net.srcp.rearrange("(j q n) -> q j n", q=112, n=128)))
    v = p.op("vector", lambda e: e.tensor_copy(rf[:], rw[:]), [l])
    q, v = turn(v, 0, None)
    c = p.op("vector", lambda e: e.tensor_copy(srcc[:], out[:, 0, :]), [v])
    v = p.op("vector", lambda e: e.memset(rf[:], 0.0), [q])
    v2 = p.op("vector", lambda e: e.memset(rg[:], 0.0))
    ls = []
    for tgt, n in ((rf, "edge_weight"), (rg, "edge_weight_n2")):
        a = io[n]
        ls.append(p.dma("sync", "ph", lambda e, tgt=tgt, a=a: e.dma_start(tgt[:, 0:6, :], a[0:672 * 128].rearrange("(j q n) -> q j n", q=112, n=128)), [v, v2]))
        ls.append(p.dma("sync", "ph", lambda e, tgt=tgt, a=a: e.dma_start(tgt[0:109, 6, :], a[672 * 128:781 * 128].rearrange("(q n) -> q n", n=128))))
        ls.append(p.dma("sync", "ph", lambda e, tgt=tgt, a=a: e.dma_start(tgt[109:110, 6, 0:32], a[781 * 128:E].rearrange("(q n) -> q n", q=1))))
    f = p.op("vector", lambda e: e.scalar_tensor_tensor(rf[:], rf[:], float(1.0 / np.sqrt(np.float32(32.0))), rg[:], ALU.mult, ALU.mult), ls)
    q, f = turn(f, 1, v)
    p.dma("scalar", "cols", lambda e: e.dma_start(net.srcc, srcc[:]), [c])
    p.dma("scalar", "cols", lambda e: e.dma_start(net.cols.rearrange("s p n -> p s n"), out[:]), [f])


def edges(net, kind, m=None):
    nc, io = net.nc, net.io
    nm = f"e{kind}"
    H = {0: 8, 1: 0, 2: 1, 3: 1}[kind]
    WT = {0: 136, 1: 128, 2: 129, 3: 129}[kind]
    W = {0: 146, 1: 128, 2: 130, 3: 130}[kind]
    R = {0: 3, 1: 4, 2: 4, 3: 4}[kind]
    tab = net.tabs[str(kind)]
    with ExitStack() as c2:
        p = Plan(nc, net.ctx, nm)
        G = [net.sb(f"{nm}G{i}", [128, KB, max(WT, W) if H < 8 else WT], ctx=c2) for i in range(R)]
        S = [net.sb(f"{nm}S{i}", [128, KB, 128], ctx=c2) for i in range(2)]
        dl = net.sb(nm + "dl", [128, KB], ctx=c2)
        PA = net.ps(nm + "PA", [128, W], c2)
        PS = net.sb(nm + "PS", [128, W], ctx=c2)
        dum = net.sb(nm + "dum", [128, 1], ctx=c2)
        sa, sp, sc = p.sem("aggv"), p.sem("aggp"), p.sem("aggs")
        for k in ("aggv", "aggp", "aggs"):
            del p.counts[k]
        P1N = {0: 0, 1: 9, 8: 6}[H]
        P2N = {0: 1, 1: 2, 8: 4}[H]
        KS = 3 if H == 8 else 4
        KA = P1N + 1 + KS + P2N
        CA = {0: 1, 1: 2, 8: 7}[H]
        z0 = p.op("vector", lambda e: e.memset(PA[:], 0.0))
        if H:
            ST = [net.sb(f"{nm}ST{i}", [128, EB], BF16, ctx=c2) for i in range(2)]
            svb = net.sb(nm + "svb", [128, 3, NT * 8], BF16, ctx=c2)
            svr = net.sb(nm + "svr", [128, NT * 8], ctx=c2)
            DR = [net.sb(f"{nm}DR{i}", [128, EB], I32, ctx=c2) for i in range(2)]
            GR = [net.sb(f"{nm}GR{i}", [H, 2, 128], ctx=c2) for i in range(2)]
            EH, FF, BB, T1, T2 = [net.sb(nm + x, [128, H, KB], ctx=c2) for x in ("EH", "FF", "BB", "T1", "T2")]
            RF = net.sb(nm + "RF", [H, 129], ctx=c2)
            RB = net.sb(nm + "RB", [H, 129], ctx=c2)
            sm = net.sb(nm + "sm", [128, 16 + 4 * H], ctx=c2)
            ac = net.sb(nm + "ac", [128, 2 * H], ctx=c2)
            PX = net.ps(nm + "PX", [128, KB, H], c2)
            PT = [net.ps(f"{nm}PT{i}", [H, 128], c2) for i in range(2)]
            PC = net.ps(nm + "PC", [128, 2, H], c2)
            xv, xp = p.sem("expv"), p.sem("expp")
            del p.counts["expv"], p.counts["expp"]
            z1 = p.op("vector", lambda e: e.tensor_copy(svb[:, 0, :], net.svf))
            z1 = p.op("vector", lambda e: e.tensor_tensor(svr[:], net.svf, svb[:, 0, :], ALU.subtract), [z1])
            z1 = p.op("vector", lambda e: e.tensor_copy(svb[:, 1, :], svr[:]), [z1])
            z1 = p.op("vector", lambda e: e.tensor_tensor(svr[:], svr[:], svb[:, 1, :], ALU.subtract), [z1])
            z1 = p.op("vector", lambda e: e.tensor_copy(svb[:, 2, :], svr[:]), [z1])
            z2 = p.op("vector", lambda e: e.memset(RF[:, 0:1], -BIG))
            z2 = p.op("vector", lambda e: e.memset(RB[:, 128:129], -BIG))
            p.raw("tensor", lambda e: e.sem_inc(xp, 1))
        if H == 8:
            MSG = [net.sb(f"{nm}M{i}", [128, KB, W], ctx=c2) for i in range(2)]
            dist = net.sb(nm + "dist", [128, 4, 128], ctx=c2)
            MFH, MBH = [net.sb(nm + x, [128, H, KB], ctx=c2) for x in ("MFH", "MBH")]
            tmp = net.sb(nm + "tmp", [128, 136], ctx=c2)
            for i in range(2):
                z2 = p.op("vector", lambda e, i=i: e.memset(MSG[i][:, :, W - 1:W], 1.0))
        if H == 1:
            EX = [net.sb(f"{nm}EX{i}", [128, KB], ctx=c2) for i in range(2)]
        p.raw("tensor", lambda e: e.sem_inc(sp, KB))
        p.raw("vector", lambda e: e.sem_inc(sa, 1))
        hi = {k: {} for k in ("vector", "tensor", "scalar")}
        gfree, drfree, grfree = [None] * R, [None, None], [None, None]
        gtok, drtok, grtok, ready, rhs = {}, {}, {}, {}, {}
        last = {"scan": None, "EH": None}

        def gather(b):
            s = b % R
            for k in range(KB):
                gtok[b] = p.dma("gpsimd", f"g{s}", lambda e, k=k: e.indirect_dma_start(
                    G[s][:, k, 0:WT], None, tab, bass.IndirectOffsetOnAxis(net.srcS[:, b * KB + k:b * KB + k + 1], 0)), [gfree[s]])

        def load_dst(b):
            s = b % 2
            drtok[b] = p.dma("sync", f"dr{s}", lambda e: e.dma_start(DR[s][:], row_bcast(net.dstp[b * EB:(b + 1) * EB], 128)), [drfree[s]])

        def load_runs(b):
            s = b % 2
            grtok[b] = p.dma("sync", f"gr{s}", lambda e: e.dma_start(GR[s][:], bass.AP(net.gfr.tensor, net.gfr.offset + b * 128, [[0, H], [NB * 128, 2], [1, 128]])), [grfree[s]])

        def load_tile(b):
            for q in ("vector", "tensor", "scalar"):
                def emit(e, q=q):
                    hi[q][b] = e.value_load(net.t0[0:1, b:b + 1], min_val=0, max_val=NT - 1)
                p.raw(q, emit)

        def released(b):
            gfree[b % R] = p.op("vector", lambda e: e.memset(dum[:], 0.0))
            if b + R < NB:
                gather(b + R)

        def expand(b):
            dr = DR[b % 2]

            def one_v(e, st, t):
                e.tensor_scalar(st[:], dr[:], net.jt[:, bass.ds(t, 1)], None, ALU.is_equal).then_inc(xv, 1)

            def expand_v(e):
                lo, up = hi["vector"][b], hi["vector"][b + 1]
                if b:
                    e.wait_ge(xp, hi["vector"][b - 1] + (b + 1))
                one_v(e, ST[0], lo)
                with e.If(lo < up):
                    with e.Fori(lo + 1, up + 1) as t:
                        e.wait_ge(xp, t + b + (t > lo + 1))
                        one_v(e, ST[1], t)

            def one_p(e, st, t, first):
                e.wait_ge(xv, t + (b + 1))
                for k in range(KB):
                    for j in range(3):
                        i = e.matmul(PX[:, k, :], st[:, k:EB:KB], svb[:, j, bass.ds(t * 8, H)], start=first and k + j == 0, stop=False, skip_group_check=True)
                i.then_inc(xp, 1)

            def expand_p(e):
                lo, up = hi["tensor"][b], hi["tensor"][b + 1]
                one_p(e, ST[0], lo, True)
                with e.If(lo < up):
                    with e.Fori(lo + 1, up + 1) as t:
                        one_p(e, ST[1], t, False)

            p.raw("vector", expand_v, [drtok[b], z1])
            p.raw("tensor", expand_p, [z1, last["EH"]])

        def fl(t):
            return t[:].rearrange("p h k -> p (h k)")

        def copy_masks(b):
            if H > 1:
                p.op("scalar", lambda e: e.copy(MFH[:], m["MF"][:, b:b + 1, :].broadcast_to([128, H, KB])), [last["scan"]])
                last["mask"] = p.op("scalar", lambda e: e.copy(MBH[:], m["MB"][:, b:b + 1, :].broadcast_to([128, H, KB])))

        def scan(b):
            g = G[b % R]
            mf, mb = (fl(MFH), fl(MBH)) if H > 1 else (m["MF"][:, b, :], m["MB"][:, b, :])
            mk = last.get("mask")
            p.raw("vector", lambda e: e.wait_ge(xp, hi["vector"][b + 1] + (b + 2)))
            v = p.op("vector", lambda e: e.tensor_tensor(EH[:], g[:, :, 128:128 + H].rearrange("p k h -> p h k"), PX[:].rearrange("p k h -> p h k"), ALU.add), [gtok[b]])
            last["EH"] = drfree[b % 2] = v
            if b + 2 < NB:
                load_dst(b + 2)
            v = p.op("vector", lambda e: e.scalar_tensor_tensor(EH[:], EH[:], 0.2, EH[:], ALU.mult, ALU.max), [v])
            f1 = p.op("vector", lambda e: e.tensor_tensor_scan(fl(FF), mf, fl(EH), -BIG, ALU.add, ALU.max), [v, mk])
            f2 = p.op("vector", lambda e: e.tensor_tensor_scan(fl(BB)[:, ::-1], mb[:, ::-1], fl(EH)[:, ::-1], -BIG, ALU.add, ALU.max), [v, mk])
            last["scan"] = f2
            last["turned"] = turned = []
            t1 = p.op("tensor", lambda e: e.matmul(PT[0][:], FF[:, :, KB - 1], net.ident[:], start=True, stop=True), [f1])
            t2 = p.op("tensor", lambda e: e.matmul(PT[1][:], BB[:, :, 0], net.ident[:], start=True, stop=True), [f2])
            turned += [t1, t2]

        def scan_across(b):
            gr = GR[b % 2]
            t1, t2 = last["turned"]
            r1 = p.op("vector", lambda e: e.tensor_tensor_scan(RF[:, 1:129], gr[:, 0, :], PT[0][:], -BIG, ALU.add, ALU.max), [t1, z2, grtok[b]])
            r2 = p.op("vector", lambda e: e.tensor_tensor_scan(RB[:, 0:128][:, ::-1], gr[:, 1, :][:, ::-1], PT[1][:, ::-1], -BIG, ALU.add, ALU.max), [t2])
            grfree[b % 2] = r2
            if b + 2 < NB:
                load_runs(b + 2)
            p.op("tensor", lambda e: e.matmul(PC[:, 0, :], RF[:, 0:128], net.ident[0:H, 0:H], start=True, stop=True), [r1])
            last["across"] = p.op("tensor", lambda e: e.matmul(PC[:, 1, :], RB[:, 1:129], net.ident[0:H, 0:H], start=True, stop=True), [r2])

        def weigh(b):
            g, c_ = G[b % R], last["across"]
            if H == 1:
                v = p.op("vector", lambda e: e.scalar_tensor_tensor(T1[:, 0, :], m["FM"][:, b, :], PC[:, 0, :], FF[:, 0, :], ALU.add, ALU.max), [c_])
                v = p.op("vector", lambda e: e.scalar_tensor_tensor(T2[:, 0, :], m["LM"][:, b, :], PC[:, 1, :], BB[:, 0, :], ALU.add, ALU.max), [c_])
            else:
                v = p.op("vector", lambda e: e.tensor_tensor(T1[:], m["FM"][:, b:b + 1, :].broadcast_to([128, H, KB]), PC[:, 0, :].rearrange("p (h o) -> p h o", o=1).broadcast_to([128, H, KB]), ALU.add), [c_])
                w = p.op("vector", lambda e: e.tensor_tensor(T2[:], m["LM"][:, b:b + 1, :].broadcast_to([128, H, KB]), PC[:, 1, :].rearrange("p (h o) -> p h o", o=1).broadcast_to([128, H, KB]), ALU.add), [c_])
                v = p.op("vector", lambda e: e.tensor_tensor(T1[:], T1[:], FF[:], ALU.max), [v])
                v = p.op("vector", lambda e: e.tensor_tensor(T2[:], T2[:], BB[:], ALU.max), [w])
            v = p.op("vector", lambda e: e.tensor_tensor(T1[:], T1[:], T2[:], ALU.max), [v])
            v = p.op("vector", lambda e: e.tensor_tensor(T2[:], EH[:], T1[:], ALU.subtract), [v])
            if H == 1:
                x = EX[b % 2]
                ex = p.op("scalar", lambda e: e.activation(x[:], T2[:, 0, :], ACT.Exp), [v])
                p.op("vector", lambda e: e.memset(g[:, :, 128:129], 1.0))
                v = p.op("vector", lambda e: e.tensor_copy(g[:, :, 129], T1[:, 0, :]))
                p.raw("scalar", lambda e: copy_sums(e, hi["scalar"][b] + b))
                rows = [p.op("scalar", lambda e, k=k: e.activation(g[:, k, 0:W], g[:, k, 0:W], ACT.Copy, scale=x[:, k:k + 1]), [v, ex]) for k in range(KB)]
                ready[b], rhs[b] = rows, [g[:, k, 0:W] for k in range(KB)]
            else:
                M = MSG[b % 2]
                ex = p.op("scalar", lambda e: e.activation(M[:, :, 128:128 + H], T2[:].rearrange("p h k -> p k h"), ACT.Exp), [v])
                il = p.op("scalar", lambda e: e.copy(M[:, :, 128 + 2 * H], m["isl"][:, b, :]))
                p.op("vector", lambda e: e.tensor_tensor(M[:, :, 128 + H:128 + 2 * H], T1[:].rearrange("p h k -> p k h"), m["isl"][:, b, :].rearrange("p (k o) -> p k o", o=1).broadcast_to([128, KB, H]), ALU.mult))
                v = p.op("vector", lambda e: e.tensor_tensor(
                    M[:, :, 0:128].rearrange("p k (d h) -> p k d h", h=H), g[:, :, 0:128].rearrange("p k (d h) -> p k d h", h=H),
                    M[:, :, 128:128 + H].rearrange("p k (o h) -> p k o h", o=1).broadcast_to([128, KB, 128 // H, H]), ALU.mult), [ex, il])
                gfree[b % R] = v
                if b + R < NB:
                    gather(b + R)
                ready[b], rhs[b] = [v], [M[:, k, :] for k in range(KB)]

        def merge_1(e, i, n, at):
            e.wait_ge(sc, i * CA + 1)

            def done(ins, wait=True):
                n[0] += 1
                ins.then_inc(sa, 1)
                if wait:
                    e.wait_ge(sa, i * KA + (n[0] + 1))

            if not H:
                return
            Am = net.acc[:, bass.ds(at * W + 128 + H, H)]
            Mb, mx, d1, d2 = [sm[:, 16 + H * q:16 + H * q + H] for q in range(4)]
            d12 = sm[:, 16 + 2 * H:16 + 4 * H]
            if H == 8:
                done(e.tensor_scalar(sm[:, 0:1], PS[:, 144:145], -1.0, BIG, ALU.add, ALU.mult))
                done(e.tensor_scalar(Mb, PS[:, 136:144], sm[:, 0:1], None, ALU.add))
            else:
                done(e.tensor_scalar(sm[:, 0:1], PS[:, 128:129], 0.0, None, ALU.is_equal))
                done(e.tensor_tensor(sm[:, 1:2], PS[:, 128:129], sm[:, 0:1], ALU.add))
                done(e.reciprocal(sm[:, 2:3], sm[:, 1:2]))
                done(e.tensor_tensor(sm[:, 3:4], PS[:, 129:130], sm[:, 2:3], ALU.mult))
                done(e.scalar_tensor_tensor(Mb, sm[:, 0:1], -BIG, sm[:, 3:4], ALU.mult, ALU.add))
            done(e.tensor_tensor(mx, Am, Mb, ALU.max))
            done(e.tensor_tensor(d1, Am, mx, ALU.subtract), False)
            done(e.tensor_tensor(d2, Mb, mx, ALU.subtract))
            done(e.tensor_scalar(Am, mx, 1.0, None, ALU.mult), False)
            assert n[0] == 1 + KS + P1N

        def merge_2(e, i, n, at):
            def done(ins, wait=True):
                n[0] += 1
                ins.then_inc(sa, 1)
                if wait:
                    e.wait_ge(sa, i * KA + (n[0] + 1))

            if not H:
                A = net.acc[:, bass.ds(at * W, W)]
                done(e.tensor_tensor(A, A, PS[:], ALU.add), False)
                return
            e.wait_ge(sc, i * CA + CA)
            An = net.acc[:, bass.ds(at * W, 128 + H)]
            if H > 1:
                An3 = An.rearrange("p (d h) -> p d h", h=H)
                nh = 128 // H + 1
                done(e.tensor_tensor(An3, An3, ac[:, 0:H].rearrange("p (o h) -> p o h", o=1).broadcast_to([128, nh, H]), ALU.mult), False)
                done(e.tensor_tensor(tmp[:].rearrange("p (d h) -> p d h", h=H), PS[:, 0:128 + H].rearrange("p (d h) -> p d h", h=H), ac[:, H:2 * H].rearrange("p (o h) -> p o h", o=1).broadcast_to([128, nh, H]), ALU.mult))
                done(e.tensor_tensor(An, An, tmp[:], ALU.add), False)
                Ac = net.acc[:, bass.ds(at * W + W - 1, 1)]
                done(e.tensor_tensor(Ac, Ac, PS[:, W - 1:W], ALU.add), False)
            else:
                done(e.tensor_scalar(An, An, ac[:, 0:1], None, ALU.mult))
                done(e.scalar_tensor_tensor(An, PS[:, 0:129], ac[:, 1:2], An, ALU.mult, ALU.add), False)

        def merge_exp(e, i):
            e.wait_ge(sa, i * KA + (1 + KS + P1N))
            e.activation(ac[:], sm[:, 16 + 2 * H:16 + 4 * H], ACT.Exp).then_inc(sc, 1)

        def last_chunks(e, i, s, free):
            e.wait_ge(sc, i * CA + 1)
            e.wait_ge(sa, i * KA + 2)
            if free is not None:
                e.wait_ge(sp, free)
            for k in range(12, KB):
                e.activation(dist[:, k - 12, :], net.iota[:], ACT.Abs, bias=dl[:, k:k + 1], scale=-1.0).then_inc(sc, 1)
            e.wait_ge(sc, i * CA + 5)
            e.activation(s[:, 12:KB, :], dist[:], ACT.Relu, bias=1.0, scale=-1.0).then_inc(sc, 1)

        def copy_sums(e, i):
            e.wait_ge(sp, i * KB + KB)
            e.wait_ge(sa, i * KA + 1)
            e.copy(PS[:], PA[:]).then_inc(sc, 1)

        def step_v(e, b, t, s, at, free):
            i, n = t + b, [1 + KS]
            if not H:
                e.wait_ge(sa, i * KA + 1)
            e.tensor_scalar(dl[:], net.dstS[:, b, :], net.tb[:, bass.ds(t, 1)], None, ALU.subtract).then_inc(sa, 1)
            e.wait_ge(sa, i * KA + 2)
            if free is not None:
                e.wait_ge(sp, free)
            for k in range(0, 4 * KS, 4):
                e.tensor_tensor(s[:, k:k + 4, :], net.iota[:].rearrange("p (o c) -> p o c", o=1).broadcast_to([128, 4, 128]),
                                dl[:, k:k + 4].rearrange("p (k o) -> p k o", o=1).broadcast_to([128, 4, 128]), ALU.is_equal).then_inc(sa, 1)
            merge_1(e, i, n, at)
            merge_2(e, i, n, at)
            assert n[0] == KA, n

        def step_p(e, b, t, s, rows=None):
            i = t + b
            e.wait_ge(sc, i * CA + 1)
            for k in range(KB):
                if k % 4 == 0:
                    if k < 4 * KS:
                        e.wait_ge(sa, i * KA + (k // 4 + 3))
                    else:
                        e.wait_ge(sc, i * CA + 6)
                    if rows:
                        e.wait_ge(p.sem("scalar"), rows[k + 3][1])
                e.matmul(PA[:], s[:, k, :], rhs[b][k], start=(k == 0), stop=(k == KB - 1)).then_inc(sp, 1)

        def first_step(b):
            def free(q):
                return (hi[q][b - 1] + (b - 1)) * KB + 2 * KB if b else None

            p.raw("vector", lambda e: step_v(e, b, hi["vector"][b], S[0], hi["vector"][b], free("vector")))
            if H == 1:
                p.raw("tensor", lambda e: step_p(e, b, hi["tensor"][b], S[0], ready[b]))
            else:
                p.raw("tensor", lambda e: step_p(e, b, hi["tensor"][b], S[0]), ready[b])
                p.raw("scalar", lambda e: copy_sums(e, hi["scalar"][b] + b))
            if H == 8:
                p.raw("scalar", lambda e: last_chunks(e, hi["scalar"][b] + b, S[0], free("scalar")))
            if H:
                p.raw("scalar", lambda e: merge_exp(e, hi["scalar"][b] + b))

        def other_steps(b):
            def on(q, body):
                def emit(e):
                    lo, up = hi[q][b], hi[q][b + 1]
                    with e.If(lo < up):
                        with e.Fori(lo + 1, up + 1) as t:
                            body(e, lo, t)
                p.raw(q, emit)

            on("vector", lambda e, lo, t: step_v(e, b, t, S[1], t - 1, (t + b) * KB + (t > lo + 1) * KB))
            on("tensor", lambda e, lo, t: step_p(e, b, t, S[1]))

            def others_s(e, lo, t):
                copy_sums(e, t + b)
                if H == 8:
                    last_chunks(e, t + b, S[1], (t + b) * KB + (t > lo + 1) * KB)
                if H:
                    merge_exp(e, t + b)

            on("scalar", others_s)

        for b in range(min(R, NB)):
            gather(b)
        if kind == 1:
            columns(net, p, c2)
        for b in range(3):
            load_tile(b)
        p.raw("scalar", lambda e: None, [z0])
        if H:
            for b in range(2):
                load_dst(b)
                load_runs(b)
            copy_masks(0)
            expand(0)
            scan(0)
            expand(1)
            scan_across(0)
            weigh(0)
        if not H:
            zs = net.sb(nm + "zs", [128, 50 * 128], ctx=c2)
            zt = p.op("gpsimd", lambda e: e.memset(zs[:], 0.0))
        for b in range(NB):
            if kind == 0:
                c = slice(2048 * b, min(2048 * b + 2048, E))
                p.dma("scalar", "attr", lambda e, c=c: e.dma_start(net.attr[0:32, c], io["attr32T"][:, c]))
                p.dma("scalar", "attr", lambda e, c=c: e.dma_start(net.attr[32:36, c], io["attr4T"][:, c]))
            if kind == 1 and b % 10 == 5 and b < 20:
                r = b // 10
                p.dma("scalar", "sums", lambda e, r=r: e.dma_start(net.sums[r].rearrange("(p t) c -> p (t c)", p=128), zs[:]), [zt])
            if b + 3 <= NB:
                load_tile(b + 3)
            more = H and b + 1 < NB
            if more:
                copy_masks(b + 1)
            if not H:
                ready[b], rhs[b] = [gtok[b]], [G[b % R][:, k, 0:W] for k in range(KB)]
            first_step(b)
            if b and H < 8:
                released(b - 1)
            if more:
                scan(b + 1)
            if H and b + 2 < NB:
                expand(b + 2)
            if more:
                scan_across(b + 1)
            other_steps(b)
            if more:
                weigh(b + 1)
        steps, n = NB + NT - 1, [1 + KS]
        p.raw("scalar", lambda e: copy_sums(e, steps))
        if H == 8:
            p.raw("scalar", lambda e: e.wait_ge(sc, steps * CA + 1))
            p.raw("scalar", lambda e: e.sem_inc(sc, 5))
        if H:
            p.raw("scalar", lambda e: merge_exp(e, steps))
        p.raw("vector", lambda e: e.wait_ge(sc, steps * CA + 1))
        p.raw("vector", lambda e: e.sem_inc(sa, 1 + KS))
        p.raw("vector", lambda e: merge_1(e, steps, n, NT - 1))
        p.raw("vector", lambda e: merge_2(e, steps, n, NT - 1))
        p.finish()


def final_attention(net, kind):
    nc, io = net.nc, net.io
    nm = f"f{kind}"
    H = 8 if kind == 0 else 1
    W = 146 if kind == 0 else 130
    A = net.acc[:, 0:NT * W].rearrange("p (t c) -> p t c", t=NT)
    with ExitStack() as c2:
        p = Plan(nc, net.ctx, nm)
        rd = net.sb(nm + "rd", [128, NT, H], ctx=c2)
        r2 = net.sb(nm + "r2", [128, NT, H], ctx=c2)
        bias = net.sb(nm + "b", [128, 128], ctx=c2)
        bname = {0: "L0_gnn_b_ff", 2: "L2_gnn_b1", 3: "L2_gnn_b2"}[kind]
        lb = p.dma("sync", "b", lambda e: e.dma_start(bias[:], row_bcast(io[bname], 128)))
        v = p.op("vector", lambda e: e.tensor_scalar(r2[:], A[:, :, 128:128 + H], 0.0, None, ALU.is_equal))
        v = p.op("vector", lambda e: e.tensor_tensor(rd[:], r2[:], A[:, :, 128:128 + H], ALU.add), [v])
        v = p.op("vector", lambda e: e.reciprocal(rd[:], rd[:]), [v])
        if kind != 0:
            o = net.sb(nm + "o", [128, NT, 128], ctx=c2)
            for t0, nt in GROUPS:
                for t in range(t0, t0 + nt):
                    last = p.op("vector", lambda e, t=t: e.scalar_tensor_tensor(o[:, t, :], A[:, t, 0:128], rd[:, t, :], bias[:], ALU.mult, ALU.add), [v, lb])
                if kind == 2:
                    p.op("scalar", lambda e, t0=t0, nt=nt: e.activation(net.aux[:, t0 * 128:(t0 + nt) * 128], o[:, t0:t0 + nt, :].rearrange("p t c -> p (t c)"), ACT.Relu), [last])
                else:
                    p.op("gpsimd", lambda e, t0=t0, nt=nt: e.tensor_tensor(net.x[:, t0:t0 + nt, :], net.x[:, t0:t0 + nt, :], o[:, t0:t0 + nt, :], ALU.add), [last])
            p.finish()
            return
        Wf = net.sb(nm + "Wf", [128, 128], ctx=c2)
        lw = p.dma("sync", "w", lambda e: e.dma_start(Wf[:], io["L0_gnn_W_ff"]))
        o = net.sb(nm + "o", [128, 3, 512], ctx=c2)
        oT = net.sb(nm + "oT", [128, 3, 512], ctx=c2)
        P1 = [net.ps(f"{nm}p{i}", [128, 4, 128], c2) for i in range(3)]
        P2 = [net.ps(f"{nm}q{i}", [128, 4, 128], c2) for i in range(3)]
        dg = net.sb(nm + "dg", [128, NT], ctx=c2)
        c = p.op("vector", lambda e: e.tensor_scalar(dg[:], A[:, :, W - 1], 1.0, None, ALU.add))
        c = p.op("scalar", lambda e: e.activation(dg[:], dg[:], ACT.Sqrt), [c])
        p.op("vector", lambda e: e.reciprocal(net.dinv[:], dg[:]), [c])
        free = [[None] * 3 for _ in range(4)]
        turned, xb = {}, {}

        def turn(g):
            (t0, nt), s = GROUPS[g], g % 3
            xb[g] = p.op("gpsimd", lambda e: e.tensor_tensor(net.x[:, t0:t0 + nt, :], net.x[:, t0:t0 + nt, :], bias[:].rearrange("p (o c) -> p o c", o=1).broadcast_to([128, nt, 128]), ALU.add), [lb])
            a = p.op("vector", lambda e: e.tensor_tensor(
                o[:, s, 0:nt * 128].rearrange("p (t d h) -> p t d h", d=16, h=8), A[:, t0:t0 + nt, 0:128].rearrange("p t (d h) -> p t d h", h=8),
                rd[:, t0:t0 + nt, :].rearrange("p t (o h) -> p t o h", o=1).broadcast_to([128, nt, 16, 8]), ALU.mult), [v, free[0][s]])
            for j in range(nt):
                b = p.op("tensor", lambda e, j=j: e.transpose(P1[s][:, j, :], o[:, s, 128 * j:128 * j + 128], net.ident[:]), [a, free[1][s]])
            free[0][s] = b
            free[1][s] = turned[g] = p.op("scalar", lambda e: e.copy(oT[:, s, 0:nt * 128], P1[s][:, 0:nt, :].rearrange("p a c -> p (a c)")), [b, free[2][s]])

        turn(0)
        turn(1)
        for g, (t0, nt) in enumerate(GROUPS):
            if g + 2 < len(GROUPS):
                turn(g + 2)
            s = g % 3
            for j in range(nt):
                d = p.op("tensor", lambda e, s=s, j=j: e.matmul(P2[s][:, j, :], oT[:, s, 128 * j:128 * j + 128], Wf[:], start=True, stop=True), [turned[g], lw, free[3][s]])
            free[2][s] = d
            free[3][s] = p.op("vector", lambda e, s=s, t0=t0, nt=nt: e.tensor_tensor(net.x[:, t0:t0 + nt, :], net.x[:, t0:t0 + nt, :], P2[s][:, 0:nt, :], ALU.add), [d, xb[g]])
        p.finish()


def final_conv(net):
    nc, io = net.nc, net.io
    A = net.acc[:, 0:NT * 128].rearrange("p (t c) -> p t c", t=NT)
    with ExitStack() as c2:
        p = Plan(nc, net.ctx, "f1")
        rows = net.sb("f1r", [128, 3, 128], ctx=c2)
        lb = [p.dma("sync", "b", lambda e, j=j, n=n: e.dma_start(rows[:, j, :], row_bcast(io[n], 128)))
              for j, n in enumerate(("L1_gnn_b", "L1_gnn_gamma", "L1_gnn_beta"))][-1]
        ones = net.sb("f1o", [128, 2, 128], ctx=c2)
        cm = net.sb("f1c", [128, 1], ctx=c2)
        mean = net.sb("f1m", [128, 128], ctx=c2)
        sq = net.sb("f1s", [128, NT, 128], ctx=c2)
        PM = net.ps("f1pm", [128, 128], c2)
        PV = net.ps("f1pv", [128, 128], c2)
        o = p.op("vector", lambda e: e.memset(ones[:, 0, :], 1.0))
        o = p.op("vector", lambda e: e.tensor_scalar(cm[:], net.jt[:, 0:1], float(TAIL), None, ALU.is_lt), [o])
        o = p.op("vector", lambda e: e.tensor_scalar(ones[:, 1, :], ones[:, 0, :], cm[:], None, ALU.mult), [o])
        for t in range(NT):
            a = p.op("vector", lambda e, t=t: e.scalar_tensor_tensor(A[:, t, :], A[:, t, :], net.dinv[:, t:t + 1], rows[:, 0, :], ALU.mult, ALU.add), [lb])
            q = p.op("tensor", lambda e, t=t: e.matmul(PM[:], ones[:, int(t == NT - 1), :], A[:, t, :], start=(t == 0), stop=(t == NT - 1)), [a, o])
        v = p.op("vector", lambda e: e.tensor_scalar(mean[:], PM[:], 1.0 / N, None, ALU.mult), [q])
        for t in range(NT):
            a = p.op("vector", lambda e, t=t: e.tensor_tensor(A[:, t, :], A[:, t, :], mean[:], ALU.subtract), [v])
            s = p.op("scalar", lambda e, t=t: e.activation(sq[:, t, :], A[:, t, :], ACT.Square), [a])
            q = p.op("tensor", lambda e, t=t: e.matmul(PV[:], ones[:, int(t == NT - 1), :], sq[:, t, :], start=(t == 0), stop=(t == NT - 1)), [s])
        s = p.op("scalar", lambda e: e.activation(mean[:], PV[:], ACT.Sqrt, bias=net.eps[:], scale=1.0 / N), [q])
        v = p.op("vector", lambda e: e.reciprocal(mean[:], mean[:]), [s])
        v = p.op("vector", lambda e: e.tensor_tensor(mean[:], mean[:], rows[:, 1, :], ALU.mult), [v])
        v = p.op("vector", lambda e: e.tensor_tensor(A, A, mean[:].rearrange("p (o c) -> p o c", o=1).broadcast_to([128, NT, 128]), ALU.mult), [v])
        v = p.op("vector", lambda e: e.tensor_tensor(A, A, rows[:, 2:3, :].broadcast_to([128, NT, 128]), ALU.add), [v])
        v = p.op("vector", lambda e: e.scalar_tensor_tensor(net.x[:].rearrange("p t c -> p (t c)"), net.acc[:, 0:NT * 128], 0.0, net.x[:].rearrange("p t c -> p (t c)"), ALU.max, ALU.add), [v])
        p.finish()


def pairs(net):
    nc, io = net.nc, net.io
    nm = "pr"
    R, RA, KH, EH, NH = 8, 2, 4, 512, 196
    tab = net.tabs["4"]
    with ExitStack() as c2:
        p = Plan(nc, net.ctx, nm)
        sb = lambda n, s, dt=F32: net.sb(nm + n, s, dt, ctx=c2)
        pm, srcF = sb("pm", [128, 784]), sb("srcF", [128, 784])
        srcC = sb("srcC", [128, 784], I32)
        t0h = sb("t0h", [1, NH + 1], I32)
        G = [sb(f"G{i}", [128, KH, 128]) for i in range(R)]
        MSG = [sb(f"MSG{i}", [128, KH, 128]) for i in range(2)]
        OUT = [sb(f"OUT{i}", [128, KH, 128]) for i in range(3)]
        EQ = [sb(f"EQ{i}", [128, KH, 128]) for i in range(3)]
        ST = sb("ST", [128, EH])
        DR = [sb(f"DR{i}", [128, EH], I32) for i in range(3)]
        SR = [sb(f"SR{i}", [128, EH], I32) for i in range(3)]
        EA = [sb(f"EA{i}", [36, EH]) for i in range(3)]
        hr, hs = sb("hr", [128, 2, 512]), sb("hs", [128, 2, 512])
        w1 = sb("w1", [36, 128])
        w2 = sb("w2", [128, 2, 128])
        b1 = sb("b1", [128, 2])
        b2 = sb("b2", [128, 2, 128])
        bb = sb("bb", [128, 4, 128])
        low = sb("low", [128, 128])
        one = sb("one", [128, 128])
        u = sb("u", [128, 512])
        al = sb("al", [128, 16])
        cnt = sb("cnt", [128, KH])
        junk = sb("junk", [128, 128])
        ti = sb("ti", [128, KH])
        trash = sb("trash", [128, 1])
        idx = [sb(f"idx{i}", [128, KH], I32) for i in range(4)]
        PQ = [net.ps(f"{nm}PQ{i}", [128, KH, 256], c2) for i in range(2)]
        PH = [net.ps(f"{nm}PH{i}", [128, 512], c2) for i in range(2)]
        PW = net.ps(nm + "PW", [128, 512], c2)
        PS = net.ps(nm + "PS", [128, 4, 128], c2)
        xv, xp = p.sem("expv"), p.sem("expp")
        for k in ("expv", "expp"):
            del p.counts[k]
        cols = [p.dma("sync", "cols", lambda e, t=t, a=a: e.dma_start(t[:], a)) for t, a in ((srcC, net.srcc), (srcF, net.cols[0]), (pm, net.cols[1]))][-1]
        l = p.dma("sync", "t0", lambda e: e.dma_start(t0h[0:1, 0:NH].rearrange("a (n o) -> a n o", o=1), net.dstp.rearrange("(b n) -> b n", n=EH)[:, 0:1].rearrange("(a b) o -> a b o", a=1), allow_slow_non_contiguous=True))
        v = p.op("vector", lambda e: e.tensor_scalar(t0h[0:1, 0:NH], t0h[0:1, 0:NH], 7, None, ALU.arith_shift_right), [l])
        v = p.op("vector", lambda e: e.memset(t0h[0:1, 0:1], 0), [v])
        tready = p.op("vector", lambda e: e.memset(t0h[0:1, NH:NH + 1], NT - 1), [v])
        ready = [p.dma("scalar", "w", lambda e: e.dma_start(w1[0:32, :], io["L3_gnn_rad_W1"])),
                 p.dma("scalar", "w", lambda e: e.dma_start(w1[32:36, :], io["L3_gnn_sph_W1"]))]
        for j, n in enumerate(("rad", "sph")):
            ready.append(p.dma("scalar", "w", lambda e, j=j, n=n: e.dma_start(w2[:, j, :], io[f"L3_gnn_{n}_W2"])))
            ready.append(p.dma("scalar", "w", lambda e, j=j, n=n: e.dma_start(b1[:, j:j + 1], io[f"L3_gnn_{n}_b1"].rearrange("(p o) -> p o", o=1))))
            ready.append(p.dma("scalar", "w", lambda e, j=j, n=n: e.dma_start(b2[:, j, :], row_bcast(io[f"L3_gnn_{n}_b2"], 128))))
        v = p.op("vector", lambda e: e.tensor_tensor(bb[:], b2[:, 0:1, :].broadcast_to([128, 4, 128]), b2[:, 1:2, :].broadcast_to([128, 4, 128]), ALU.add), ready)
        v = p.op("vector", lambda e: e.memset(one[:], 1.0), [v])
        z1 = p.op("vector", lambda e: e.tensor_scalar(trash[:], net.jt[:, 0:1], float(NP), None, ALU.add), [v])
        lo_ = p.op("gpsimd", lambda e: e.affine_select(out=low[:], in_=one[:], compare_op=ALU.is_gt, fill=0.0, base=0, pattern=[[-1, 128]], channel_multiplier=1), [z1])
        p.raw("tensor", lambda e: e.sem_inc(xp, 1))
        hi = {"vector": {}, "tensor": {}}
        gfree, gtok, rtok, etok = [None] * R, {}, {}, {}
        rfree, eafree = [None] * 3, [None] * 3
        phf, hf, pqf, msgf, eqf = [None] * 2, [None] * 2, [None] * 2, [None] * 2, [None] * 3
        psf = pwf = None
        hid, ixr, msg, scat, landed = {}, {}, {}, {}, [None] * RA

        def gather(b, lo=0, hi=KH, after=()):
            s = b % R
            for k in range(lo, hi):
                gtok[b] = p.dma("gpsimd", f"g{s}", lambda e, k=k: e.indirect_dma_start(
                    G[s][:, k, :], None, tab, bass.IndirectOffsetOnAxis(srcC[:, b * KH + k:b * KH + k + 1], 0)), [gfree[s], *after])

        def load(b):
            s = b % 3
            rtok[b] = [p.dma("sync", f"dr{s}", lambda e: e.dma_start(DR[s][:], row_bcast(net.dstp[b * EH:(b + 1) * EH], 128)), [rfree[s]]),
                       p.dma("sync", f"sr{s}", lambda e: e.dma_start(SR[s][:], row_bcast(net.srcp[b * EH:(b + 1) * EH], 128)), [rfree[s]])]
            etok[b] = p.dma("sync", f"ea{s}", lambda e: e.dma_start(EA[s][:], net.attr[:, b * EH:(b + 1) * EH]), [eafree[s]])

        def load_tile(b):
            for q in ("vector", "tensor"):
                def emit(e, q=q):
                    hi[q][b] = e.value_load(t0h[0:1, b:b + 1], min_val=0, max_val=NT - 1)
                p.raw(q, emit, [tready])

        def expand(b):
            dr, pq = DR[b % 3], PQ[b % 2]

            def one_v(e, t):
                e.wait_ge(xp, t + (b + 1))
                e.tensor_scalar(ST[:], dr[:], net.jt[:, bass.ds(t, 1)], None, ALU.is_equal).then_inc(xv, 1)

            def one_p(e, t, first):
                e.wait_ge(xv, t + (b + 1))
                for k in range(KH):
                    i = e.matmul(pq[:, k, :], ST[:, k * 128:k * 128 + 128], net.kv[:, bass.ds(t * 256, 256)], start=first and k % 2 == 0, stop=False, skip_group_check=True)
                i.then_inc(xp, 1)

            def expand_v(e):
                one_v(e, hi["vector"][b])
                with e.If(hi["vector"][b] < hi["vector"][b + 1]):
                    with e.Fori(hi["vector"][b] + 1, hi["vector"][b + 1] + 1) as t:
                        one_v(e, t)

            def expand_p(e):
                one_p(e, hi["tensor"][b], True)
                with e.If(hi["tensor"][b] < hi["tensor"][b + 1]):
                    with e.Fori(hi["tensor"][b] + 1, hi["tensor"][b + 1] + 1) as t:
                        one_p(e, t, False)

            p.raw("vector", expand_v, [rtok[b][0]])
            p.raw("tensor", expand_p, [pqf[b % 2]])

        def hidden(b):
            ea, h = EA[b % 3], b % 2
            a1 = p.op("tensor", lambda e: e.matmul(PH[0][:], w1[0:32, :], ea[0:32, :], start=True, stop=True), [etok[b], phf[0], *ready])
            a2 = p.op("tensor", lambda e: e.matmul(PH[1][:], w1[32:36, :], ea[32:36, :], start=True, stop=True), [phf[1]])
            eafree[b % 3] = a2
            phf[0] = p.op("scalar", lambda e: e.activation(hr[:, h, :], PH[0][:], ACT.Silu, bias=b1[:, 0:1]), [a1, hf[h], *ready])
            phf[1] = hid[b] = p.op("scalar", lambda e: e.activation(hs[:, h, :], PH[1][:], ACT.Silu, bias=b1[:, 1:2]), [a2])

        def equal(b):
            sr, eq, ix = SR[b % 3], EQ[b % 3], idx[b % 4]
            for k in range(KH):
                c = slice(128 * k, 128 * k + 128)
                v = p.op("vector", lambda e, c=c, k=k: e.tensor_scalar(eq[:, k, :], sr[:, c], srcF[:, b * KH + k:b * KH + k + 1], None, ALU.is_equal), [rtok[b][1], eqf[b % 3], cols])
            rfree[b % 3] = v
            for k in range(KH):
                v = p.op("vector", lambda e, k=k: e.scalar_tensor_tensor(junk[:], eq[:, k, :], 1.0, low[:], ALU.mult, ALU.mult, accum_out=cnt[:, k:k + 1]), [v, lo_])
            sc = srcF[:, b * KH:b * KH + KH]
            v = p.op("vector", lambda e: e.tensor_scalar(cnt[:], cnt[:], 0.5, None, ALU.is_gt), [v])
            w = p.op("vector", lambda e: e.tensor_scalar(ti[:], sc, -1.0, trash[:], ALU.mult, ALU.add))
            v = p.op("vector", lambda e: e.tensor_tensor(ti[:], ti[:], cnt[:], ALU.mult), [w])
            ixr[b] = p.op("vector", lambda e: e.tensor_tensor(ix[:], ti[:], sc, ALU.add), [v, scat.get(b - 4)])

        def filters(b):
            h = b % 2
            for k in range(KH):
                q = slice(128 * k, 128 * k + 128)
                p.op("tensor", lambda e, q=q: e.matmul(PW[:, q], hr[:, h, q], w2[:, 0, :], start=True, stop=False, skip_group_check=True), [hid[b], pwf])
                hf[h] = p.op("tensor", lambda e, q=q: e.matmul(PW[:, q], hs[:, h, q], w2[:, 1, :], start=False, stop=True, skip_group_check=True))

        def weigh(b):
            nonlocal pwf
            g, pq, ms = G[b % R], PQ[b % 2], MSG[b % 2]
            u4 = u[:].rearrange("p (a c) -> p a c", c=128)
            a3 = al[:].rearrange("p (a h) -> p a h", h=4)
            pwf = p.op("vector", lambda e: e.tensor_tensor(u[:], PW[:], bb[:].rearrange("p a c -> p (a c)"), ALU.add), [hf[b % 2]])
            p.raw("vector", lambda e: e.wait_ge(xp, hi["vector"][b + 1] + (b + 2)))
            v = p.op("vector", lambda e: e.tensor_tensor(u4, u4, pq[:, :, 0:128], ALU.mult), [pwf])
            gfree[b % R] = v = p.op("vector", lambda e: e.tensor_tensor(u4, u4, g[:], ALU.mult), [v, gtok[b]])
            v = p.op("vector", lambda e: e.tensor_reduce(al[:], u[:].rearrange("p (a c) -> p a c", c=32), AX.X, ALU.add), [v])
            v = p.op("vector", lambda e: e.tensor_tensor(a3, a3, pm[:, b * KH:b * KH + KH].rearrange("p (a o) -> p a o", o=1).broadcast_to([128, KH, 4]), ALU.mult), [v, cols])
            pqf[b % 2] = msg[b] = p.op("vector", lambda e: e.tensor_tensor(
                ms[:].rearrange("p a (h c) -> p a h c", c=32), pq[:, :, 128:256].rearrange("p a (h c) -> p a h c", c=32),
                al[:].rearrange("p (a h o) -> p a h o", h=4, o=1).broadcast_to([128, KH, 4, 32]), ALU.mult), [v, msgf[b % 2]])

        def add(b):
            nonlocal psf
            eq, ms, out, ix = EQ[b % 3], MSG[b % 2], OUT[b % 3], idx[b % 4]
            for k in range(KH):
                q = p.op("tensor", lambda e, k=k: e.matmul(PS[:, k, :], eq[:, k, :], ms[:, k, :], start=True, stop=True), [msg[b], psf])
            eqf[b % 3] = msgf[b % 2] = q
            psf = p.op("scalar", lambda e: e.copy(out[:], PS[:]), [q, scat.get(b - 3)])
            for k in range(KH):
                r = k % RA
                landed[r] = p.dma("gpsimd", f"s{r}", lambda e, k=k, r=r: e.indirect_dma_start(
                    net.sums[r], bass.IndirectOffsetOnAxis(ix[:, k:k + 1], 0), out[:, k, :], None, compute_op=ALU.add), [psf, ixr[b], landed[r]])
                if r == RA - 1 and b + R < NH:
                    gather(b + R, k - 1, k + 1)
            scat[b] = list(landed)

        for b in range(R):
            gather(b, after=[cols])
        for b in range(3):
            load(b)
        load_tile(0)
        load_tile(1)
        hidden(0)
        expand(0)
        equal(0)
        for b in range(NH):
            if b + 1 < NH:
                load_tile(b + 2)
                hidden(b + 1)
            filters(b)
            if b + 1 < NH:
                expand(b + 1)
            weigh(b)
            if b + 1 < NH:
                equal(b + 1)
            if b:
                add(b - 1)
            if b + 3 < NH:
                load(b + 3)
        add(NH - 1)
        last = [(f"s{r}", p.counts[f"s{r}"]) for r in range(RA)]
        L = [G[0:RA], G[RA:2 * RA]]
        done = ("vector", p.counts["vector"])
        lf = [[None] * RA for _ in range(2)]
        slots = [f"{n}{i}" for n in ("dr", "sr", "ea") for i in range(3)]
        for j, t0 in enumerate(range(0, NT, KH)):
            n, s = min(KH, NT - t0), j % 2
            for r in range(RA):
                ld = p.dma("sync", slots[s * RA + r], lambda e, r=r, s=s, t0=t0, n=n: e.dma_start(L[s][r][:, 0:n, :], net.sums[r][t0 * 128:(t0 + n) * 128, :].rearrange("(t q) c -> q t c", q=128)), [*last, done, lf[s][r]])
                a = lf[s][r] = p.op("vector", lambda e, r=r, s=s, t0=t0, n=n: e.tensor_tensor(net.x[:, t0:t0 + n, :], net.x[:, t0:t0 + n, :], L[s][r][:, 0:n, :], ALU.add), [ld, ("vector", p.counts["vector"])])
        p.dma("sync", "out", lambda e: e.dma_start(io["out"][0:(NT - 1) * 128, :].rearrange("(t q) c -> q t c", q=128), net.x[:, 0:NT - 1, :]), [a])
        p.dma("sync", "out", lambda e: e.dma_start(io["out"][(NT - 1) * 128:N, :], net.x[0:TAIL, NT - 1, :]), [a])
        p.finish()


def build(nc, io):
    with ExitStack() as ctx:
        net = Net(nc, ctx, io)
        setup(net)
        with ExitStack() as c2:
            net.sv = net.sb("sv", [128, NT, 8], ctx=c2)
            net.svf = net.sv[:].rearrange("p t h -> p (t h)")
            net.acc = net.sb("acc", [128, NT * 146], ctx=c2)
            net.aux = net.sb("aux", [128, NT * 128], ctx=c2)
            m = masks(net, c2)
            nodes(net, 0)
            edges(net, 0, m)
            final_attention(net, 0)
            nodes(net, 1)
            edges(net, 1)
            final_conv(net)
            for kind in (2, 3):
                nodes(net, kind)
                edges(net, kind, m)
                final_attention(net, kind)
        net.kv = net.sb("kv", [128, NT * 256])
        nodes(net, 4)
        pairs(net)


FLOATS = ["x", "edge_weight", "edge_weight_n2", "L0_gnn_ln_gamma", "L0_gnn_ln_beta", "L0_gnn_W_in", "L0_gnn_b_in",
          "L0_gnn_W_u", "L0_gnn_b_u", "L0_gnn_W_v", "L0_gnn_W_ff", "L0_gnn_b_ff", "L1_gnn_W", "L1_gnn_b",
          "L1_gnn_gamma", "L1_gnn_beta", "L2_gnn_W1", "L2_gnn_as1", "L2_gnn_ad1", "L2_gnn_b1", "L2_gnn_W2",
          "L2_gnn_as2", "L2_gnn_ad2", "L2_gnn_b2", "L3_gnn_rad_W1", "L3_gnn_rad_b1", "L3_gnn_rad_W2",
          "L3_gnn_rad_b2", "L3_gnn_sph_W1", "L3_gnn_sph_b1", "L3_gnn_sph_W2", "L3_gnn_sph_b2", "L3_gnn_Wq",
          "L3_gnn_Wk", "L3_gnn_Wv"]


def kernel(**inputs):
    import numpy as _np
    import concourse.bacc as _bacc
    from concourse import mybir as _mybir
    from concourse.bass_utils import run_bass_kernel_spmd as _run

    nc = _bacc.Bacc("TRN2", target_bir_lowering=False, num_devices=1)
    arrays = {n: _np.ascontiguousarray(inputs[n]) for n in FLOATS + ["src", "dst"]}
    arrays["attr32T"] = _np.ascontiguousarray(_np.asarray(inputs["edge_attr_32"]).T)
    arrays["attr4T"] = _np.ascontiguousarray(_np.asarray(inputs["edge_attr_4"]).T)
    maps, io = {}, {}
    for n, a in arrays.items():
        maps[f"in_{n}"] = a
        io[n] = nc.dram_tensor(f"in_{n}", a.shape, _mybir.dt.from_np(a.dtype), kind="ExternalInput").ap()
    io["out"] = nc.dram_tensor("out_x", (N, D), _mybir.dt.float32, kind="ExternalOutput").ap()
    build(nc, io)
    r = _run(nc, [maps], core_ids=[0])
    return r.results[0]["out_x"]
```
